# Optimizing a Trainium2 kernel written in Bass

```python
import numpy as np
import jax
import jax.numpy as jnp

def _softmax(x, axis=-1):
    return jax.nn.softmax(x, axis=axis)

def _gelu(x):
    return jax.nn.gelu(x, approximate=True)

def _silu(x):
    return jax.nn.silu(x)

def _sigmoid(x):
    return jax.nn.sigmoid(x)

def _layernorm(x, axis=-1, eps=1e-05):
    m = jnp.mean(x, axis=axis, keepdims=True)
    v = jnp.var(x, axis=axis, keepdims=True)
    return (x - m) / jnp.sqrt(v + eps)

def _scatter_add(tgt, idx, src, axis=0):
    return tgt.at[idx].add(src)

def _segment_sum(src, seg, n):
    return jax.ops.segment_sum(src, seg, n)
kernel_name = 'mk_sandwich_d1_jaxref_r8_65a3ac'

def setup_inputs(seed: int=0):
    np.random.seed(seed)
    _w = jnp.asarray

    def _L0_attn_setup():
        import jax, jax.numpy as jnp
        import numpy as np
        CHUNK = 64
        HEADS = 16

        def _chunk_mask(T, cs):
            idx = jnp.arange(T)
            blk = idx // cs * cs
            qb = blk[:, None]
            kb = blk[None, :]
            masked = (qb >= kb) & (idx[None, :] - idx[:, None] - 2 * (kb - qb) >= 1)
            return masked
        key = jax.random.key(seed)
        ks = jax.random.split(key, 6)
        B, T, C = (2, 256, 128)
        w = 0.02
        return {'x': jax.random.normal(ks[0], (B, T, C), jnp.float32), 'Wq': jax.random.normal(ks[1], (C, C), jnp.float32) * w, 'bq': jnp.zeros((C,), jnp.float32), 'Wk': jax.random.normal(ks[2], (C, C), jnp.float32) * w, 'bk': jnp.zeros((C,), jnp.float32), 'Wv': jax.random.normal(ks[3], (C, C), jnp.float32) * w, 'bv': jnp.zeros((C,), jnp.float32), 'Wo': jax.random.normal(ks[4], (C, C), jnp.float32) * w, 'bo': jnp.zeros((C,), jnp.float32), 'attn_scale': jnp.full((1,), 1.0 / np.sqrt(C // HEADS), jnp.float32)}
    _L0_attn_in = _L0_attn_setup()

    def _L0_ffn_setup():
        import jax, jax.numpy as jnp
        import numpy as np
        DIM = 128
        E = 16
        TOPK = 2
        G = 4
        TOPK_G = 2
        INTER = 64
        N_SHARED = 2
        ROUTE_SCALE = 1.0

        def _gate(xf, gate_w, gate_b):
            scores = xf @ gate_w.T
            scores = jax.nn.softmax(scores.astype(jnp.float32), axis=-1)
            orig = scores
            scores = scores + gate_b
            T = xf.shape[0]
            sg = scores.reshape(T, G, E // G)
            group_scores = jax.lax.top_k(sg, 2)[0].sum(-1)
            _, gidx = jax.lax.top_k(group_scores, TOPK_G)
            keep = jax.nn.one_hot(gidx, G).sum(axis=1) > 0
            sg = jnp.where(keep[:, :, None], sg, -jnp.inf)
            scores = sg.reshape(T, E)
            _, idx = jax.lax.top_k(scores, TOPK)
            weights = jnp.take_along_axis(orig, idx, axis=1)
            weights = (weights * ROUTE_SCALE).astype(xf.dtype)
            return (weights, idx)
        key = jax.random.key(seed)
        ks = jax.random.split(key, 16)
        s = lambda fan_in: 1.0 / np.sqrt(fan_in)
        inp = {'x': jax.random.normal(ks[0], (4, 128, DIM), dtype=jnp.float32), 'gate_w': jax.random.normal(ks[1], (E, DIM), dtype=jnp.float32) * s(DIM), 'gate_b': jnp.zeros((E,), dtype=jnp.float32), 'We1': jax.random.normal(ks[2], (E, DIM, INTER), dtype=jnp.float32) * s(DIM), 'be1': jnp.zeros((E, INTER), dtype=jnp.float32), 'We2': jax.random.normal(ks[3], (E, INTER, DIM), dtype=jnp.float32) * s(INTER), 'be2': jnp.zeros((E, DIM), dtype=jnp.float32), 'We3': jax.random.normal(ks[4], (E, DIM, INTER), dtype=jnp.float32) * s(DIM), 'be3': jnp.zeros((E, INTER), dtype=jnp.float32), 'ws1': jax.random.normal(ks[5], (DIM, N_SHARED * INTER), dtype=jnp.float32) * s(DIM), 'bs1': jnp.zeros((N_SHARED * INTER,), dtype=jnp.float32), 'ws2': jax.random.normal(ks[6], (N_SHARED * INTER, DIM), dtype=jnp.float32) * s(N_SHARED * INTER), 'bs2': jnp.zeros((DIM,), dtype=jnp.float32), 'ws3': jax.random.normal(ks[7], (DIM, N_SHARED * INTER), dtype=jnp.float32) * s(DIM), 'bs3': jnp.zeros((N_SHARED * INTER,), dtype=jnp.float32)}
        return inp
    _L0_ffn_in = _L0_ffn_setup()
    _d = {'L0_attn_x': _L0_attn_in['x'], 'L0_attn_Wq': _L0_attn_in['Wq'], 'L0_attn_bq': _L0_attn_in['bq'], 'L0_attn_Wk': _L0_attn_in['Wk'], 'L0_attn_bk': _L0_attn_in['bk'], 'L0_attn_Wv': _L0_attn_in['Wv'], 'L0_attn_bv': _L0_attn_in['bv'], 'L0_attn_Wo': _L0_attn_in['Wo'], 'L0_attn_bo': _L0_attn_in['bo'], 'L0_attn_attn_scale': _L0_attn_in['attn_scale'], 'L0_ffn_gate_w': _L0_ffn_in['gate_w'], 'L0_ffn_gate_b': _L0_ffn_in['gate_b'], 'L0_ffn_We1': _L0_ffn_in['We1'], 'L0_ffn_be1': _L0_ffn_in['be1'], 'L0_ffn_We2': _L0_ffn_in['We2'], 'L0_ffn_be2': _L0_ffn_in['be2'], 'L0_ffn_We3': _L0_ffn_in['We3'], 'L0_ffn_be3': _L0_ffn_in['be3'], 'L0_ffn_ws1': _L0_ffn_in['ws1'], 'L0_ffn_bs1': _L0_ffn_in['bs1'], 'L0_ffn_ws2': _L0_ffn_in['ws2'], 'L0_ffn_bs2': _L0_ffn_in['bs2'], 'L0_ffn_ws3': _L0_ffn_in['ws3'], 'L0_ffn_bs3': _L0_ffn_in['bs3']}
    _x0 = _d['L0_attn_x']
    _d['L0_attn_x'] = jax.random.normal(jax.random.fold_in(jax.random.key(seed), 1), (8, 512, 128), dtype=_x0.dtype)
    del _x0
    return _d

def reference(L0_attn_x, L0_attn_Wq, L0_attn_bq, L0_attn_Wk, L0_attn_bk, L0_attn_Wv, L0_attn_bv, L0_attn_Wo, L0_attn_bo, L0_attn_attn_scale, L0_ffn_gate_w, L0_ffn_gate_b, L0_ffn_We1, L0_ffn_be1, L0_ffn_We2, L0_ffn_be2, L0_ffn_We3, L0_ffn_be3, L0_ffn_ws1, L0_ffn_bs1, L0_ffn_ws2, L0_ffn_bs2, L0_ffn_ws3, L0_ffn_bs3):

    def _L0_attn_ref(x, Wq, bq, Wk, bk, Wv, bv, Wo, bo, attn_scale):
        import jax, jax.numpy as jnp
        import numpy as np
        CHUNK = 64
        HEADS = 16

        def _chunk_mask(T, cs):
            idx = jnp.arange(T)
            blk = idx // cs * cs
            qb = blk[:, None]
            kb = blk[None, :]
            masked = (qb >= kb) & (idx[None, :] - idx[:, None] - 2 * (kb - qb) >= 1)
            return masked
        B, T, C = x.shape
        H = HEADS
        D = C // H
        q = (x @ Wq.T + bq).reshape(B, T, H, D)
        k = (x @ Wk.T + bk).reshape(B, T, H, D)
        v = (x @ Wv.T + bv).reshape(B, T, H, D)
        scores = jnp.einsum('bqhd,bkhd->bhqk', q, k) * attn_scale[0]
        mask = _chunk_mask(T, CHUNK)
        scores = jnp.where(mask[None, None], -jnp.inf, scores)
        attn = jax.nn.softmax(scores, axis=-1)
        out = jnp.einsum('bhqk,bkhd->bqhd', attn, v).reshape(B, T, C)
        return out @ Wo.T + bo

    def _L0_ffn_ref(x, gate_w, gate_b, We1, be1, We2, be2, We3, be3, ws1, bs1, ws2, bs2, ws3, bs3):
        import jax, jax.numpy as jnp
        import numpy as np
        DIM = 128
        E = 16
        TOPK = 2
        G = 4
        TOPK_G = 2
        INTER = 64
        N_SHARED = 2
        ROUTE_SCALE = 1.0

        def _gate(xf, gate_w, gate_b):
            scores = xf @ gate_w.T
            scores = jax.nn.softmax(scores.astype(jnp.float32), axis=-1)
            orig = scores
            scores = scores + gate_b
            T = xf.shape[0]
            sg = scores.reshape(T, G, E // G)
            group_scores = jax.lax.top_k(sg, 2)[0].sum(-1)
            _, gidx = jax.lax.top_k(group_scores, TOPK_G)
            keep = jax.nn.one_hot(gidx, G).sum(axis=1) > 0
            sg = jnp.where(keep[:, :, None], sg, -jnp.inf)
            scores = sg.reshape(T, E)
            _, idx = jax.lax.top_k(scores, TOPK)
            weights = jnp.take_along_axis(orig, idx, axis=1)
            weights = (weights * ROUTE_SCALE).astype(xf.dtype)
            return (weights, idx)
        shape = x.shape
        xf = x.reshape(-1, DIM)
        weights, idx = _gate(xf, gate_w, gate_b)
        combine = (jax.nn.one_hot(idx, E, dtype=xf.dtype) * weights[..., None]).sum(1)
        h1 = jnp.einsum('td,edi->tei', xf, We1) + be1
        h3 = jnp.einsum('td,edi->tei', xf, We3) + be3
        h = jax.nn.silu(h1) * h3
        yo = jnp.einsum('tei,eid->ted', h, We2) + be2
        y = jnp.einsum('te,ted->td', combine, yo)
        z = jax.nn.silu(xf @ ws1 + bs1) * (xf @ ws3 + bs3) @ ws2 + bs2
        return (y + z).reshape(shape)
    x = L0_attn_x
    x = x + _layernorm(_L0_attn_ref(_layernorm(x, axis=-1), L0_attn_Wq, L0_attn_bq, L0_attn_Wk, L0_attn_bk, L0_attn_Wv, L0_attn_bv, L0_attn_Wo, L0_attn_bo, L0_attn_attn_scale), axis=-1)
    x = x + _layernorm(_L0_ffn_ref(_layernorm(x, axis=-1), L0_ffn_gate_w, L0_ffn_gate_b, L0_ffn_We1, L0_ffn_be1, L0_ffn_We2, L0_ffn_be2, L0_ffn_We3, L0_ffn_be3, L0_ffn_ws1, L0_ffn_bs1, L0_ffn_ws2, L0_ffn_bs2, L0_ffn_ws3, L0_ffn_bs3), axis=-1)
    return x

_drawn_inputs = setup_inputs


def setup_inputs(seed=0):
    import zlib

    import numpy as np

    out = dict(_drawn_inputs(seed))
    spreads = {'L0_attn_bq': (0.0, 0.8),
     'L0_attn_bk': (0.0, 0.8),
     'L0_attn_bv': (0.0, 0.1),
     'L0_attn_bo': (0.0, 0.1),
     'L0_ffn_gate_b': (0.0, 0.1),
     'L0_ffn_be1': (0.0, 0.524),
     'L0_ffn_be2': (0.0, 0.364),
     'L0_ffn_be3': (0.0, 0.545),
     'L0_ffn_bs1': (0.0, 0.1),
     'L0_ffn_bs2': (0.0, 0.1),
     'L0_ffn_bs3': (0.0, 0.1)}
    factors = {'L0_attn_Wq': 8.0, 'L0_attn_Wk': 8.0}
    for name, (base, spread) in spreads.items():
        noise = np.random.default_rng([zlib.crc32(name.encode()), seed]).standard_normal(out[name].shape)
        drawn = base * np.exp(spread * noise) if base else spread * noise
        out[name] = jnp.asarray(drawn.astype(out[name].dtype))
    for name, factor in factors.items():
        out[name] = (out[name] * factor).astype(out[name].dtype)
    return out
```

```python
from contextlib import ExitStack

import numpy as np

import concourse.bass as bass
from concourse import mybir

F32 = mybir.dt.float32
F32R = mybir.dt.float32r
BF16 = mybir.dt.bfloat16
ALU = mybir.AluOpType
ACT = mybir.ActivationFunctionType
AX = mybir.AxisListType

P = 128
B, T, C = 8, 512, 128
NT = T // P
CHUNK = 64
H, D = 16, 8
G, HG = 4, 4
E, INTER = 16, 64
NP = 1 + E // 2
EG = 4
VW = 32
EPS = 1e-5
MASKED = -3.0e38
BIG = 1.0e30

ROWS = 3 * HG * D
ROWS_SHIFTED = ROWS + 2 * HG

MAX_UNITS = [(0, (0, 1)), (0, (2, 3)), (1, (0, 1)), (1, (2, 3)), (2, (0, 1, 2, 3)), (3, (0, 1, 2, 3))]
NU = len(MAX_UNITS)
EXP_UNITS = [(3, (0,)), (3, (1,)), (3, (2,)), (3, (3,)), (2, (0,)), (2, (1,)), (2, (2,)), (2, (3,)),
             (1, (0, 1)), (1, (2, 3)), (0, (0, 1, 2, 3))]
NV = len(EXP_UNITS)

USES = ["shift0", "otr0", "otr1", "otr2", "otr3", "xT", "shift1", "q", "k", "onT", "oproj",
        "shift2", "v", "xfT", "shift3", "logits"]
TAIL = ("otr0", "otr1", "otr2", "otr3", "onT", "oproj", "xfT", "logits")
STAGE = ("xT", "q", "k", "v")
FIRST_USES = [u for u in USES if u not in TAIL]
LAST_USES = [u for u in USES if u not in STAGE]

PAIR_DMAS = 2 * 3 + 3 * HG


def use_number(b, name):
    if b is None:
        return STAGE.index(name)
    after_prologue = len(STAGE)
    after_first = after_prologue + len(FIRST_USES)
    if isinstance(b, int) and b == 0:
        return after_prologue + FIRST_USES.index(name)
    if isinstance(b, int) and b == B - 1:
        return after_first + len(USES) * (B - 2) + LAST_USES.index(name)
    if isinstance(b, int) and b == B:
        return after_first + len(USES) * (B - 2) + len(LAST_USES) + TAIL.index(name)
    return b * len(USES) + (after_first - len(USES) + USES.index(name))


def kq_channel_order():
    order = np.zeros(C, np.int64)
    for g in range(G):
        for j in range(HG):
            for d in range(D):
                order[64 * (g // 2) + 16 * j + 2 * d + g % 2] = (HG * g + j) * D + d
    return order


IDENT, MASK, SEL, TRI, REV = 0, P, 2 * P, 2 * P + (NP - 1) * P, 2 * P + (NP - 1) * P + EG * EG
ONES = REV + E
NCONST = ONES + HG


def shape_constants():
    c = np.zeros((P, NCONST), np.float32)
    c[:, IDENT:IDENT + P] = np.eye(P)
    q, k = np.arange(P)[:, None], np.arange(P)[None, :]
    allowed = (k // CHUNK > q // CHUNK) | ((k // CHUNK == q // CHUNK) & (k <= q))
    c[:, MASK:MASK + P] = np.where(allowed, 0.0, MASKED)
    for p in range(NP - 1):
        for col in range(P):
            for half in range(2):
                c[half * E + 2 * p + col // INTER, SEL + p * P + col] = 1.0
    c[:, TRI:TRI + EG * EG] = (np.arange(EG)[None, :] < np.arange(EG)[:, None]).astype(np.float32).reshape(1, -1)
    c[:, REV:REV + E] = E - np.arange(E)
    for j in range(HG):
        c[ROWS + j, ONES + j] = c[ROWS + HG + j, ONES + j] = 1.0
    return c


def block_kernel(nc, x, w_attn, cols, w13, w2, b13, gate_w, rows, be2, const, out):
    ctx = ExitStack()
    with ctx:
        def sb(name, shape, dt=F32):
            return ctx.enter_context(nc.sbuf_tensor(name, shape, dt))

        def sem(name):
            return ctx.enter_context(nc.semaphore(name))

        xall = sb("xall", [P, B * NT, C])
        cst = sb("cst", [P, NCONST])
        ident_bf = sb("ident_bf", [P, P], BF16)
        mask_bf = sb("mask_bf", [P, P], BF16)
        sel = sb("sel", [2 * E, (NP - 1) * P], F32R)
        wa = sb("wa", [P, 4, C])
        wa_hi = sb("wa_hi", [P, 4, C], F32R)
        wa_lo = sb("wa_lo", [P, 4, C], F32R)
        gw = sb("gw", [P, E])
        gw_hi = sb("gw_hi", [P, E], F32R)
        gw_lo = sb("gw_lo", [P, E], F32R)
        col = sb("col", [P, 6])
        b13c = sb("b13c", [P, 2, NP])
        row = sb("row", [P, C + E])
        be = sb("be", [2 * E, C])
        be_hi = sb("be_hi", [2 * E, C], F32R)
        be_lo = sb("be_lo", [2 * E, C], F32R)
        w13_hi = sb("w13_hi", [P, 2, NP, P], F32R)
        w13_lo = sb("w13_lo", [P, 2, NP, P], F32R)
        w2_hi = sb("w2_hi", [P, NP, C], F32R)
        w2_lo = sb("w2_lo", [P, NP, C], F32R)
        halfneg = sb("halfneg", [P, NT])
        pt = sb("pt", [P, NT, HG, T])
        km = sb("km", [P, G, HG, T], F32R)
        qd = sb("qd", [P, G, T], F32R)
        vaug = sb("vaug", [P, NT, H, VW])
        xn = sb("xn", [P, NT, C])
        xnT_hi = sb("xnT_hi", [P, T], F32R)
        xnT_lo = sb("xnT_lo", [P, T], F32R)
        qk_f = sb("qk_f", [P, 2, T])
        qk_hi = sb("qk_hi", [P, 2, T], F32R)
        qk_lo = sb("qk_lo", [P, 2, T], F32R)
        vraw = sb("vraw", [P, NT, C])
        negmax = sb("negmax", [P, 2, NT, HG])
        shift = sb("shift", [P, NT, 2 * HG])
        o_raw = sb("o_raw", [P, G, T])
        rsum = sb("rsum", [P, NT, H])
        on = sb("on", [P, NT, C])
        oT_hi = sb("oT_hi", [P, T], F32R)
        oT_lo = sb("oT_lo", [P, T], F32R)
        att = sb("att", [P, NT, C])
        attn_n = sb("attn_n", [P, NT, C])
        xf = sb("xf", [P, NT, C])
        bst = sb("bst", [P, 4, NT, 6])
        mv = sb("mv", [P, 4, NT, 2])
        ve = sb("ve", [P, 4, NT])
        rstd = sb("rstd", [P, 4, NT])
        xfT_hi = [sb(f"xfT_hi{i}", [P, T], F32R) for i in range(2)]
        xfT_lo = [sb(f"xfT_lo{i}", [P, T], F32R) for i in range(2)]
        xfT_kept = nc.dram_tensor("xfT_kept", [2, P, B * T], F32, kind="Internal").ap()
        xfs_hi = sb("xfs_hi", [P, T], F32R)
        xfs_lo = sb("xfs_lo", [P, T], F32R)
        lmax = sb("lmax", [P, NT])
        lsub = sb("lsub", [P, NT, E])
        gexp = sb("gexp", [P, B, NT, E])
        ptf = pt[:, :, :, :].rearrange("p k h t -> p (k h) t")
        silu = [ptf[:, i, :] for i in range(3)]
        gated = [ptf[:, 3 + i, :] for i in range(3)]
        hbuf = [ptf[:, 6 + i, :] for i in range(3)]
        y_sb = ptf[:, 9, :]
        y_n = ptf[:, 10, :].rearrange("p (t c) -> p t c", t=NT)
        out_sb = ptf[:, 11, :].rearrange("p (t c) -> p t c", t=NT)
        kmf = km[:, :, :, :].rearrange("p g j t -> p (g j) t")
        h_hi = [kmf[:, i, :] for i in range(3)]
        h_lo = [kmf[:, 3 + i, :] for i in range(3)]
        cT = [kmf[0:2 * E, 6 + i, :] for i in range(2)]
        comb = sb("comb", [P, NT, 2 * E])
        comb_all = sb("comb_all", [P, B * NT, E])
        rt = [ptf[:, i, :].rearrange("p (t e) -> p t e", e=E) for i in range(14)]
        rs = [ptf[:, 14 + i // 4, 128 * (i % 4):128 * (i % 4) + 128].rearrange("p (t g) -> p t g", g=EG)
              for i in range(8)]
        rm = [sb(f"rm{i}", [P, B * NT]) for i in range(6)]

        ps_a = [ctx.enter_context(nc.psum_tensor(f"ps_a{i}", [P, 1024], F32)) for i in range(2)]
        ps_b = [ctx.enter_context(nc.psum_tensor(f"ps_b{i}", [P, 512], F32)) for i in range(2)]
        ps_o = ctx.enter_context(nc.psum_tensor("ps_o", [P, 512], F32))
        ps_m = ctx.enter_context(nc.psum_tensor("ps_m", [P, 512], F32))
        ps_h1 = [ps_a[0][:, 512 * i:512 * i + 512] for i in range(2)]
        ps_h3 = [ps_a[1][:, 512 * i:512 * i + 512] for i in range(2)]
        ps_c = ps_b
        ps_y = ps_o

        x_first, x_rest = sem("x_first"), sem("x_rest")
        const_in, wattn_in, w_in = sem("const_in"), sem("wattn_in"), sem("w_in")
        attn_weights, small_hi = sem("attn_weights"), sem("small_hi")
        weights_hi, weights_lo = sem("weights_hi"), sem("weights_lo")
        operands_cleared, ones_placed, half_set = sem("operands_cleared"), sem("ones_placed"), sem("half_set")
        scores_ready, maxes_done = sem("scores_ready"), sem("maxes_done")
        shift_hi, shift_split = sem("shift_hi"), sem("shift_split")
        st_ready, exps_done, masks_done = sem("st_ready"), sem("exps_done"), sem("masks_done")
        pv_done, o_evacuated = sem("pv_done"), sem("o_evacuated")
        misc_ready, misc_evacuated = sem("misc_ready"), sem("misc_evacuated")
        xT_hi, onT_hi, xfT_hi_done = sem("xT_hi"), sem("onT_hi"), sem("xfT_hi_done")
        stats = [sem(f"stats{i}") for i in range(4)]
        moments = [sem(f"moments{i}") for i in range(4)]
        eps_added = [sem(f"eps_added{i}") for i in range(4)]
        rstds = [sem(f"rstds{i}") for i in range(4)]
        xn_ready, attn_normed, x2_ready, xf_ready = sem("xn_ready"), sem("attn_normed"), sem("x2_ready"), sem("xf_ready")
        sums_inverted, logit_max, gate_exp = sem("sums_inverted"), sem("logit_max"), sem("gate_exp")
        qk_split, v_placed = sem("qk_split"), sem("v_placed")
        kq_in = [sem("kq_in0"), sem("kq_in1")]
        h1_ready, h3_ready, silu_done, gated_done, h_done = (
            sem("h1_ready"), sem("h3_ready"), sem("silu_done"), sem("gated_done"), sem("h_done"))
        h_hi_done, h_split, down_done = sem("h_hi_done"), sem("h_split"), sem("down_done")
        y_evacuated, yT_ready, y_normed = sem("y_evacuated"), sem("yT_ready"), sem("y_normed")
        router_step, cT_in_psum, cT_ready = sem("router_step"), sem("cT_in_psum"), sem("cT_ready")
        xf_saved, combine_ready, comb_hi, km_zeroed = sem("xf_saved"), sem("combine_ready"), sem("comb_hi"), sem("km_zeroed")
        xf_in = [sem("xf_in0"), sem("xf_in1")]
        wait_carrier = [sem("wait_carrier_dve"), sem("wait_carrier_pool")]
        out_ready, stored = sem("out_ready"), sem("stored")

        block = ctx.enter_context(nc.Block())

        def tile_of(b, t):
            return bass.ds(b * NT + t, 1) if not isinstance(b, int) else slice(b * NT + t, b * NT + t + 1)

        def batch_of(b, width):
            return bass.ds(b * width, width) if not isinstance(b, int) else slice(b * width, (b + 1) * width)

        x_dram = x.rearrange("(n p) c -> p n c", p=P)
        out_dram = out.rearrange("(n p) c -> p n c", p=P)

        @block.sync
        def _(sp):
            sp.sem_inc(xf_saved, 1)
            sp.sem_inc(stored, 1)
            sp.dma_start(xall[:, 0:NT, :], x_dram[:, 0:NT, :]).then_inc(x_first, 16)
            sp.dma_start(wa[:, :, :], w_attn).then_inc(wattn_in, 16)
            sp.dma_start(cst[:, :], const).then_inc(const_in, 16)
            sp.dma_start(col[:, 0:5], cols).then_inc(const_in, 16)
            sp.dma_start(xall[:, NT:, :], x_dram[:, NT:, :]).then_inc(x_rest, 16)
            sp.dma_start(row[:, :], rows).then_inc(const_in, 16)
            sp.dma_start(gw[:, :], gate_w).then_inc(const_in, 16)
            sp.dma_start(be[:, :], be2).then_inc(const_in, 16)
            sp.dma_start(b13c[:, :, :], b13).then_inc(const_in, 16)
            sp.dma_start(ptf[:, 0:5, :].rearrange("p a b -> p (a b)")[:, 0:2 * NP * P], w13).then_inc(w_in, 16)
            sp.dma_start(ptf[:, 5:8, :].rearrange("p a b -> p (a b)")[:, 0:NP * C], w2).then_inc(w_in, 16)

            def place_pair(s, pair):
                if isinstance(s, int) and s == 0:
                    sp.wait_ge(qk_split, 2)
                    sp.wait_ge(operands_cleared, 1)
                else:
                    sp.wait_ge(qk_split, s * 2 + 2)
                    sp.wait_ge(st_ready, s * (G * NV) + (NV * (2 * pair + 2) - G * NV))
                for part, src in ((0, qk_hi), (1, qk_lo), (2, qk_hi)):
                    for j in range(HG):
                        sp.dma_start(km[32 * part + D * j:32 * part + D * (j + 1), 2 * pair:2 * pair + 2, j, :].bitcast(F32),
                                     src[64 * pair + 16 * j:64 * pair + 16 * (j + 1), 1, :].bitcast(F32)
                                     ).then_inc(kq_in[pair], 16)
                for part, src in ((0, qk_hi), (1, qk_hi), (2, qk_lo)):
                    for g in (0, 1):
                        sp.dma_start(qd[32 * part:32 * part + 32, 2 * pair + g, :].bitcast(F32),
                                     src[64 * pair + g:64 * pair + 64:2, 0, :].bitcast(F32)).then_inc(kq_in[pair], 16)

            for pair in range(2):
                place_pair(0, pair)
            def save_xf(b, number):
                sp.wait_ge(misc_evacuated, number + 1)
                sp.dma_start(xfT_kept[0, :, batch_of(b, T)], xfs_hi[:, :].bitcast(F32)).then_inc(xf_saved, 16)
                sp.dma_start(xfT_kept[1, :, batch_of(b, T)], xfs_lo[:, :].bitcast(F32)).then_inc(xf_saved, 16)

            def load_xf(b, parity):
                if not (isinstance(b, int) and b < 2):
                    sp.wait_ge(h3_ready, (b - 1) * NP)
                sp.dma_start(xfT_hi[parity][:, :].bitcast(F32), xfT_kept[0, :, batch_of(b, T)]).then_inc(xf_in[parity], 16)
                sp.dma_start(xfT_lo[parity][:, :].bitcast(F32), xfT_kept[1, :, batch_of(b, T)]).then_inc(xf_in[parity], 16)

            def store_out(b):
                sp.wait_ge(out_ready, b + 1)
                sp.dma_start(out_dram[:, batch_of(b, NT), :], out_sb).then_inc(stored, 16)

            for pair in range(2):
                place_pair(1, pair)
            with sp.Fori(1, B - 1) as b:
                place_pair(b + 1, 0)
                save_xf(b - 1, use_number(b, "xfT"))
                place_pair(b + 1, 1)
            save_xf(B - 2, use_number(B - 1, "xfT"))
            save_xf(B - 1, use_number(B, "xfT"))
            sp.wait_ge(xf_saved, 32 * B + 1)
            load_xf(0, 0)
            load_xf(1, 1)
            load_xf(2, 0)
            with sp.Fori(0, B // 2 - 2) as i:
                store_out(i * 2)
                load_xf(i * 2 + 3, 1)
                store_out(i * 2 + 1)
                load_xf(i * 2 + 4, 0)
            store_out(B - 4)
            load_xf(B - 1, 1)
            for b in range(B - 3, B):
                store_out(b)
            sp.wait_ge(stored, 16 * B + 1)

        @block.tensor
        def _(pe):
            ident = cst[:, IDENT:IDENT + P]

            def claim_misc(number):
                if not (isinstance(number, int) and number == 0):
                    pe.wait_ge(misc_evacuated, number)

            def three_pass(dst, lhs_hi, lhs_lo, rhs_hi, rhs_lo, start=True, stop=True):
                nc.tensor.matmul(dst, lhs_hi, rhs_hi, start=start, stop=False)
                nc.tensor.matmul(dst, lhs_hi, rhs_lo, start=False, stop=False)
                return nc.tensor.matmul(dst, lhs_lo, rhs_hi, start=False, stop=stop)

            def transpose_tiles(number, src):
                claim_misc(number)
                for t in range(NT):
                    last = nc.tensor.transpose(ps_m[:, P * t:P * t + P], src[:, t, :], ident)
                last.then_inc(misc_ready, 1)

            def project_T(number, which):
                claim_misc(number)
                three_pass(ps_m[:, :], wa_hi[:, which, :], wa_lo[:, which, :], xnT_hi[:, :], xnT_lo[:, :]
                           ).then_inc(misc_ready, 1)

            def project_tokens(number, which, src_hi, src_lo):
                claim_misc(number)
                for t in range(NT):
                    s = slice(P * t, P * t + P)
                    last = three_pass(ps_m[:, s], src_hi[:, s], src_lo[:, s], wa_hi[:, which, :], wa_lo[:, which, :])
                last.then_inc(misc_ready, 1)

            def scores(b, g, u):
                t, heads = MAX_UNITS[u]
                n6 = b * (G * NU) + (g * NU + u)
                if not (isinstance(b, int) and b == 0 and g == 0 and u < 2):
                    pe.wait_ge(maxes_done, n6 - 1)
                if u == 0 and g % 2 == 0:
                    pe.wait_ge(kq_in[g // 2], b * (16 * PAIR_DMAS) + 16 * PAIR_DMAS)
                width = T - P * t
                pitch = 512 if width > 256 else width
                a = ps_a[u % 2]
                for i, j in enumerate(heads):
                    o = i * pitch
                    nc.tensor.matmul(a[:, o:o + width], qd[0:ROWS, g, P * t:P * t + P], km[0:ROWS, g, j, P * t:T],
                                     start=True, stop=False)
                    last = nc.tensor.matmul(a[:, o:o + P], ident_bf[:, :], mask_bf[:, :], start=False, stop=True)
                last.then_inc(scores_ready, 1)

            def shift_rows(b, g, number):
                pe.wait_ge(shift_split, b * G + (g + 1))
                claim_misc(number)
                for t in range(NT):
                    last = nc.tensor.transpose(ps_m[0:2 * HG, P * t:P * t + P], shift[:, t, :], ident)
                last.then_inc(misc_ready, 1)

            def scores_T(b, g, v, number):
                k, heads = EXP_UNITS[v]
                if v == 0:
                    pe.wait_ge(misc_evacuated, number + 1)
                if not (isinstance(b, int) and b == 0 and g == 0 and v < 2):
                    pe.wait_ge(exps_done, b * (G * NV) + (g * NV + v - 1))
                width = P * (k + 1)
                bank = ps_b[(g * NV + v) % 2]
                for i, j in enumerate(heads):
                    last = nc.tensor.matmul(bank[:, i * width:i * width + width],
                                            km[0:ROWS_SHIFTED, g, j, P * k:P * k + P],
                                            qd[0:ROWS_SHIFTED, g, 0:width], start=True, stop=True)
                last.then_inc(st_ready, 1)

            def values(b, g, k):
                n = b * G + g
                if k == NT - 1:
                    pe.wait_ge(v_placed, n + 1)
                    if not (isinstance(n, int) and n == 0):
                        pe.wait_ge(o_evacuated, n)
                pe.wait_ge(masks_done, n * 6 + (3 if k >= 2 else 6))
                width = P * (k + 1)
                for j in range(HG):
                    last = nc.tensor.matmul(ps_o[32 * j:32 * j + VW, 0:width], vaug[:, k, HG * g + j, :],
                                            pt[:, k, j, T - width:T], start=k == NT - 1, stop=k == 0)
                last.then_inc(pv_done, 1)

            def o_transposes(b, t, number):
                if t == 0:
                    pe.wait_ge(o_evacuated, b * G + G)
                claim_misc(number)
                for g in range(G):
                    last = nc.tensor.transpose(ps_m[:, P * g:P * g + P], o_raw[:, g, P * t:P * t + P], ident)
                last.then_inc(misc_ready, 1)

            def logits(b, number):
                claim_misc(number)
                for t in range(NT):
                    hi, lo = xfs_hi[:, P * t:P * t + P], xfs_lo[:, P * t:P * t + P]
                    last = three_pass(ps_m[:, E * t:E * t + E], hi, lo, gw_hi[:, :], gw_lo[:, :])
                last.then_inc(misc_ready, 1)

            def iteration(b, tail, stage):
                def use(name):
                    return use_number(b, name)

                for g in range(G):
                    follows = stage or g < G - 1
                    nb, ng = (b, g + 1) if g < G - 1 else (b + 1, 0)
                    pb, pg = (b, g - 1) if g else (b - 1, G - 1)
                    if follows:
                        scores(nb, ng, 0)
                    if tail or g:
                        values(pb, pg, 1)
                        values(pb, pg, 0)
                    if follows:
                        scores(nb, ng, 1)
                    shift_rows(b, g, use(f"shift{g}"))
                    if g == 0 and tail:
                        o_transposes(b - 1, 0, use("otr0"))
                    scores_T(b, g, 0, use(f"shift{g}"))
                    scores_T(b, g, 1, None)
                    if follows:
                        scores(nb, ng, 2)
                    if g == 0 and tail:
                        o_transposes(b - 1, 1, use("otr1"))
                    if g == 1 and stage:
                        project_T(use("q"), 0)
                    if g == 2 and stage:
                        project_tokens(use("v"), 2, xnT_hi, xnT_lo)
                    scores_T(b, g, 2, None)
                    scores_T(b, g, 3, None)
                    if follows:
                        scores(nb, ng, 3)
                    if g == 0 and tail:
                        o_transposes(b - 1, 2, use("otr2"))
                    if g == 1 and stage:
                        project_T(use("k"), 1)
                    scores_T(b, g, 4, None)
                    scores_T(b, g, 5, None)
                    if g == 0 and tail:
                        o_transposes(b - 1, 3, use("otr3"))
                    if g == 1 and tail:
                        transpose_tiles(use("onT"), on)
                    if follows:
                        scores(nb, ng, 4)
                    scores_T(b, g, 6, None)
                    scores_T(b, g, 7, None)
                    if g == 0 and stage:
                        pe.wait_ge(xn_ready, b + 2)
                        transpose_tiles(use("xT"), xn)
                    if g == 1 and tail:
                        project_tokens(use("oproj"), 3, oT_hi, oT_lo)
                    if g == 3 and tail:
                        logits(b - 1, use("logits"))
                    scores_T(b, g, 8, None)
                    if follows:
                        scores(nb, ng, 5)
                    values(b, g, 3)
                    if g == 2 and tail:
                        pe.wait_ge(xf_ready, b)
                        transpose_tiles(use("xfT"), xf)
                    scores_T(b, g, 9, None)
                    scores_T(b, g, 10, None)
                    values(b, g, 2)

            pe.wait_ge(const_in, 96)
            pe.wait_ge(xn_ready, 1)
            transpose_tiles(use_number(None, "xT"), xn)
            pe.wait_ge(attn_weights, 2)
            project_T(use_number(None, "q"), 0)
            project_T(use_number(None, "k"), 1)
            project_tokens(use_number(None, "v"), 2, xnT_hi, xnT_lo)
            pe.wait_ge(small_hi, 3)
            for u in range(NU):
                scores(0, 0, u)
            iteration(0, tail=False, stage=True)
            with pe.Fori(1, B - 1) as b:
                iteration(b, tail=True, stage=True)
            iteration(B - 1, tail=True, stage=False)
            values(B - 1, G - 1, 1)
            values(B - 1, G - 1, 0)
            for t in range(NT):
                o_transposes(B - 1, t, use_number(B, f"otr{t}"))
            transpose_tiles(use_number(B, "onT"), on)
            project_tokens(use_number(B, "oproj"), 3, oT_hi, oT_lo)
            pe.wait_ge(xf_ready, B)
            transpose_tiles(use_number(B, "xfT"), xf)
            logits(B - 1, use_number(B, "logits"))

            def unit(b, p, par, down_prev):
                q = b * NP + p
                odd = (par + p) % 2
                if p == 0:
                    pe.wait_ge(xf_in[odd], 32 * (b // 2) + 32 if isinstance(b, int) else (b - odd) * 16 + 32)
                xs_hi, xs_lo = xfT_hi[odd][:, :], xfT_lo[odd][:, :]
                early = isinstance(q, int) and q < 2
                if not early:
                    pe.wait_ge(silu_done, q - 1)
                three_pass(ps_h1[par], w13_hi[:, 0, p, :], w13_lo[:, 0, p, :], xs_hi, xs_lo
                           ).then_inc(h1_ready, 1)
                if not early:
                    pe.wait_ge(h_done, q - 1)
                last = three_pass(ps_h3[par], w13_hi[:, 1, p, :], w13_lo[:, 1, p, :], xs_hi, xs_lo)
                if p >= 1:
                    if p == 1:
                        pe.wait_ge(cT_ready, b + 1)
                    last = nc.tensor.matmul(ps_c[par][:, :], sel[:, P * (p - 1):P * p], cT[b_parity(b, par, p)],
                                            start=True, stop=True)
                last.then_inc(h3_ready, 1)
                if down_prev:
                    down(b if p >= 2 else b - 1, (p - 2) % NP, par)

            def b_parity(b, par, p):
                return (par + p) % 2

            def down(b, p, par):
                q = b * NP + p
                if p == 0 and not (isinstance(b, int) and b == 0):
                    pe.wait_ge(y_evacuated, b)
                pe.wait_ge(h_split, q + 1)
                if p == 1:
                    c = cT[b_parity(b, par, p)]
                    nc.tensor.matmul(ps_y[:, :], be_hi[:, :], c, start=False, stop=False)
                    nc.tensor.matmul(ps_y[:, :], be_lo[:, :], c, start=False, stop=False)
                last = three_pass(ps_y[:, :], w2_hi[:, p, :], w2_lo[:, p, :], h_hi[p % 3], h_lo[p % 3],
                                  start=p == 0, stop=p == NP - 1)
                last.then_inc(down_done, 1)

            def y_transposes(b):
                pe.wait_ge(y_evacuated, b + 1)
                pe.wait_ge(cT_ready, min(b + 2, B) if isinstance(b, int) else b + 2)
                for t in range(NT):
                    last = nc.tensor.transpose(ps_m[:, P * t:P * t + P], y_sb[:, P * t:P * t + P], ident)
                last.then_inc(yT_ready, 1)

            def c_transposes(b):
                pe.wait_ge(combine_ready, b + 1)
                for t in range(NT):
                    last = nc.tensor.transpose(ps_m[0:2 * E, P * t:P * t + P], comb[:, t, :], ident)
                last.then_inc(cT_in_psum, 1)

            def expert_batch(b, parity, first, last_batch):
                for p in range(NP):
                    unit(b, p, (parity + p) % 2, not first or p >= 2)
                    if p == 4 and not first:
                        y_transposes(b - 1)
                    if p == 7 and not last_batch:
                        if not first:
                            pe.wait_ge(y_normed, b)
                        c_transposes(b + 1)

            pe.wait_ge(maxes_done, B * G * NU)
            pe.wait_ge(exps_done, B * G * NV)
            pe.wait_ge(o_evacuated, B * G)
            pe.wait_ge(misc_evacuated, use_number(B, "logits") + 1)
            pe.wait_ge(weights_lo, 4)
            c_transposes(0)
            expert_batch(0, 0, True, False)
            with pe.Fori(0, B // 2 - 1) as i:
                expert_batch(i * 2 + 1, 1, False, False)
                expert_batch(i * 2 + 2, 0, False, False)
            expert_batch(B - 1, 1, False, True)
            down(B - 1, NP - 2, (B - 1 + NP - 2) % 2)
            down(B - 1, NP - 1, (B - 1 + NP - 1) % 2)
            y_transposes(B - 1)

        @block.scalar
        def _(act):
            def split_hi(number, dst, bias, done):
                act.wait_ge(misc_ready, number + 1)
                nc.scalar.activation(dst, ps_m[:, :], ACT.Identity, bias=bias).then_inc(done, 1)

            def read_qk(s, number, which):
                if which == 0 and not (isinstance(s, int) and s == 0):
                    for pair in range(2):
                        act.wait_ge(kq_in[pair], s * (16 * PAIR_DMAS))
                act.wait_ge(misc_ready, number + 1)
                scale, bias = (col[:, 4:5], col[:, 5:6]) if which == 0 else (1.0, col[:, 1:2])
                nc.scalar.activation(qk_hi[:, which, :], ps_m[:, :], ACT.Identity, bias=bias, scale=scale)
                nc.scalar.activation(qk_f[:, which, :], ps_m[:, :], ACT.Identity, bias=bias, scale=scale
                                     ).then_inc(misc_evacuated, 1)

            def read_v(s, number):
                if not (isinstance(s, int) and s == 0):
                    act.wait_ge(v_placed, s * G)
                act.wait_ge(misc_ready, number + 1)
                nc.scalar.activation(vraw[:, :, :].rearrange("p t c -> p (t c)"), ps_m[:, :], ACT.Identity
                                     ).then_inc(misc_evacuated, 1)

            def place_shift(b, g, number):
                act.wait_ge(misc_ready, number + 1)
                nc.scalar.activation(qd[ROWS:ROWS_SHIFTED, g, :], ps_m[0:2 * HG, :], ACT.Identity
                                     ).then_inc(misc_evacuated, 1)

            def exponentials(b, g, v):
                k, heads = EXP_UNITS[v]
                n = b * G + g
                if v in (0, 4, 8, 10) and not (isinstance(n, int) and n == 0):
                    act.wait_ge(pv_done, n * NT - k)
                act.wait_ge(st_ready, n * NV + (v + 1))
                width = P * (k + 1)
                src = ps_b[(g * NV + v) % 2][:, 0:len(heads) * width].rearrange("p (h q) -> p h q", q=width)
                nc.scalar.activation(pt[:, k, heads[0]:heads[0] + len(heads), T - width:T], src, ACT.Exp
                                     ).then_inc(exps_done, 1)

            def evacuate_o(b, g):
                act.wait_ge(pv_done, (b * G + g) * NT + NT)
                nc.scalar.activation(o_raw[:, g, :], ps_o[:, :], ACT.Identity).then_inc(o_evacuated, 1)

            def gate_exponentials(b, number):
                act.wait_ge(misc_evacuated, number + 1)
                nc.scalar.activation(gexp[:, batch_of(b, 1), :, :].rearrange("p a t e -> p (a t) e"), lsub[:, :, :],
                                     ACT.Exp).then_inc(gate_exp, 1)

            def iteration(b, tail, stage):
                def use(name):
                    return use_number(b, name)

                for g in range(G):
                    if tail or g:
                        pb, pg = (b, g - 1) if g else (b - 1, G - 1)
                        if tail and g == 1:
                            act.wait_ge(misc_ready, use("otr3") + 1)
                        evacuate_o(pb, pg)
                    place_shift(b, g, use(f"shift{g}"))
                    for v in range(NV):
                        if v == 4 and g == 1 and stage:
                            read_qk(b + 1, use("q"), 0)
                        if v == 5 and g == 2 and stage:
                            read_v(b + 1, use("v"))
                        if v == 6 and g == 1 and stage:
                            read_qk(b + 1, use("k"), 1)
                        if v == 7 and g == 1 and tail:
                            split_hi(use("onT"), oT_hi[:, :], col[:, 2:3], onT_hi)
                        if v == 10 and g == 2 and tail:
                            act.wait_ge(xf_saved, (b - 1) * 32 + 1)
                            split_hi(use("xfT"), xfs_hi[:, :], 0.0, xfT_hi_done)
                        if v == 9 and g == 0 and stage:
                            split_hi(use("xT"), xnT_hi[:, :], 0.0, xT_hi)
                        exponentials(b, g, v)
                    if g == 3 and tail:
                        gate_exponentials(b - 1, use("logits"))

            act.wait_ge(wattn_in, 16)
            nc.scalar.activation(wa_hi[:, :, :], wa[:, :, :], ACT.Identity).then_inc(attn_weights, 1)
            act.wait_ge(const_in, 96)
            nc.scalar.activation(ident_bf[:, :], cst[:, IDENT:IDENT + P], ACT.Identity).then_inc(small_hi, 1)
            nc.scalar.activation(mask_bf[:, :], cst[:, MASK:MASK + P], ACT.Identity).then_inc(small_hi, 1)
            nc.scalar.activation(col[:, 5:6], col[:, 0:1], ACT.Identity, scale=col[:, 4:5]).then_inc(small_hi, 1)
            split_hi(use_number(None, "xT"), xnT_hi[:, :], 0.0, xT_hi)
            act.wait_ge(small_hi, 3)
            read_qk(0, use_number(None, "q"), 0)
            read_qk(0, use_number(None, "k"), 1)
            read_v(0, use_number(None, "v"))
            nc.scalar.activation(gw_hi[:, :], gw[:, :], ACT.Identity).then_inc(weights_hi, 1)
            nc.scalar.activation(be_hi[:, :], be[:, :], ACT.Identity).then_inc(weights_hi, 1)
            nc.scalar.activation(sel[:, :], cst[0:2 * E, SEL:TRI], ACT.Identity).then_inc(weights_hi, 1)
            act.wait_ge(w_in, 32)
            nc.scalar.activation(w13_hi[:, :, :, :].rearrange("p a b c -> p (a b c)"),
                                 ptf[:, 0:5, :].rearrange("p a b -> p (a b)")[:, 0:2 * NP * P], ACT.Identity
                                 ).then_inc(weights_hi, 1)
            nc.scalar.activation(w2_hi[:, :, :].rearrange("p b c -> p (b c)"),
                                 ptf[:, 5:8, :].rearrange("p a b -> p (a b)")[:, 0:NP * C], ACT.Identity
                                 ).then_inc(weights_hi, 1)
            act.wait_ge(weights_lo, 4)
            iteration(0, tail=False, stage=True)
            with act.Fori(1, B - 1) as b:
                iteration(b, tail=True, stage=True)
            iteration(B - 1, tail=True, stage=False)
            evacuate_o(B - 1, G - 1)
            split_hi(use_number(B, "onT"), oT_hi[:, :], col[:, 2:3], onT_hi)
            act.wait_ge(xf_saved, (B - 1) * 32 + 1)
            split_hi(use_number(B, "xfT"), xfs_hi[:, :], 0.0, xfT_hi_done)
            gate_exponentials(B - 1, use_number(B, "logits"))

            def silu_tile(b, p, par):
                q = b * NP + p
                act.wait_ge(h1_ready, q + 1)
                if not (isinstance(q, int) and q < 3):
                    act.wait_ge(h_done, q - 2)
                nc.scalar.activation(silu[p % 3], ps_h1[par], ACT.Silu, bias=b13c[:, 0, p:p + 1]).then_inc(silu_done, 1)

            def hidden_hi(b, p):
                q = b * NP + p
                act.wait_ge(h_done, q + 1)
                if not (isinstance(q, int) and q < 3):
                    act.wait_ge(down_done, q - 2)
                nc.scalar.activation(h_hi[p % 3], hbuf[p % 3], ACT.Identity).then_inc(h_hi_done, 1)

            def evacuate_y(b):
                act.wait_ge(down_done, b * NP + NP)
                nc.scalar.activation(y_sb, ps_y[:, :], ACT.Identity, bias=col[:, 3:4]).then_inc(y_evacuated, 1)

            def evacuate_c(b, parity):
                act.wait_ge(cT_in_psum, b + 1)
                nc.scalar.activation(cT[parity], ps_m[0:2 * E, :], ACT.Identity).then_inc(cT_ready, 1)

            def expert_batch(b, parity, first, last_batch):
                for p in range(NP):
                    if p == 2 and not first:
                        evacuate_y(b - 1)
                    silu_tile(b, p, (parity + p) % 2)
                    if not first or p >= 1:
                        hidden_hi(b if p else b - 1, (p - 1) % NP)
                    if p == NP - 1 and not last_batch:
                        evacuate_c(b + 1, 1 - parity)

            act.wait_ge(pv_done, B * G * NT)
            act.wait_ge(st_ready, B * G * NV)
            evacuate_c(0, 0)
            expert_batch(0, 0, True, False)
            with act.Fori(0, B // 2 - 1) as i:
                expert_batch(i * 2 + 1, 1, False, False)
                expert_batch(i * 2 + 2, 0, False, False)
            expert_batch(B - 1, 1, False, True)
            hidden_hi(B - 1, NP - 1)
            evacuate_y(B - 1)

        @block.vector
        def _(dve):
            def norm_stats(i, count, tiles):
                for t in range(NT):
                    nc.vector.bn_stats(bst[:, i, t, :], tiles(t)).then_inc(stats[i], 1)
                dve.wait_ge(stats[i], count * NT + NT)
                dve.sem_inc(wait_carrier[0], 1)
                for t in range(NT):
                    last = nc.vector.bn_aggr(mv[:, i, t, :], bst[:, i, t, :])
                last.then_inc(moments[i], 1)

            def normalise(i, count, tiles, dst, done):
                dve.wait_ge(rstds[i], count + 1)
                for t in range(NT):
                    last = nc.vector.tensor_scalar(dst[:, t, :], tiles(t), mv[:, i, t, 0:1], rstd[:, i, t:t + 1],
                                                   ALU.subtract, ALU.mult)
                last.then_inc(done, 1)

            def x_tile(b):
                return lambda t: xall[:, tile_of(b, t), :].rearrange("p a c -> p (a c)")

            def tile_in(buf):
                return lambda t: buf[:, t, :]

            def split_lo(dst, hi, hi_done, count, bias=0.0):
                dve.wait_ge(hi_done, count + 1)
                nc.vector.scalar_tensor_tensor(dst, ps_m[:, :], bias, hi.bitcast(F32), ALU.add, ALU.subtract
                                               ).then_inc(misc_evacuated, 1)

            def maxima(b, g, u):
                t, heads = MAX_UNITS[u]
                n = b * G + g
                if u == 0 and not (isinstance(n, int) and n < 2):
                    dve.wait_ge(shift_split, n - 1)
                dve.wait_ge(scores_ready, n * NU + (u + 1))
                width = T - P * t
                pitch = 512 if width > 256 else width
                src = ps_a[u % 2][:, 0:len(heads) * pitch].rearrange("p (h k) -> p h k", k=pitch)[:, :, 0:width]
                nc.vector.tensor_reduce(negmax[:, g % 2, t, heads[0]:heads[0] + len(heads)], src, AX.X, ALU.max,
                                        negate=True).then_inc(maxes_done, 1)

            def normalise_o(b, t, number):
                dve.wait_ge(misc_ready, number + 1)
                heads = ps_m[:, :].rearrange("p (h w) -> p h w", w=VW)
                nc.vector.reciprocal(rsum[:, t, :], heads[:, :, D]).then_inc(sums_inverted, 1)
                dve.wait_ge(sums_inverted, b * NT + (t + 1))
                nc.vector.tensor_tensor(on[:, t, :].rearrange("p (h d) -> p h d", d=D), heads[:, :, 0:D],
                                        rsum[:, t, :].unsqueeze(2).broadcast_to([P, H, D]), ALU.mult
                                        ).then_inc(misc_evacuated, 1)

            def add_bo(number):
                dve.wait_ge(misc_ready, number + 1)
                nc.vector.tensor_tensor(att[:, :, :], ps_m[:, :].rearrange("p (t c) -> p t c", t=NT),
                                        row[:, 0:C].unsqueeze(1).broadcast_to([P, NT, C]), ALU.add
                                        ).then_inc(misc_evacuated, 1)

            def shift_logits(b, number):
                dve.wait_ge(misc_ready, number + 1)
                lg = ps_m[:, 0:NT * E].rearrange("p (t e) -> p t e", e=E)
                nc.vector.tensor_reduce(lmax[:, :], lg, AX.X, ALU.max).then_inc(logit_max, 1)
                dve.wait_ge(logit_max, b + 1)
                nc.vector.tensor_tensor(lsub[:, :, :], lg, lmax[:, :].unsqueeze(2).broadcast_to([P, NT, E]),
                                        ALU.subtract).then_inc(misc_evacuated, 1)

            def iteration(b, tail, stage):
                def use(name):
                    return use_number(b, name)

                for g in range(G):
                    follows = stage or g < G - 1
                    nb, ng = (b, g + 1) if g < G - 1 else (b + 1, 0)
                    for u in range(NU):
                        if u >= 2 and g == 0 and tail:
                            normalise_o(b - 1, u - 2, use(f"otr{u - 2}"))
                        if u == 5 and g == 1 and tail:
                            split_lo(oT_lo[:, :], oT_hi[:, :], onT_hi, b - 1, col[:, 2:3])
                        if follows:
                            maxima(nb, ng, u)
                        if g == 0 and u == 0 and stage:
                            if isinstance(b, int):
                                dve.wait_ge(x_rest, 16)
                            norm_stats(0, b + 1, x_tile(b + 1))
                        if g == 0 and u == 2 and stage:
                            normalise(0, b + 1, x_tile(b + 1), xn, xn_ready)
                        if g == 2 and u == 0 and tail:
                            dve.wait_ge(misc_evacuated, use("oproj") + 1)
                            norm_stats(1, b - 1, tile_in(att))
                        if g == 2 and u == 1 and tail:
                            normalise(1, b - 1, tile_in(att), attn_n, attn_normed)
                        if g == 2 and u == 3 and tail:
                            dve.wait_ge(x2_ready, b)
                            norm_stats(2, b - 1, x_tile(b - 1))
                        if g == 2 and u == 4 and tail:
                            normalise(2, b - 1, x_tile(b - 1), xf, xf_ready)
                    if g == 0 and stage:
                        split_lo(xnT_lo[:, :], xnT_hi[:, :], xT_hi, b + 1)
                    if g == 1 and tail:
                        add_bo(use("oproj"))
                    if g == 2 and tail:
                        split_lo(xfs_lo[:, :], xfs_hi[:, :], xfT_hi_done, b - 1)
                    if g == 3 and tail:
                        shift_logits(b - 1, use("logits"))

            nc.vector.memset(halfneg[:, :], -0.5).then_inc(half_set, 1)
            dve.wait_ge(x_first, 16)
            norm_stats(0, 0, x_tile(0))
            dve.wait_ge(attn_weights, 1)
            nc.vector.tensor_tensor(wa_lo[:, :, :], wa[:, :, :], wa_hi[:, :, :].bitcast(F32), ALU.subtract
                                    ).then_inc(attn_weights, 1)
            normalise(0, 0, x_tile(0), xn, xn_ready)
            split_lo(xnT_lo[:, :], xnT_hi[:, :], xT_hi, 0)
            for u in range(NU):
                maxima(0, 0, u)
            dve.wait_ge(weights_hi, 5)
            nc.vector.tensor_tensor(gw_lo[:, :], gw[:, :], gw_hi[:, :].bitcast(F32), ALU.subtract
                                    ).then_inc(weights_lo, 1)
            nc.vector.tensor_tensor(be_lo[:, :], be[:, :], be_hi[:, :].bitcast(F32), ALU.subtract
                                    ).then_inc(weights_lo, 1)
            nc.vector.tensor_tensor(w13_lo[:, :, :, :].rearrange("p a b c -> p (a b c)"),
                                    ptf[:, 0:5, :].rearrange("p a b -> p (a b)")[:, 0:2 * NP * P],
                                    w13_hi[:, :, :, :].rearrange("p a b c -> p (a b c)").bitcast(F32), ALU.subtract
                                    ).then_inc(weights_lo, 1)
            nc.vector.tensor_tensor(w2_lo[:, :, :].rearrange("p b c -> p (b c)"),
                                    ptf[:, 5:8, :].rearrange("p a b -> p (a b)")[:, 0:NP * C],
                                    w2_hi[:, :, :].rearrange("p b c -> p (b c)").bitcast(F32), ALU.subtract
                                    ).then_inc(weights_lo, 1)
            iteration(0, tail=False, stage=True)
            with dve.Fori(1, B - 1) as b:
                iteration(b, tail=True, stage=True)
            iteration(B - 1, tail=True, stage=False)
            for t in range(NT):
                normalise_o(B - 1, t, use_number(B, f"otr{t}"))
            split_lo(oT_lo[:, :], oT_hi[:, :], onT_hi, B - 1, col[:, 2:3])
            add_bo(use_number(B, "oproj"))
            dve.wait_ge(misc_evacuated, use_number(B, "oproj") + 1)
            norm_stats(1, B - 1, tile_in(att))
            normalise(1, B - 1, tile_in(att), attn_n, attn_normed)
            dve.wait_ge(x2_ready, B)
            norm_stats(2, B - 1, x_tile(B - 1))
            normalise(2, B - 1, x_tile(B - 1), xf, xf_ready)
            split_lo(xfs_lo[:, :], xfs_hi[:, :], xfT_hi_done, B - 1)
            shift_logits(B - 1, use_number(B, "logits"))

            steps = [0]

            def step(instruction):
                steps[0] += 1
                instruction.then_inc(router_step, 1)
                dve.wait_ge(router_step, steps[0])

            def tt(dst, a, b, op):
                step(nc.vector.tensor_tensor(dst, a, b, op))

            N = B * NT

            def per_tile(a, n):
                return a.unsqueeze(2).broadcast_to([P, N, n])

            dve.wait_ge(pv_done, B * G * NT)
            dve.wait_ge(gate_exp, B)
            ge = gexp[:, :, :, :].rearrange("p b t e -> p (b t) e")
            total, inv, m1, w1, m2, w2_ = (r[:, :] for r in rm)
            orig, s, sm, e1, o1, sm2, e2, o2, pick = rt[0:9]
            step(nc.vector.tensor_reduce(total, ge, AX.X, ALU.add))
            step(nc.vector.reciprocal(inv, total))
            tt(orig, ge, per_tile(inv, E), ALU.mult)
            tt(s, orig, row[:, C:C + E].unsqueeze(1).broadcast_to([P, N, E]), ALU.add)
            hi2 = rt[9][:, :, 0:2 * EG].rearrange("p t (g k) -> p t g k", k=2)
            lo2 = rt[10][:, :, 0:2 * EG].rearrange("p t (g k) -> p t g k", k=2)
            quad = s.rearrange("p t (g k a) -> p t g k a", k=2, a=2)
            for k in range(2):
                tt(hi2[:, :, :, k], quad[:, :, :, k, 0], quad[:, :, :, k, 1], ALU.max)
                tt(lo2[:, :, :, k], quad[:, :, :, k, 0], quad[:, :, :, k, 1], ALU.min)
            top, mn, ml, gs, rank, keep, pen = rs[0:7]
            tt(top, hi2[:, :, :, 0], hi2[:, :, :, 1], ALU.max)
            tt(mn, hi2[:, :, :, 0], hi2[:, :, :, 1], ALU.min)
            tt(ml, lo2[:, :, :, 0], lo2[:, :, :, 1], ALU.max)
            tt(mn, mn, ml, ALU.max)
            tt(gs, top, mn, ALU.add)
            other = gs.unsqueeze(2).broadcast_to([P, N, EG, EG])
            own = gs.unsqueeze(3).broadcast_to([P, N, EG, EG])
            gt = rt[11].rearrange("p t (g h) -> p t g h", h=EG)
            eq = rt[12].rearrange("p t (g h) -> p t g h", h=EG)
            tt(gt, other, own, ALU.is_gt)
            tt(eq, other, own, ALU.is_equal)
            tt(rt[12], rt[12], cst[:, TRI:TRI + EG * EG].unsqueeze(1).broadcast_to([P, N, EG * EG]), ALU.mult)
            tt(rt[11], rt[11], rt[12], ALU.add)
            step(nc.vector.tensor_reduce(rank, gt, AX.X, ALU.add))
            step(nc.vector.tensor_scalar(keep, rank, 2.0, None, ALU.is_lt))
            step(nc.vector.tensor_scalar(pen, keep, BIG, BIG, ALU.mult, ALU.subtract))
            s4 = s.rearrange("p t (g k) -> p t g k", k=E // EG)
            sm4 = sm.rearrange("p t (g k) -> p t g k", k=E // EG)
            tt(sm4, s4, keep.unsqueeze(3).broadcast_to([P, N, EG, E // EG]), ALU.mult)
            tt(sm4, sm4, pen.unsqueeze(3).broadcast_to([P, N, EG, E // EG]), ALU.add)
            rev = cst[:, REV:REV + E].unsqueeze(1).broadcast_to([P, N, E])

            def first_largest(src, largest, weight, marked, one_hot):
                step(nc.vector.tensor_reduce(largest, src, AX.X, ALU.max))
                tt(marked, src, per_tile(largest, E), ALU.is_equal)
                tt(marked, marked, rev, ALU.mult)
                step(nc.vector.tensor_reduce(weight, marked, AX.X, ALU.max))
                tt(one_hot, marked, per_tile(weight, E), ALU.is_equal)

            first_largest(sm, m1, w1, e1, o1)
            step(nc.vector.scalar_tensor_tensor(sm2, o1, -BIG, sm, ALU.mult, ALU.add))
            first_largest(sm2, m2, w2_, e2, o2)
            tt(pick, o1, o2, ALU.add)
            tt(comb_all[:, :, :], orig, pick, ALU.mult)

            def combine(b):
                if not (isinstance(b, int) and b == 0):
                    dve.wait_ge(cT_in_psum, b)
                c = comb_all[:, batch_of(b, NT), :]
                nc.vector.tensor_copy(comb[:, :, 0:E].bitcast(F32R), c).then_inc(comb_hi, 1)
                dve.wait_ge(comb_hi, b + 1)
                nc.vector.tensor_tensor(comb[:, :, E:2 * E].bitcast(F32R), c, comb[:, :, 0:E], ALU.subtract
                                        ).then_inc(combine_ready, 1)

            def hidden(b, p, par):
                q = b * NP + p
                dve.wait_ge(silu_done, q + 1)
                dve.wait_ge(h3_ready, q + 1)
                if not (isinstance(q, int) and q < 3):
                    dve.wait_ge(h_split, q - 2)
                if p == 0:
                    nc.vector.scalar_tensor_tensor(hbuf[0], ps_h3[par], b13c[:, 1, 0:1], silu[0], ALU.add, ALU.mult
                                                   ).then_inc(h_done, 1)
                    return
                nc.vector.scalar_tensor_tensor(gated[p % 3], ps_h3[par], b13c[:, 1, p:p + 1], silu[p % 3],
                                               ALU.add, ALU.mult).then_inc(gated_done, 1)
                dve.wait_ge(gated_done, b * (NP - 1) + p)
                nc.vector.tensor_tensor(hbuf[p % 3], ps_c[par][:, :], gated[p % 3], ALU.mult).then_inc(h_done, 1)

            def y_tiles(t):
                return ps_m[:, P * t:P * t + P]

            def expert_batch(b, parity, first, last_batch):
                for p in range(NP):
                    hidden(b, p, (parity + p) % 2)
                    if p == 5 and not first:
                        dve.wait_ge(yT_ready, b)
                        norm_stats(3, b - 1, y_tiles)
                    if p == 6 and not first:
                        normalise(3, b - 1, y_tiles, y_n, y_normed)
                    if p == 2 and not last_batch:
                        combine(b + 1)

            combine(0)
            expert_batch(0, 0, True, False)
            with dve.Fori(0, B // 2 - 1) as i:
                expert_batch(i * 2 + 1, 1, False, False)
                expert_batch(i * 2 + 2, 0, False, False)
            expert_batch(B - 1, 1, False, True)
            dve.wait_ge(yT_ready, B)
            norm_stats(3, B - 1, y_tiles)
            normalise(3, B - 1, y_tiles, y_n, y_normed)

        @block.gpsimd
        def _(pool):
            def carry_wait():
                pool.sem_inc(wait_carrier[1], 1)

            def inverse_deviation(i, count):
                pool.wait_ge(moments[i], count + 1)
                carry_wait()
                nc.gpsimd.tensor_scalar(ve[:, i, :], mv[:, i, :, 1], EPS, 1.0, ALU.add, ALU.mult
                                        ).then_inc(eps_added[i], 1)
                pool.wait_ge(eps_added[i], count + 1)
                nc.gpsimd.tensor_tensor(rstd[:, i, :], ve[:, i, :], halfneg[:, :], ALU.pow).then_inc(rstds[i], 1)
                pool.wait_ge(rstds[i], count + 1)

            def qk_lower(s, number, which):
                pool.wait_ge(misc_evacuated, number + 1)
                nc.gpsimd.tensor_tensor(qk_lo[:, which, :], qk_f[:, which, :], qk_hi[:, which, :].bitcast(F32),
                                        ALU.subtract).then_inc(qk_split, 1)
                pool.wait_ge(qk_split, s * 2 + (which + 1))

            def place_v(s, g, number):
                pool.wait_ge(misc_evacuated, number + 1)
                if not (isinstance(s, int) and s == 0):
                    pool.wait_ge(pv_done, (s * G + g - G) * NT + NT)
                carry_wait()
                nc.gpsimd.tensor_scalar(vaug[:, :, HG * g:HG * (g + 1), 0:D],
                                        vraw[:, :, D * HG * g:D * HG * (g + 1)].rearrange("p t (h d) -> p t h d", d=D),
                                        1.0, 1.0, ALU.mult, ALU.mult).then_inc(v_placed, 1)
                pool.wait_ge(v_placed, s * G + (g + 1))

            def mask_exponentials(b, g, upper):
                n = b * G + g
                pool.wait_ge(exps_done, n * NV + (8 if upper else NV))
                carry_wait()
                k = slice(2, 4) if upper else slice(0, 2)
                d = T - P
                for part in range(2):
                    v = pt[CHUNK * part:CHUNK * (part + 1), k, :, d + CHUNK * part:d + CHUNK * (part + 1)]
                    nc.gpsimd.affine_select(out=v, in_=v, compare_op=ALU.is_ge, fill=0.0, base=0,
                                            pattern=[[0, 2], [0, HG], [1, CHUNK]], channel_multiplier=-1
                                            ).then_inc(masks_done, 1)
                    pool.wait_ge(masks_done, n * 6 + ((0 if upper else 3) + part + 1))
                    carry_wait()
                nc.gpsimd.memset(pt[0:CHUNK, k, :, d + CHUNK:T], 0.0).then_inc(masks_done, 1)
                pool.wait_ge(masks_done, n * 6 + (3 if upper else 6))

            def split_shift(b, g, number):
                n = b * G + g
                pool.wait_ge(maxes_done, n * NU + NU)
                if number is not None:
                    pool.wait_ge(misc_ready, number + 1)
                carry_wait()
                src = negmax[:, g % 2, :, :]
                nc.gpsimd.tensor_scalar(shift[:, :, 0:HG].bitcast(F32R), src, 1.0, 1.0, ALU.mult, ALU.mult
                                        ).then_inc(shift_hi, 1)
                pool.wait_ge(shift_hi, n + 1)
                nc.gpsimd.tensor_tensor(shift[:, :, HG:2 * HG].bitcast(F32R), src, shift[:, :, 0:HG], ALU.subtract
                                        ).then_inc(shift_split, 1)
                pool.wait_ge(shift_split, n + 1)

            def add_x(b):
                pool.wait_ge(attn_normed, b + 1)
                v = xall[:, batch_of(b, NT), :]
                nc.gpsimd.tensor_tensor(v, v, attn_n[:, :, :], ALU.add).then_inc(x2_ready, 1)
                pool.wait_ge(x2_ready, b + 1)

            def iteration(b, tail, stage, v_number):
                def use(name):
                    return use_number(b, name)

                for g in range(G):
                    follows = stage or g < G - 1
                    nb, ng = (b, g + 1) if g < G - 1 else (b + 1, 0)
                    if g == 0 and stage:
                        inverse_deviation(0, b + 1)
                    if g == 1:
                        place_v(b, G - 1, v_number)
                        if stage:
                            qk_lower(b + 1, use("q"), 0)
                            qk_lower(b + 1, use("k"), 1)
                    if g == 2 and tail:
                        inverse_deviation(1, b - 1)
                        add_x(b - 1)
                        inverse_deviation(2, b - 1)
                    mask_exponentials(b, g, True)
                    if g == 3 and stage:
                        for gg in range(G - 1):
                            place_v(b + 1, gg, use("v"))
                    mask_exponentials(b, g, False)
                    if follows:
                        split_shift(nb, ng, use(f"shift{g}"))

            nc.gpsimd.memset(km[:, :, :, :].rearrange("p g j t -> p (g j t)").bitcast(F32), 0.0).then_inc(km_zeroed, 1)
            pool.wait_ge(half_set, 1)
            inverse_deviation(0, 0)
            nc.gpsimd.memset(vaug[:, :, :, D + 1:VW], 0.0).then_inc(ones_placed, 1)
            nc.gpsimd.memset(vaug[:, :, :, D:D + 1], 1.0).then_inc(ones_placed, 1)
            pool.wait_ge(km_zeroed, 1)
            pool.wait_ge(ones_placed, 2)
            pool.wait_ge(const_in, 96)
            nc.gpsimd.tensor_scalar(km[ROWS:ROWS_SHIFTED, :, :, :],
                                    cst[ROWS:ROWS_SHIFTED, ONES:ONES + HG].unsqueeze(1).unsqueeze(3).broadcast_to(
                                        [ROWS_SHIFTED - ROWS, G, HG, T]), 1.0, 1.0, ALU.mult, ALU.mult
                                    ).then_inc(operands_cleared, 1)
            pool.wait_ge(operands_cleared, 1)
            qk_lower(0, use_number(None, "q"), 0)
            qk_lower(0, use_number(None, "k"), 1)
            for g in range(G - 1):
                place_v(0, g, use_number(None, "v"))
            split_shift(0, 0, None)
            iteration(0, False, True, use_number(None, "v"))
            iteration(1, True, True, use_number(0, "v"))
            with pool.Fori(2, B - 1) as b:
                iteration(b, True, True, use_number(b, "v") - len(USES))
            iteration(B - 1, True, False, use_number(B - 2, "v"))
            inverse_deviation(1, B - 1)
            add_x(B - 1)
            inverse_deviation(2, B - 1)

            def hidden_lower(b, p):
                q = b * NP + p
                pool.wait_ge(h_hi_done, q + 1)
                nc.gpsimd.tensor_tensor(h_lo[p % 3], hbuf[p % 3], h_hi[p % 3].bitcast(F32), ALU.subtract
                                        ).then_inc(h_split, 1)

            def finish(b):
                pool.wait_ge(y_normed, b + 1)
                pool.wait_ge(stored, b * 16 + 1)
                nc.gpsimd.tensor_tensor(out_sb, y_n, xall[:, batch_of(b, NT), :], ALU.add).then_inc(out_ready, 1)

            def expert_batch(b, first):
                for p in range(NP):
                    hidden_lower(b, p)
                    if p == 5 and not first:
                        inverse_deviation(3, b - 1)
                    if p == 7 and not first:
                        finish(b - 1)

            expert_batch(0, True)
            with pool.Fori(1, B) as b:
                expert_batch(b, False)
            inverse_deviation(3, B - 1)
            finish(B - 1)


_OUT = ((B, T, C), "float32")


def kernel(**inputs):
    import concourse.bacc as bacc
    from concourse.bass_utils import run_bass_kernel_spmd

    a = {k: np.asarray(v) for k, v in inputs.items()}
    at, ff = (lambda n: a["L0_attn_" + n]), (lambda n: a["L0_ffn_" + n])
    order = kq_channel_order()

    def pairs_in(w):
        return w.reshape(E // 2, 2, C, INTER).transpose(2, 0, 1, 3).reshape(C, E // 2, P)

    def up_weights(shared, experts):
        return np.concatenate([shared[:, None, :], pairs_in(experts)], axis=1)

    w_attn = np.stack([at("Wq").T[:, order], at("Wk").T[:, order], at("Wv").T, at("Wo").T], axis=1)
    cols = np.stack([at("bq")[order], at("bk")[order], at("bv"), ff("bs2"),
                     np.broadcast_to(at("attn_scale"), (C,))], axis=1)
    w13 = np.stack([up_weights(ff("ws1"), ff("We1")), up_weights(ff("ws3"), ff("We3"))], axis=1).reshape(C, -1)
    w2 = np.concatenate([ff("ws2")[None], ff("We2").reshape(E // 2, P, C)], axis=0).transpose(1, 0, 2).reshape(P, -1)
    b13 = np.stack([np.concatenate([ff("bs1")[None], ff("be1").reshape(E // 2, P)], axis=0).T,
                    np.concatenate([ff("bs3")[None], ff("be3").reshape(E // 2, P)], axis=0).T], axis=1)
    rows = np.broadcast_to(np.concatenate([at("bo"), ff("gate_b")])[None, :], (P, C + E))
    arrays = {
        "x": a["L0_attn_x"].reshape(B * T, C), "w_attn": w_attn, "cols": cols, "w13": w13, "w2": w2, "b13": b13,
        "gate_w": ff("gate_w").T, "rows": rows, "be2": np.concatenate([ff("be2"), ff("be2")], axis=0),
        "const": shape_constants(),
    }
    arrays = {k: np.ascontiguousarray(v) for k, v in arrays.items()}
    nc = bacc.Bacc("TRN2", target_bir_lowering=False, num_devices=1)
    args = [nc.dram_tensor(f"in_{k}", v.shape, mybir.dt.from_np(v.dtype), kind="ExternalInput").ap()
            for k, v in arrays.items()]
    args.append(nc.dram_tensor("out_0", (B * T, C), F32, kind="ExternalOutput").ap())
    block_kernel(nc, *args)
    r = run_bass_kernel_spmd(nc, [{f"in_{k}": v for k, v in arrays.items()}], core_ids=[0])
    return r.results[0]["out_0"].reshape(_OUT[0])
```

```python
from contextlib import ExitStack

import numpy as np

import concourse.bass as bass
from concourse import mybir

F32 = mybir.dt.float32
F32R = mybir.dt.float32r
BF16 = mybir.dt.bfloat16
ALU = mybir.AluOpType
ACT = mybir.ActivationFunctionType
AX = mybir.AxisListType

P = 128
B, T, C = 8, 512, 128
NT = T // P
CHUNK = 64
H, D = 16, 8
G, HG = 4, 4
E, INTER = 16, 64
NP = 1 + E // 2
EG = 4
VW = 32
EPS = 1e-5
MASKED = -3.0e38
BIG = 1.0e30

ROWS = 3 * HG * D
ROWS_SHIFTED = ROWS + 2 * HG

MAX_UNITS = [(0, (0, 1)), (0, (2, 3)), (1, (0, 1)), (1, (2, 3)), (2, (0, 1, 2, 3)), (3, (0, 1, 2, 3))]
NU = len(MAX_UNITS)
EXP_UNITS = [(3, (0,)), (3, (1,)), (3, (2,)), (3, (3,)), (2, (0,)), (2, (1,)), (2, (2,)), (2, (3,)),
             (1, (0, 1)), (1, (2, 3)), (0, (0, 1, 2, 3))]
NV = len(EXP_UNITS)
SHIFT_PLACE = 8


def exp_bank(v):
    return v % 2 if v < SHIFT_PLACE else (v + 1) % 2



USES = ["xT", "otr0", "otr1", "otr2", "q", "otr3", "k", "onT", "oproj", "v", "xfT", "logits"]
TAIL = ("otr0", "otr1", "otr2", "otr3", "onT", "oproj", "xfT", "logits")
STAGE = ("xT", "q", "k", "v")
FIRST_USES = [u for u in USES if u not in TAIL]
LAST_USES = [u for u in USES if u not in STAGE]

GROUP_DMAS = 2 + 2 * HG


def use_number(b, name):
    if b is None:
        return STAGE.index(name)
    after_prologue = len(STAGE)
    after_first = after_prologue + len(FIRST_USES)
    if isinstance(b, int) and b == 0:
        return after_prologue + FIRST_USES.index(name)
    if isinstance(b, int) and b == B - 1:
        return after_first + len(USES) * (B - 2) + LAST_USES.index(name)
    if isinstance(b, int) and b == B:
        return after_first + len(USES) * (B - 2) + len(LAST_USES) + TAIL.index(name)
    return b * len(USES) + (after_first - len(USES) + USES.index(name))


IDENT, MASK, SEL, TRI, REV = 0, P, 2 * P, 2 * P + (NP - 1) * P, 2 * P + (NP - 1) * P + EG * EG
ONES = REV + E
NCONST = ONES + HG


def follower(b, g, stage):
    if g < G - 1:
        return b, g + 1
    return (b + 1, 0) if stage else None


def units_ahead(b, g, stage, m):
    steps, u = (1, m + NU // 2) if m < NU // 2 else (2, m - NU // 2)
    if g + steps < G:
        return b, g + steps, u
    return (b + 1, g + steps - G, u) if stage else None


def shape_constants():
    c = np.zeros((P, NCONST), np.float32)
    c[:, IDENT:IDENT + P] = np.eye(P)
    q, k = np.arange(P)[:, None], np.arange(P)[None, :]
    allowed = (k // CHUNK > q // CHUNK) | ((k // CHUNK == q // CHUNK) & (k <= q))
    c[:, MASK:MASK + P] = np.where(allowed, 0.0, MASKED)
    for p in range(NP - 1):
        for col in range(P):
            for half in range(2):
                c[half * E + 2 * p + col // INTER, SEL + p * P + col] = 1.0
    c[:, TRI:TRI + EG * EG] = (np.arange(EG)[None, :] < np.arange(EG)[:, None]).astype(np.float32).reshape(1, -1)
    c[:, REV:REV + E] = E - np.arange(E)
    for j in range(HG):
        c[ROWS + j, ONES + j] = c[ROWS + HG + j, ONES + j] = 1.0
    return c


def block_kernel(nc, x, w_attn, cols, w13, w2, b13, gate_w, rows, be2, const, out):
    ctx = ExitStack()
    with ctx:
        def sb(name, shape, dt=F32):
            return ctx.enter_context(nc.sbuf_tensor(name, shape, dt))

        def sem(name):
            return ctx.enter_context(nc.semaphore(name))

        xall = sb("xall", [P, B * NT, C])
        cst = sb("cst", [P, NCONST])
        ident_bf = sb("ident_bf", [P, P], BF16)
        mask_bf = sb("mask_bf", [P, P], BF16)
        sel = sb("sel", [2 * E, (NP - 1) * P], F32R)
        wa = sb("wa", [P, 4, C])
        wa_hi = sb("wa_hi", [P, 4, C], F32R)
        wa_lo = sb("wa_lo", [P, 4, C], F32R)
        gw = sb("gw", [P, E])
        gw_hi = sb("gw_hi", [P, E], F32R)
        gw_lo = sb("gw_lo", [P, E], F32R)
        col = sb("col", [P, 6])
        b13c = sb("b13c", [P, 2, NP])
        row = sb("row", [P, C + E])
        be = sb("be", [2 * E, C])
        be_hi = sb("be_hi", [2 * E, C], F32R)
        be_lo = sb("be_lo", [2 * E, C], F32R)
        w13_hi = sb("w13_hi", [P, 2, NP, P], F32R)
        w13_lo = sb("w13_lo", [P, 2, NP, P], F32R)
        w2_hi = sb("w2_hi", [P, NP, C], F32R)
        w2_lo = sb("w2_lo", [P, NP, C], F32R)
        halfneg = sb("halfneg", [P, NT])
        pt = sb("pt", [P, NT, HG, T])
        km = sb("km", [P, G, HG, T], F32R)
        qd = sb("qd", [P, G, T], F32R)
        vaug = sb("vaug", [P, NT, H, VW])
        xn = sb("xn", [P, NT, C])
        xnT_hi = sb("xnT_hi", [P, T], F32R)
        xnT_lo = sb("xnT_lo", [P, T], F32R)
        qk_f = sb("qk_f", [P, 2, T])
        qk_split = sb("qk_split", [P, 2, 2, T], F32R)
        vraw = sb("vraw", [P, NT, C])
        negmax = sb("negmax", [P, 2, NT, HG])
        shift = sb("shift", [P, NT, 2 * HG])
        o_raw = sb("o_raw", [P, G, T])
        rsum = sb("rsum", [P, NT, H])
        oT_hi = sb("oT_hi", [P, T], F32R)
        oT_lo = sb("oT_lo", [P, T], F32R)
        bst = sb("bst", [P, 4, NT, 6])
        mv = sb("mv", [P, 4, NT, 2])
        ve = sb("ve", [P, 4, NT])
        rstd = sb("rstd", [P, 4, NT])
        xfT_hi = [sb(f"xfT_hi{i}", [P, T], F32R) for i in range(2)]
        xfT_lo = [sb(f"xfT_lo{i}", [P, T], F32R) for i in range(2)]
        xfT_kept = nc.dram_tensor("xfT_kept", [2, P, B * T], F32, kind="Internal").ap()
        xfs_hi = sb("xfs_hi", [P, T], F32R)
        xfs_lo = sb("xfs_lo", [P, T], F32R)
        lmax = sb("lmax", [P, NT])
        after = sb("after", [P, 5, T])
        on, att, attn_n, xf = (after[:, i, :].rearrange("p (t c) -> p t c", t=NT) for i in range(4))
        gexp = after[:, 4, :].rearrange("p (b t e) -> p b t e", b=B, t=NT)
        w13_raw = after[:, :, :].rearrange("p a b -> p (a b)")[:, 0:2 * NP * P]
        w2_raw = o_raw[:, :, :].rearrange("p a b -> p (a b)")[:, 0:NP * C]
        ptf = pt[:, :, :, :].rearrange("p k h t -> p (k h) t")
        silu = [ptf[:, i, :] for i in range(3)]
        gated = [ptf[:, 3 + i, :] for i in range(3)]
        hbuf = [ptf[:, 6 + i, :] for i in range(3)]
        y_sb = ptf[:, 9, :]
        y_n = ptf[:, 10, :].rearrange("p (t c) -> p t c", t=NT)
        out_sb = ptf[:, 11, :].rearrange("p (t c) -> p t c", t=NT)
        kmf = km[:, :, :, :].rearrange("p g j t -> p (g j) t")
        h_hi = [kmf[:, i, :] for i in range(3)]
        h_lo = [kmf[:, 3 + i, :] for i in range(3)]
        cT = [kmf[0:2 * E, 6 + i, :] for i in range(2)]
        comb = sb("comb", [P, NT, 2 * E])
        comb_all = sb("comb_all", [P, B * NT, E])
        rt = [ptf[:, i, :].rearrange("p (t e) -> p t e", e=E) for i in range(14)]
        rs = [ptf[:, 14 + i // 4, 128 * (i % 4):128 * (i % 4) + 128].rearrange("p (t g) -> p t g", g=EG)
              for i in range(8)]
        rm = [sb(f"rm{i}", [P, B * NT]) for i in range(6)]

        ps_a = [ctx.enter_context(nc.psum_tensor(f"ps_a{i}", [P, 1024], F32)) for i in range(2)]
        ps_b = [ctx.enter_context(nc.psum_tensor(f"ps_b{i}", [P, 512], F32)) for i in range(2)]
        ps_o = ctx.enter_context(nc.psum_tensor("ps_o", [P, 512], F32))
        ps_m = ctx.enter_context(nc.psum_tensor("ps_m", [P, 512], F32))
        ps_h1 = [ps_a[0][:, 512 * i:512 * i + 512] for i in range(2)]
        ps_h3 = [ps_a[1][:, 512 * i:512 * i + 512] for i in range(2)]
        ps_c = ps_b
        ps_y = ps_o

        x_first, x_rest = sem("x_first"), sem("x_rest")
        const_in, wattn_in, w_in = sem("const_in"), sem("wattn_in"), sem("w_in")
        attn_weights, small_hi = sem("attn_weights"), sem("small_hi")
        weights_hi, weights_lo = sem("weights_hi"), sem("weights_lo")
        operands_cleared, ones_placed, half_set = sem("operands_cleared"), sem("ones_placed"), sem("half_set")
        scores_ready, maxes_done = sem("scores_ready"), sem("maxes_done")
        shift_hi, shift_split = sem("shift_hi"), sem("shift_split")
        shift_in_psum, shift_placed = sem("shift_in_psum"), sem("shift_placed")
        st_ready, exps_done, masks_done = sem("st_ready"), sem("exps_done"), sem("masks_done")
        pv_done, o_evacuated = sem("pv_done"), sem("o_evacuated")
        misc_ready, misc_evacuated = sem("misc_ready"), sem("misc_evacuated")
        xT_hi, onT_hi, xfT_hi_done = sem("xT_hi"), sem("onT_hi"), sem("xfT_hi_done")
        stats = [sem(f"stats{i}") for i in range(4)]
        moments = [sem(f"moments{i}") for i in range(4)]
        eps_added = [sem(f"eps_added{i}") for i in range(4)]
        rstds = [sem(f"rstds{i}") for i in range(4)]
        xn_ready, attn_normed, x2_ready, xf_ready = sem("xn_ready"), sem("attn_normed"), sem("x2_ready"), sem("xf_ready")
        sums_inverted, logit_max, gate_exp = sem("sums_inverted"), sem("logit_max"), sem("gate_exp")
        qk_lower_done, v_placed = sem("qk_lower_done"), sem("v_placed")
        kq_in = [sem(f"kq_in{g}") for g in range(G)]
        h1_ready, h3_ready, silu_done, gated_done, h_done = (
            sem("h1_ready"), sem("h3_ready"), sem("silu_done"), sem("gated_done"), sem("h_done"))
        h_hi_done, h_split, down_done = sem("h_hi_done"), sem("h_split"), sem("down_done")
        y_evacuated, yT_ready, y_normed = sem("y_evacuated"), sem("yT_ready"), sem("y_normed")
        router_step, cT_in_psum, cT_ready = sem("router_step"), sem("cT_in_psum"), sem("cT_ready")
        xf_saved, combine_ready, comb_hi, km_zeroed = sem("xf_saved"), sem("combine_ready"), sem("comb_hi"), sem("km_zeroed")
        xf_in = [sem("xf_in0"), sem("xf_in1")]
        wait_carrier = [sem("wait_carrier_dve"), sem("wait_carrier_pool")]
        out_ready, stored = sem("out_ready"), sem("stored")

        block = ctx.enter_context(nc.Block())

        def tile_of(b, t):
            return bass.ds(b * NT + t, 1) if not isinstance(b, int) else slice(b * NT + t, b * NT + t + 1)

        def batch_of(b, width):
            return bass.ds(b * width, width) if not isinstance(b, int) else slice(b * width, (b + 1) * width)

        def third(part):
            if part == 0:
                hi, lo = (w[:, :, :].rearrange("p b c -> p (b c)") for w in (w2_hi, w2_lo))
                return hi, lo, w2_raw
            hi, lo = (w[:, part - 1, :, :].rearrange("p b c -> p (b c)") for w in (w13_hi, w13_lo))
            return hi, lo, w13_raw[:, NP * P * (part - 1):NP * P * part]

        x_dram = x.rearrange("(n p) c -> p n c", p=P)
        out_dram = out.rearrange("(n p) c -> p n c", p=P)

        @block.sync
        def _(sp):
            sp.sem_inc(xf_saved, 1)
            sp.sem_inc(stored, 1)
            sp.dma_start(xall[:, 0:NT, :], x_dram[:, 0:NT, :]).then_inc(x_first, 16)
            sp.dma_start(wa[:, :, :], w_attn).then_inc(wattn_in, 16)
            sp.dma_start(cst[:, :], const).then_inc(const_in, 16)
            sp.dma_start(col[:, 0:5], cols).then_inc(const_in, 16)
            sp.dma_start(xall[:, NT:, :], x_dram[:, NT:, :]).then_inc(x_rest, 16)
            sp.dma_start(row[:, :], rows).then_inc(const_in, 16)
            sp.dma_start(gw[:, :], gate_w).then_inc(const_in, 16)
            sp.dma_start(be[:, :], be2).then_inc(const_in, 16)
            sp.dma_start(b13c[:, :, :], b13).then_inc(const_in, 16)
            sp.dma_start(w2_raw, w2).then_inc(w_in, 16)
            sp.dma_start(w13_raw, w13).then_inc(w_in, 16)

            def place_group(s, g):
                if isinstance(s, int) and s == 0:
                    sp.wait_ge(qk_lower_done, 2)
                    sp.wait_ge(operands_cleared, 1)
                else:
                    if g == 0:
                        sp.wait_ge(qk_lower_done, s * 2 + 2)
                    sp.wait_ge(st_ready, s * (G * NV) + (NV * (g + 1) - G * NV))
                rows_of = HG * D
                sp.dma_start(qd[0:2 * rows_of, g, :].bitcast(F32),
                             qk_split[rows_of * g:rows_of * (g + 1), 0, :, :].bitcast(F32)).then_inc(kq_in[g], 16)
                sp.dma_start(qd[2 * rows_of:ROWS, g, :].bitcast(F32),
                             qk_split[rows_of * g:rows_of * (g + 1), 0, 0, :].bitcast(F32)).then_inc(kq_in[g], 16)
                for j in range(HG):
                    own = slice(rows_of * g + D * j, rows_of * g + D * (j + 1))
                    sp.dma_start(km[2 * D * j:2 * D * (j + 1), g, j, :].bitcast(F32),
                                 qk_split[own, 1, 0, :].bitcast(F32).unsqueeze(1).broadcast_to([D, 2, T])
                                 ).then_inc(kq_in[g], 16)
                    sp.dma_start(km[2 * rows_of + D * j:2 * rows_of + D * (j + 1), g, j, :].bitcast(F32),
                                 qk_split[own, 1, 1, :].bitcast(F32)).then_inc(kq_in[g], 16)

            for g in range(G):
                place_group(0, g)

            def save_xf(b, number):
                sp.wait_ge(misc_evacuated, number + 1)
                sp.dma_start(xfT_kept[0, :, batch_of(b, T)], xfs_hi[:, :].bitcast(F32)).then_inc(xf_saved, 16)
                sp.dma_start(xfT_kept[1, :, batch_of(b, T)], xfs_lo[:, :].bitcast(F32)).then_inc(xf_saved, 16)

            def load_xf(b, parity):
                if not (isinstance(b, int) and b < 2):
                    sp.wait_ge(h3_ready, (b - 1) * NP)
                sp.dma_start(xfT_hi[parity][:, :].bitcast(F32), xfT_kept[0, :, batch_of(b, T)]).then_inc(xf_in[parity], 16)
                sp.dma_start(xfT_lo[parity][:, :].bitcast(F32), xfT_kept[1, :, batch_of(b, T)]).then_inc(xf_in[parity], 16)

            def store_out(b):
                sp.wait_ge(out_ready, b + 1)
                sp.dma_start(out_dram[:, batch_of(b, NT), :], out_sb).then_inc(stored, 16)

            for g in range(G):
                place_group(1, g)
            with sp.Fori(1, B - 1) as b:
                for g in range(G):
                    place_group(b + 1, g)
                save_xf(b - 1, use_number(b, "xfT"))
            save_xf(B - 2, use_number(B - 1, "xfT"))
            save_xf(B - 1, use_number(B, "xfT"))
            sp.wait_ge(xf_saved, 32 * B + 1)
            load_xf(0, 0)
            load_xf(1, 1)
            load_xf(2, 0)
            with sp.Fori(0, B // 2 - 2) as i:
                store_out(i * 2)
                load_xf(i * 2 + 3, 1)
                store_out(i * 2 + 1)
                load_xf(i * 2 + 4, 0)
            store_out(B - 4)
            load_xf(B - 1, 1)
            for b in range(B - 3, B):
                store_out(b)
            sp.wait_ge(stored, 16 * B + 1)

        @block.tensor
        def _(pe):
            ident = cst[:, IDENT:IDENT + P]

            def claim_misc(number):
                if not (isinstance(number, int) and number == 0):
                    pe.wait_ge(misc_evacuated, number)

            def three_pass(dst, lhs_hi, lhs_lo, rhs_hi, rhs_lo, start=True, stop=True):
                nc.tensor.matmul(dst, lhs_hi, rhs_hi, start=start, stop=False)
                nc.tensor.matmul(dst, lhs_hi, rhs_lo, start=False, stop=False)
                return nc.tensor.matmul(dst, lhs_lo, rhs_hi, start=False, stop=stop)

            def transpose_tiles(number, src):
                claim_misc(number)
                for t in range(NT):
                    last = nc.tensor.transpose(ps_m[:, P * t:P * t + P], src[:, t, :], ident)
                last.then_inc(misc_ready, 1)

            def project_T(number, which):
                claim_misc(number)
                three_pass(ps_m[:, :], wa_hi[:, which, :], wa_lo[:, which, :], xnT_hi[:, :], xnT_lo[:, :]
                           ).then_inc(misc_ready, 1)

            def project_tokens(number, which, src_hi, src_lo):
                claim_misc(number)
                for t in range(NT):
                    s = slice(P * t, P * t + P)
                    last = three_pass(ps_m[:, s], src_hi[:, s], src_lo[:, s], wa_hi[:, which, :], wa_lo[:, which, :])
                last.then_inc(misc_ready, 1)

            def scores(b, g, u):
                t, heads = MAX_UNITS[u]
                n6 = b * (G * NU) + (g * NU + u)
                if not (isinstance(b, int) and b == 0 and g == 0 and u < 2):
                    pe.wait_ge(maxes_done, n6 - 1)
                if u == 0:
                    pe.wait_ge(kq_in[g], b * (16 * GROUP_DMAS) + 16 * GROUP_DMAS)
                width = T - P * t
                pitch = 512 if width > 256 else width
                a = ps_a[u % 2]
                for i, j in enumerate(heads):
                    o = i * pitch
                    nc.tensor.matmul(a[:, o:o + width], qd[0:ROWS, g, P * t:P * t + P], km[0:ROWS, g, j, P * t:T],
                                     start=True, stop=False)
                    last = nc.tensor.matmul(a[:, o:o + P], ident_bf[:, :], mask_bf[:, :], start=False, stop=True)
                last.then_inc(scores_ready, 1)

            def shift_rows(b, g):
                n = b * G + g
                pe.wait_ge(shift_split, n + 1)
                if not (isinstance(n, int) and n == 0):
                    pe.wait_ge(exps_done, n * NV + (SHIFT_PLACE - 1 - NV))
                for t in range(NT):
                    last = nc.tensor.transpose(ps_b[0][0:2 * HG, P * t:P * t + P], shift[:, t, :], ident)
                last.then_inc(shift_in_psum, 1)

            def scores_T(b, g, v):
                k, heads = EXP_UNITS[v]
                n = b * G + g
                if v == 0:
                    pe.wait_ge(shift_placed, n + 1)
                if v == SHIFT_PLACE + 1 and not (isinstance(n, int) and n == B * G - 1):
                    pe.wait_ge(shift_placed, n + 2)
                elif not (isinstance(n, int) and n == 0 and v < 2):
                    pe.wait_ge(exps_done, n * NV + (v if v == SHIFT_PLACE else v - 1))
                width = P * (k + 1)
                bank = ps_b[exp_bank(v)]
                for i, j in enumerate(heads):
                    last = nc.tensor.matmul(bank[:, i * width:i * width + width],
                                            km[0:ROWS_SHIFTED, g, j, P * k:P * k + P],
                                            qd[0:ROWS_SHIFTED, g, 0:width], start=True, stop=True)
                last.then_inc(st_ready, 1)

            def values(b, g, k):
                n = b * G + g
                if k == NT - 1:
                    pe.wait_ge(v_placed, n + 1)
                    if not (isinstance(n, int) and n == 0):
                        pe.wait_ge(o_evacuated, n)
                pe.wait_ge(masks_done, n * 6 + (3 if k >= 2 else 6))
                width = P * (k + 1)
                for j in range(HG):
                    last = nc.tensor.matmul(ps_o[32 * j:32 * j + VW, 0:width], vaug[:, k, HG * g + j, :],
                                            pt[:, k, j, T - width:T], start=k == NT - 1, stop=k == 0)
                last.then_inc(pv_done, 1)

            def o_transposes(b, t, number):
                if t == 0:
                    pe.wait_ge(o_evacuated, b * G + G)
                claim_misc(number)
                for g in range(G):
                    last = nc.tensor.transpose(ps_m[:, P * g:P * g + P], o_raw[:, g, P * t:P * t + P], ident)
                last.then_inc(misc_ready, 1)

            def logits(b, number):
                claim_misc(number)
                for t in range(NT):
                    hi, lo = xfs_hi[:, P * t:P * t + P], xfs_lo[:, P * t:P * t + P]
                    last = three_pass(ps_m[:, E * t:E * t + E], hi, lo, gw_hi[:, :], gw_lo[:, :])
                last.then_inc(misc_ready, 1)

            def iteration(b, tail, stage):
                def use(name):
                    return use_number(b, name)

                for g in range(G):
                    ahead = [units_ahead(b, g, stage, m) for m in range(NU)]
                    before = (b, g - 1) if g else (b - 1, G - 1)
                    has_before = tail or g > 0

                    def scores_ahead(m):
                        if ahead[m]:
                            scores(*ahead[m])

                    scores_ahead(0)
                    if has_before:
                        values(*before, 2)
                    scores_T(b, g, 0)
                    if g == 0 and stage:
                        pe.wait_ge(xn_ready, b + 2)
                        transpose_tiles(use("xT"), xn)
                    if g == 1 and stage:
                        project_T(use("q"), 0)
                    if g == 2 and tail:
                        project_tokens(use("oproj"), 3, oT_hi, oT_lo)
                    scores_T(b, g, 1)
                    scores_ahead(1)
                    scores_T(b, g, 2)
                    if has_before:
                        values(*before, 1)
                    scores_T(b, g, 3)
                    scores_ahead(2)
                    if has_before:
                        values(*before, 0)
                    if g == 1 and tail:
                        o_transposes(b - 1, 3, use("otr3"))
                    scores_T(b, g, 4)
                    scores_T(b, g, 5)
                    scores_ahead(3)
                    if g == 0 and tail:
                        o_transposes(b - 1, 0, use("otr0"))
                    if g == 1 and stage:
                        project_T(use("k"), 1)
                    scores_T(b, g, 6)
                    scores_T(b, g, 7)
                    scores_ahead(4)
                    if g == 0 and tail:
                        o_transposes(b - 1, 1, use("otr1"))
                    if g == 1 and tail:
                        transpose_tiles(use("onT"), on)
                    if g == 2 and stage:
                        project_tokens(use("v"), 2, xnT_hi, xnT_lo)
                    if g == 3 and tail:
                        pe.wait_ge(xf_ready, b)
                        transpose_tiles(use("xfT"), xf)
                    if follower(b, g, stage):
                        shift_rows(*follower(b, g, stage))
                    scores_T(b, g, 8)
                    scores_T(b, g, 9)
                    scores_ahead(5)
                    if g == 0 and tail:
                        o_transposes(b - 1, 2, use("otr2"))
                    scores_T(b, g, 10)
                    values(b, g, 3)
                    if g == 3 and tail:
                        logits(b - 1, use("logits"))

            pe.wait_ge(const_in, 96)
            pe.wait_ge(xn_ready, 1)
            transpose_tiles(use_number(None, "xT"), xn)
            pe.wait_ge(attn_weights, 2)
            project_T(use_number(None, "q"), 0)
            project_T(use_number(None, "k"), 1)
            project_tokens(use_number(None, "v"), 2, xnT_hi, xnT_lo)
            pe.wait_ge(small_hi, 3)
            for u in range(NU):
                scores(0, 0, u)
            for u in range(NU // 2):
                scores(0, 1, u)
            shift_rows(0, 0)
            iteration(0, tail=False, stage=True)
            with pe.Fori(1, B - 1) as b:
                iteration(b, tail=True, stage=True)
            iteration(B - 1, tail=True, stage=False)
            values(B - 1, G - 1, 2)
            values(B - 1, G - 1, 1)
            values(B - 1, G - 1, 0)
            for t in range(NT):
                o_transposes(B - 1, t, use_number(B, f"otr{t}"))
            transpose_tiles(use_number(B, "onT"), on)
            project_tokens(use_number(B, "oproj"), 3, oT_hi, oT_lo)
            pe.wait_ge(xf_ready, B)
            transpose_tiles(use_number(B, "xfT"), xf)
            logits(B - 1, use_number(B, "logits"))

            def unit(b, p, par, down_prev):
                q = b * NP + p
                odd = (par + p) % 2
                if p == 0:
                    pe.wait_ge(xf_in[odd], 32 * (b // 2) + 32 if isinstance(b, int) else (b - odd) * 16 + 32)
                xs_hi, xs_lo = xfT_hi[odd][:, :], xfT_lo[odd][:, :]
                early = isinstance(q, int) and q < 2
                if not early:
                    pe.wait_ge(silu_done, q - 1)
                three_pass(ps_h1[par], w13_hi[:, 0, p, :], w13_lo[:, 0, p, :], xs_hi, xs_lo
                           ).then_inc(h1_ready, 1)
                if not early:
                    pe.wait_ge(h_done, q - 1)
                last = three_pass(ps_h3[par], w13_hi[:, 1, p, :], w13_lo[:, 1, p, :], xs_hi, xs_lo)
                if p >= 1:
                    if p == 1:
                        pe.wait_ge(cT_ready, b + 1)
                    last = nc.tensor.matmul(ps_c[par][:, :], sel[:, P * (p - 1):P * p], cT[b_parity(b, par, p)],
                                            start=True, stop=True)
                last.then_inc(h3_ready, 1)
                if down_prev:
                    down(b if p >= 2 else b - 1, (p - 2) % NP, par)

            def b_parity(b, par, p):
                return (par + p) % 2

            def down(b, p, par):
                q = b * NP + p
                if p == 0 and not (isinstance(b, int) and b == 0):
                    pe.wait_ge(y_evacuated, b)
                pe.wait_ge(h_split, q + 1)
                if p == 1:
                    c = cT[b_parity(b, par, p)]
                    nc.tensor.matmul(ps_y[:, :], be_hi[:, :], c, start=False, stop=False)
                    nc.tensor.matmul(ps_y[:, :], be_lo[:, :], c, start=False, stop=False)
                last = three_pass(ps_y[:, :], w2_hi[:, p, :], w2_lo[:, p, :], h_hi[p % 3], h_lo[p % 3],
                                  start=p == 0, stop=p == NP - 1)
                last.then_inc(down_done, 1)

            def y_transposes(b):
                pe.wait_ge(y_evacuated, b + 1)
                pe.wait_ge(cT_ready, min(b + 2, B) if isinstance(b, int) else b + 2)
                for t in range(NT):
                    last = nc.tensor.transpose(ps_m[:, P * t:P * t + P], y_sb[:, P * t:P * t + P], ident)
                last.then_inc(yT_ready, 1)

            def c_transposes(b):
                pe.wait_ge(combine_ready, b + 1)
                for t in range(NT):
                    last = nc.tensor.transpose(ps_m[0:2 * E, P * t:P * t + P], comb[:, t, :], ident)
                last.then_inc(cT_in_psum, 1)

            def expert_batch(b, parity, first, last_batch):
                for p in range(NP):
                    unit(b, p, (parity + p) % 2, not first or p >= 2)
                    if p == 4 and not first:
                        y_transposes(b - 1)
                    if p == 7 and not last_batch:
                        if not first:
                            pe.wait_ge(y_normed, b)
                        c_transposes(b + 1)

            pe.wait_ge(maxes_done, B * G * NU)
            pe.wait_ge(exps_done, B * G * NV)
            pe.wait_ge(o_evacuated, B * G)
            pe.wait_ge(misc_evacuated, use_number(B, "logits") + 1)
            pe.wait_ge(weights_lo, 5)
            c_transposes(0)
            expert_batch(0, 0, True, False)
            with pe.Fori(0, B // 2 - 1) as i:
                expert_batch(i * 2 + 1, 1, False, False)
                expert_batch(i * 2 + 2, 0, False, False)
            expert_batch(B - 1, 1, False, True)
            down(B - 1, NP - 2, (B - 1 + NP - 2) % 2)
            down(B - 1, NP - 1, (B - 1 + NP - 1) % 2)
            y_transposes(B - 1)

        @block.scalar
        def _(act):
            def split_hi(number, dst, bias, done):
                act.wait_ge(misc_ready, number + 1)
                nc.scalar.activation(dst, ps_m[:, :], ACT.Identity, bias=bias).then_inc(done, 1)

            def read_qk(s, number, which):
                if which == 0 and not (isinstance(s, int) and s == 0):
                    for g in range(G):
                        act.wait_ge(kq_in[g], s * (16 * GROUP_DMAS))
                act.wait_ge(misc_ready, number + 1)
                scale, bias = (col[:, 4:5], col[:, 5:6]) if which == 0 else (1.0, col[:, 1:2])
                nc.scalar.activation(qk_split[:, which, 0, :], ps_m[:, :], ACT.Identity, bias=bias, scale=scale)
                nc.scalar.activation(qk_f[:, which, :], ps_m[:, :], ACT.Identity, bias=bias, scale=scale
                                     ).then_inc(misc_evacuated, 1)

            def read_v(s, number):
                if not (isinstance(s, int) and s == 0):
                    act.wait_ge(v_placed, s * G)
                act.wait_ge(misc_ready, number + 1)
                nc.scalar.activation(vraw[:, :, :].rearrange("p t c -> p (t c)"), ps_m[:, :], ACT.Identity
                                     ).then_inc(misc_evacuated, 1)

            def place_shift(b, g):
                act.wait_ge(shift_in_psum, b * G + (g + 1))
                nc.scalar.activation(qd[ROWS:ROWS_SHIFTED, g, :], ps_b[0][0:2 * HG, :], ACT.Identity
                                     ).then_inc(shift_placed, 1)

            def exponentials(b, g, v):
                k, heads = EXP_UNITS[v]
                n = b * G + g
                if v in (0, 4, 8, 10) and not (isinstance(n, int) and n == 0):
                    act.wait_ge(pv_done, n * NT - k)
                act.wait_ge(st_ready, n * NV + (v + 1))
                width = P * (k + 1)
                src = ps_b[exp_bank(v)][:, 0:len(heads) * width].rearrange("p (h q) -> p h q", q=width)
                nc.scalar.activation(pt[:, k, heads[0]:heads[0] + len(heads), T - width:T], src, ACT.Exp
                                     ).then_inc(exps_done, 1)

            def evacuate_o(b, g):
                act.wait_ge(pv_done, (b * G + g) * NT + NT)
                nc.scalar.activation(o_raw[:, g, :], ps_o[:, :], ACT.Identity).then_inc(o_evacuated, 1)

            def split_experts(part):
                if part == 0:
                    act.wait_ge(w_in, 32)
                    for dst, src in ((gw_hi, gw), (be_hi, be)):
                        nc.scalar.activation(dst[:, :], src[:, :], ACT.Identity).then_inc(weights_hi, 1)
                    nc.scalar.activation(sel[:, :], cst[0:2 * E, SEL:TRI], ACT.Identity).then_inc(weights_hi, 1)
                dst, _, src = third(part)
                nc.scalar.activation(dst, src, ACT.Identity).then_inc(weights_hi, 1)

            def iteration(b, tail, stage):
                def use(name):
                    return use_number(b, name)

                for g in range(G):
                    before = (b, g - 1) if g else (b - 1, G - 1)
                    for v in range(NV):
                        if v == SHIFT_PLACE and follower(b, g, stage):
                            place_shift(*follower(b, g, stage))
                        exponentials(b, g, v)
                        if v == 0 and g == 0 and stage:
                            split_hi(use("xT"), xnT_hi[:, :], 0.0, xT_hi)
                        if v == 0 and g == 1 and stage:
                            read_qk(b + 1, use("q"), 0)
                        if v == 4 and g == 1 and not tail:
                            act.wait_ge(weights_lo, 3)
                        if v == 4 and (tail or g):
                            if tail and g == 1:
                                act.wait_ge(misc_ready, use("otr3") + 1)
                            evacuate_o(*before)
                        if v == 5 and g == 1 and stage:
                            read_qk(b + 1, use("k"), 1)
                        if v == 7 and g == 1 and tail:
                            split_hi(use("onT"), oT_hi[:, :], col[:, 2:3], onT_hi)
                        if v == 7 and g == 2 and stage:
                            read_v(b + 1, use("v"))
                        if v == 7 and g == 3 and tail:
                            act.wait_ge(xf_saved, (b - 1) * 32 + 1)
                            split_hi(use("xfT"), xfs_hi[:, :], 0.0, xfT_hi_done)
                        if v == 5 and g < 3 and not tail:
                            split_experts(g)

            act.wait_ge(wattn_in, 16)
            nc.scalar.activation(wa_hi[:, :, :], wa[:, :, :], ACT.Identity).then_inc(attn_weights, 1)
            act.wait_ge(const_in, 96)
            nc.scalar.activation(ident_bf[:, :], cst[:, IDENT:IDENT + P], ACT.Identity).then_inc(small_hi, 1)
            nc.scalar.activation(mask_bf[:, :], cst[:, MASK:MASK + P], ACT.Identity).then_inc(small_hi, 1)
            nc.scalar.activation(col[:, 5:6], col[:, 0:1], ACT.Identity, scale=col[:, 4:5]).then_inc(small_hi, 1)
            split_hi(use_number(None, "xT"), xnT_hi[:, :], 0.0, xT_hi)
            act.wait_ge(small_hi, 3)
            read_qk(0, use_number(None, "q"), 0)
            read_qk(0, use_number(None, "k"), 1)
            read_v(0, use_number(None, "v"))
            place_shift(0, 0)
            iteration(0, tail=False, stage=True)
            with act.Fori(1, B - 1) as b:
                iteration(b, tail=True, stage=True)
            iteration(B - 1, tail=True, stage=False)
            evacuate_o(B - 1, G - 1)
            split_hi(use_number(B, "onT"), oT_hi[:, :], col[:, 2:3], onT_hi)
            act.wait_ge(xf_saved, (B - 1) * 32 + 1)
            split_hi(use_number(B, "xfT"), xfs_hi[:, :], 0.0, xfT_hi_done)
            act.wait_ge(misc_evacuated, use_number(B, "logits") + 1)
            ge = gexp[:, :, :, :].rearrange("p b t e -> p (b t e)")
            nc.scalar.activation(ge, ge, ACT.Exp).then_inc(gate_exp, 1)

            def silu_tile(b, p, par):
                q = b * NP + p
                act.wait_ge(h1_ready, q + 1)
                if not (isinstance(q, int) and q < 3):
                    act.wait_ge(h_done, q - 2)
                nc.scalar.activation(silu[p % 3], ps_h1[par], ACT.Silu, bias=b13c[:, 0, p:p + 1]).then_inc(silu_done, 1)

            def hidden_hi(b, p):
                q = b * NP + p
                act.wait_ge(h_done, q + 1)
                if not (isinstance(q, int) and q < 3):
                    act.wait_ge(down_done, q - 2)
                nc.scalar.activation(h_hi[p % 3], hbuf[p % 3], ACT.Identity).then_inc(h_hi_done, 1)

            def evacuate_y(b):
                act.wait_ge(down_done, b * NP + NP)
                nc.scalar.activation(y_sb, ps_y[:, :], ACT.Identity, bias=col[:, 3:4]).then_inc(y_evacuated, 1)

            def evacuate_c(b, parity):
                act.wait_ge(cT_in_psum, b + 1)
                nc.scalar.activation(cT[parity], ps_m[0:2 * E, :], ACT.Identity).then_inc(cT_ready, 1)

            def expert_batch(b, parity, first, last_batch):
                for p in range(NP):
                    if p == 2 and not first:
                        evacuate_y(b - 1)
                    silu_tile(b, p, (parity + p) % 2)
                    if not first or p >= 1:
                        hidden_hi(b if p else b - 1, (p - 1) % NP)
                    if p == NP - 1 and not last_batch:
                        evacuate_c(b + 1, 1 - parity)

            act.wait_ge(pv_done, B * G * NT)
            act.wait_ge(st_ready, B * G * NV)
            evacuate_c(0, 0)
            expert_batch(0, 0, True, False)
            with act.Fori(0, B // 2 - 1) as i:
                expert_batch(i * 2 + 1, 1, False, False)
                expert_batch(i * 2 + 2, 0, False, False)
            expert_batch(B - 1, 1, False, True)
            hidden_hi(B - 1, NP - 1)
            evacuate_y(B - 1)

        @block.vector
        def _(dve):
            def norm_stats(i, count, tiles):
                for t in range(NT):
                    nc.vector.bn_stats(bst[:, i, t, :], tiles(t)).then_inc(stats[i], 1)
                dve.wait_ge(stats[i], count * NT + NT)
                dve.sem_inc(wait_carrier[0], 1)
                for t in range(NT):
                    last = nc.vector.bn_aggr(mv[:, i, t, :], bst[:, i, t, :])
                last.then_inc(moments[i], 1)

            def normalise(i, count, tiles, dst, done):
                dve.wait_ge(rstds[i], count + 1)
                for t in range(NT):
                    last = nc.vector.tensor_scalar(dst[:, t, :], tiles(t), mv[:, i, t, 0:1], rstd[:, i, t:t + 1],
                                                   ALU.subtract, ALU.mult)
                last.then_inc(done, 1)

            def x_tile(b):
                return lambda t: xall[:, tile_of(b, t), :].rearrange("p a c -> p (a c)")

            def tile_in(buf):
                return lambda t: buf[:, t, :]

            def split_lo(dst, hi, hi_done, count, bias=0.0):
                dve.wait_ge(hi_done, count + 1)
                nc.vector.scalar_tensor_tensor(dst, ps_m[:, :], bias, hi.bitcast(F32), ALU.add, ALU.subtract
                                               ).then_inc(misc_evacuated, 1)

            def maxima(b, g, u):
                t, heads = MAX_UNITS[u]
                n = b * G + g
                if u == 0 and not (isinstance(n, int) and n < 2):
                    dve.wait_ge(shift_split, n - 1)
                dve.wait_ge(scores_ready, n * NU + (u + 1))
                width = T - P * t
                pitch = 512 if width > 256 else width
                src = ps_a[u % 2][:, 0:len(heads) * pitch].rearrange("p (h k) -> p h k", k=pitch)[:, :, 0:width]
                nc.vector.tensor_reduce(negmax[:, g % 2, t, heads[0]:heads[0] + len(heads)], src, AX.X, ALU.max,
                                        negate=True).then_inc(maxes_done, 1)

            def normalise_o(b, t, number):
                dve.wait_ge(misc_ready, number + 1)
                heads = ps_m[:, :].rearrange("p (h w) -> p h w", w=VW)
                nc.vector.reciprocal(rsum[:, t, :], heads[:, :, D]).then_inc(sums_inverted, 1)
                dve.wait_ge(sums_inverted, b * NT + (t + 1))
                nc.vector.tensor_tensor(on[:, t, :].rearrange("p (h d) -> p h d", d=D), heads[:, :, 0:D],
                                        rsum[:, t, :].unsqueeze(2).broadcast_to([P, H, D]), ALU.mult
                                        ).then_inc(misc_evacuated, 1)

            def add_bo(number):
                dve.wait_ge(misc_ready, number + 1)
                nc.vector.tensor_tensor(att[:, :, :], ps_m[:, :].rearrange("p (t c) -> p t c", t=NT),
                                        row[:, 0:C].unsqueeze(1).broadcast_to([P, NT, C]), ALU.add
                                        ).then_inc(misc_evacuated, 1)

            def shift_logits(b, number):
                dve.wait_ge(misc_ready, number + 1)
                lg = ps_m[:, 0:NT * E].rearrange("p (t e) -> p t e", e=E)
                nc.vector.tensor_reduce(lmax[:, :], lg, AX.X, ALU.max).then_inc(logit_max, 1)
                dve.wait_ge(logit_max, b + 1)
                nc.vector.tensor_tensor(gexp[:, batch_of(b, 1), :, :].rearrange("p a t e -> p (a t) e"), lg, lmax[:, :].unsqueeze(2).broadcast_to([P, NT, E]),
                                        ALU.subtract).then_inc(misc_evacuated, 1)

            def split_experts(part):
                dve.wait_ge(weights_hi, 4 + part)
                if part == 0:
                    for dst, src, hi in ((gw_lo, gw, gw_hi), (be_lo, be, be_hi)):
                        nc.vector.tensor_tensor(dst[:, :], src[:, :], hi[:, :].bitcast(F32), ALU.subtract
                                                ).then_inc(weights_lo, 1)
                hi, lo, src = third(part)
                nc.vector.tensor_tensor(lo, src, hi.bitcast(F32), ALU.subtract).then_inc(weights_lo, 1)

            def iteration(b, tail, stage, stage_norm):
                def use(name):
                    return use_number(b, name)

                for g in range(G):
                    for m in range(NU):
                        if units_ahead(b, g, stage, m):
                            maxima(*units_ahead(b, g, stage, m))
                        if m == 0:
                            if g == 1 and stage_norm:
                                norm_stats(0, b + 2, x_tile(b + 2))
                            if g == 2 and tail:
                                add_bo(use("oproj"))
                            if g == 3 and tail:
                                dve.wait_ge(x2_ready, b)
                                norm_stats(2, b - 1, x_tile(b - 1))
                        if m == 1:
                            if g == 0 and stage:
                                split_lo(xnT_lo[:, :], xnT_hi[:, :], xT_hi, b + 1)
                            if g == 2 and tail:
                                dve.wait_ge(misc_evacuated, use("oproj") + 1)
                                norm_stats(1, b - 1, tile_in(att))
                        if m == 2:
                            if g == 1 and tail:
                                normalise_o(b - 1, 3, use("otr3"))
                            if g == 1 and stage_norm:
                                dve.wait_ge(misc_ready, use("xT") + 1)
                                normalise(0, b + 2, x_tile(b + 2), xn, xn_ready)
                            if g == 3 and tail:
                                normalise(2, b - 1, x_tile(b - 1), xf, xf_ready)
                        if m == 3:
                            if g == 0 and tail:
                                normalise_o(b - 1, 0, use("otr0"))
                            if g == 2 and tail:
                                normalise(1, b - 1, tile_in(att), attn_n, attn_normed)
                        if m == 4 and g == 0 and tail:
                            normalise_o(b - 1, 1, use("otr1"))
                        if m == 5:
                            if g == 0 and tail:
                                normalise_o(b - 1, 2, use("otr2"))
                            if g == 1 and tail:
                                split_lo(oT_lo[:, :], oT_hi[:, :], onT_hi, b - 1, col[:, 2:3])
                            if g == 3 and tail:
                                split_lo(xfs_lo[:, :], xfs_hi[:, :], xfT_hi_done, b - 1)
                                shift_logits(b - 1, use("logits"))
                        if m == 4 and g < 3 and not tail:
                            split_experts(g)

            nc.vector.memset(halfneg[:, :], -0.5).then_inc(half_set, 1)
            dve.wait_ge(x_first, 16)
            norm_stats(0, 0, x_tile(0))
            dve.wait_ge(attn_weights, 1)
            nc.vector.tensor_tensor(wa_lo[:, :, :], wa[:, :, :], wa_hi[:, :, :].bitcast(F32), ALU.subtract
                                    ).then_inc(attn_weights, 1)
            normalise(0, 0, x_tile(0), xn, xn_ready)
            split_lo(xnT_lo[:, :], xnT_hi[:, :], xT_hi, 0)
            dve.wait_ge(x_rest, 16)
            norm_stats(0, 1, x_tile(1))
            normalise(0, 1, x_tile(1), xn, xn_ready)
            for u in range(NU):
                maxima(0, 0, u)
            for u in range(NU // 2):
                maxima(0, 1, u)
            iteration(0, tail=False, stage=True, stage_norm=True)
            with dve.Fori(1, B - 2) as b:
                iteration(b, tail=True, stage=True, stage_norm=True)
            iteration(B - 2, tail=True, stage=True, stage_norm=False)
            iteration(B - 1, tail=True, stage=False, stage_norm=False)
            for t in range(NT):
                normalise_o(B - 1, t, use_number(B, f"otr{t}"))
            split_lo(oT_lo[:, :], oT_hi[:, :], onT_hi, B - 1, col[:, 2:3])
            add_bo(use_number(B, "oproj"))
            dve.wait_ge(misc_evacuated, use_number(B, "oproj") + 1)
            norm_stats(1, B - 1, tile_in(att))
            normalise(1, B - 1, tile_in(att), attn_n, attn_normed)
            dve.wait_ge(x2_ready, B)
            norm_stats(2, B - 1, x_tile(B - 1))
            normalise(2, B - 1, x_tile(B - 1), xf, xf_ready)
            split_lo(xfs_lo[:, :], xfs_hi[:, :], xfT_hi_done, B - 1)
            shift_logits(B - 1, use_number(B, "logits"))

            steps = [0]

            def step(instruction):
                steps[0] += 1
                instruction.then_inc(router_step, 1)
                dve.wait_ge(router_step, steps[0])

            def tt(dst, a, b, op):
                step(nc.vector.tensor_tensor(dst, a, b, op))

            N = B * NT

            def per_tile(a, n):
                return a.unsqueeze(2).broadcast_to([P, N, n])

            dve.wait_ge(pv_done, B * G * NT)
            dve.wait_ge(gate_exp, 1)
            ge = gexp[:, :, :, :].rearrange("p b t e -> p (b t) e")
            total, inv, m1, w1, m2, w2_ = (r[:, :] for r in rm)
            orig, s, sm, e1, o1, sm2, e2, o2, pick = rt[0:9]
            step(nc.vector.tensor_reduce(total, ge, AX.X, ALU.add))
            step(nc.vector.reciprocal(inv, total))
            tt(orig, ge, per_tile(inv, E), ALU.mult)
            tt(s, orig, row[:, C:C + E].unsqueeze(1).broadcast_to([P, N, E]), ALU.add)
            hi2 = rt[9][:, :, 0:2 * EG].rearrange("p t (g k) -> p t g k", k=2)
            lo2 = rt[10][:, :, 0:2 * EG].rearrange("p t (g k) -> p t g k", k=2)
            quad = s.rearrange("p t (g k a) -> p t g k a", k=2, a=2)
            for k in range(2):
                tt(hi2[:, :, :, k], quad[:, :, :, k, 0], quad[:, :, :, k, 1], ALU.max)
                tt(lo2[:, :, :, k], quad[:, :, :, k, 0], quad[:, :, :, k, 1], ALU.min)
            top, mn, ml, gs, rank, keep, pen = rs[0:7]
            tt(top, hi2[:, :, :, 0], hi2[:, :, :, 1], ALU.max)
            tt(mn, hi2[:, :, :, 0], hi2[:, :, :, 1], ALU.min)
            tt(ml, lo2[:, :, :, 0], lo2[:, :, :, 1], ALU.max)
            tt(mn, mn, ml, ALU.max)
            tt(gs, top, mn, ALU.add)
            other = gs.unsqueeze(2).broadcast_to([P, N, EG, EG])
            own = gs.unsqueeze(3).broadcast_to([P, N, EG, EG])
            gt = rt[11].rearrange("p t (g h) -> p t g h", h=EG)
            eq = rt[12].rearrange("p t (g h) -> p t g h", h=EG)
            tt(gt, other, own, ALU.is_gt)
            tt(eq, other, own, ALU.is_equal)
            tt(rt[12], rt[12], cst[:, TRI:TRI + EG * EG].unsqueeze(1).broadcast_to([P, N, EG * EG]), ALU.mult)
            tt(rt[11], rt[11], rt[12], ALU.add)
            step(nc.vector.tensor_reduce(rank, gt, AX.X, ALU.add))
            step(nc.vector.tensor_scalar(keep, rank, 2.0, None, ALU.is_lt))
            step(nc.vector.tensor_scalar(pen, keep, BIG, BIG, ALU.mult, ALU.subtract))
            s4 = s.rearrange("p t (g k) -> p t g k", k=E // EG)
            sm4 = sm.rearrange("p t (g k) -> p t g k", k=E // EG)
            tt(sm4, s4, keep.unsqueeze(3).broadcast_to([P, N, EG, E // EG]), ALU.mult)
            tt(sm4, sm4, pen.unsqueeze(3).broadcast_to([P, N, EG, E // EG]), ALU.add)
            rev = cst[:, REV:REV + E].unsqueeze(1).broadcast_to([P, N, E])

            def first_largest(src, largest, weight, marked, one_hot):
                step(nc.vector.tensor_reduce(largest, src, AX.X, ALU.max))
                tt(marked, src, per_tile(largest, E), ALU.is_equal)
                tt(marked, marked, rev, ALU.mult)
                step(nc.vector.tensor_reduce(weight, marked, AX.X, ALU.max))
                tt(one_hot, marked, per_tile(weight, E), ALU.is_equal)

            first_largest(sm, m1, w1, e1, o1)
            step(nc.vector.scalar_tensor_tensor(sm2, o1, -BIG, sm, ALU.mult, ALU.add))
            first_largest(sm2, m2, w2_, e2, o2)
            tt(pick, o1, o2, ALU.add)
            tt(comb_all[:, :, :], orig, pick, ALU.mult)

            def combine(b):
                if not (isinstance(b, int) and b == 0):
                    dve.wait_ge(cT_in_psum, b)
                c = comb_all[:, batch_of(b, NT), :]
                nc.vector.tensor_copy(comb[:, :, 0:E].bitcast(F32R), c).then_inc(comb_hi, 1)
                dve.wait_ge(comb_hi, b + 1)
                nc.vector.tensor_tensor(comb[:, :, E:2 * E].bitcast(F32R), c, comb[:, :, 0:E], ALU.subtract
                                        ).then_inc(combine_ready, 1)

            def hidden(b, p, par):
                q = b * NP + p
                dve.wait_ge(silu_done, q + 1)
                dve.wait_ge(h3_ready, q + 1)
                if not (isinstance(q, int) and q < 3):
                    dve.wait_ge(h_split, q - 2)
                if p == 0:
                    nc.vector.scalar_tensor_tensor(hbuf[0], ps_h3[par], b13c[:, 1, 0:1], silu[0], ALU.add, ALU.mult
                                                   ).then_inc(h_done, 1)
                    return
                nc.vector.scalar_tensor_tensor(gated[p % 3], ps_h3[par], b13c[:, 1, p:p + 1], silu[p % 3],
                                               ALU.add, ALU.mult).then_inc(gated_done, 1)
                dve.wait_ge(gated_done, b * (NP - 1) + p)
                nc.vector.tensor_tensor(hbuf[p % 3], ps_c[par][:, :], gated[p % 3], ALU.mult).then_inc(h_done, 1)

            def y_tiles(t):
                return ps_m[:, P * t:P * t + P]

            def expert_batch(b, parity, first, last_batch):
                for p in range(NP):
                    hidden(b, p, (parity + p) % 2)
                    if p == 5 and not first:
                        dve.wait_ge(yT_ready, b)
                        norm_stats(3, b - 1, y_tiles)
                    if p == 6 and not first:
                        normalise(3, b - 1, y_tiles, y_n, y_normed)
                    if p == 2 and not last_batch:
                        combine(b + 1)

            combine(0)
            expert_batch(0, 0, True, False)
            with dve.Fori(0, B // 2 - 1) as i:
                expert_batch(i * 2 + 1, 1, False, False)
                expert_batch(i * 2 + 2, 0, False, False)
            expert_batch(B - 1, 1, False, True)
            dve.wait_ge(yT_ready, B)
            norm_stats(3, B - 1, y_tiles)
            normalise(3, B - 1, y_tiles, y_n, y_normed)

        @block.gpsimd
        def _(pool):
            def carry_wait():
                pool.sem_inc(wait_carrier[1], 1)

            def inverse_deviation(i, count):
                pool.wait_ge(moments[i], count + 1)
                carry_wait()
                nc.gpsimd.tensor_scalar(ve[:, i, :], mv[:, i, :, 1], EPS, 1.0, ALU.add, ALU.mult
                                        ).then_inc(eps_added[i], 1)
                pool.wait_ge(eps_added[i], count + 1)
                nc.gpsimd.tensor_tensor(rstd[:, i, :], ve[:, i, :], halfneg[:, :], ALU.pow).then_inc(rstds[i], 1)
                pool.wait_ge(rstds[i], count + 1)

            def qk_lower(s, number, which):
                pool.wait_ge(misc_evacuated, number + 1)
                nc.gpsimd.tensor_tensor(qk_split[:, which, 1, :], qk_f[:, which, :],
                                        qk_split[:, which, 0, :].bitcast(F32), ALU.subtract).then_inc(qk_lower_done, 1)
                pool.wait_ge(qk_lower_done, s * 2 + (which + 1))

            def place_v(s, g, number):
                pool.wait_ge(misc_evacuated, number + 1)
                if not (isinstance(s, int) and s == 0):
                    pool.wait_ge(pv_done, (s * G + g - G) * NT + NT)
                carry_wait()
                nc.gpsimd.tensor_scalar(vaug[:, :, HG * g:HG * (g + 1), 0:D],
                                        vraw[:, :, D * HG * g:D * HG * (g + 1)].rearrange("p t (h d) -> p t h d", d=D),
                                        1.0, 1.0, ALU.mult, ALU.mult).then_inc(v_placed, 1)
                pool.wait_ge(v_placed, s * G + (g + 1))

            def mask_exponentials(b, g, upper):
                n = b * G + g
                pool.wait_ge(exps_done, n * NV + (8 if upper else NV))
                carry_wait()
                k = slice(2, 4) if upper else slice(0, 2)
                d = T - P
                for part in range(2):
                    v = pt[CHUNK * part:CHUNK * (part + 1), k, :, d + CHUNK * part:d + CHUNK * (part + 1)]
                    nc.gpsimd.affine_select(out=v, in_=v, compare_op=ALU.is_ge, fill=0.0, base=0,
                                            pattern=[[0, 2], [0, HG], [1, CHUNK]], channel_multiplier=-1
                                            ).then_inc(masks_done, 1)
                    pool.wait_ge(masks_done, n * 6 + ((0 if upper else 3) + part + 1))
                    carry_wait()
                nc.gpsimd.memset(pt[0:CHUNK, k, :, d + CHUNK:T], 0.0).then_inc(masks_done, 1)
                pool.wait_ge(masks_done, n * 6 + (3 if upper else 6))

            def split_shift(b, g):
                n = b * G + g
                pool.wait_ge(maxes_done, n * NU + NU)
                if not (isinstance(n, int) and n == 0):
                    pool.wait_ge(shift_in_psum, n)
                carry_wait()
                src = negmax[:, g % 2, :, :]
                nc.gpsimd.tensor_scalar(shift[:, :, 0:HG].bitcast(F32R), src, 1.0, 1.0, ALU.mult, ALU.mult
                                        ).then_inc(shift_hi, 1)
                pool.wait_ge(shift_hi, n + 1)
                nc.gpsimd.tensor_tensor(shift[:, :, HG:2 * HG].bitcast(F32R), src, shift[:, :, 0:HG], ALU.subtract
                                        ).then_inc(shift_split, 1)
                pool.wait_ge(shift_split, n + 1)

            def add_x(b):
                pool.wait_ge(attn_normed, b + 1)
                v = xall[:, batch_of(b, NT), :]
                nc.gpsimd.tensor_tensor(v, v, attn_n[:, :, :], ALU.add).then_inc(x2_ready, 1)
                pool.wait_ge(x2_ready, b + 1)

            def iteration(b, tail, stage, v_number, stage_norm):
                def use(name):
                    return use_number(b, name)

                for g in range(G):
                    if tail or g:
                        mask_exponentials(*((b, g - 1) if g else (b - 1, G - 1)), False)
                    if g == 1 and stage:
                        qk_lower(b + 1, use("q"), 0)
                    if g == 3 and tail:
                        inverse_deviation(2, b - 1)
                    if follower(b, g, stage):
                        split_shift(*follower(b, g, stage))
                    if g == 0:
                        place_v(b, G - 1, v_number)
                    if g == 1:
                        if stage:
                            qk_lower(b + 1, use("k"), 1)
                        if stage_norm:
                            inverse_deviation(0, b + 2)
                    if g == 2 and tail:
                        inverse_deviation(1, b - 1)
                    mask_exponentials(b, g, True)
                    if g == 2 and tail:
                        add_x(b - 1)
                    if g == 3 and stage:
                        for gg in range(G - 1):
                            place_v(b + 1, gg, use("v"))

            nc.gpsimd.memset(km[:, :, :, :].rearrange("p g j t -> p (g j t)").bitcast(F32), 0.0).then_inc(km_zeroed, 1)
            pool.wait_ge(half_set, 1)
            inverse_deviation(0, 0)
            nc.gpsimd.memset(vaug[:, :, :, D + 1:VW], 0.0).then_inc(ones_placed, 1)
            nc.gpsimd.memset(vaug[:, :, :, D:D + 1], 1.0).then_inc(ones_placed, 1)
            pool.wait_ge(km_zeroed, 1)
            pool.wait_ge(ones_placed, 2)
            pool.wait_ge(const_in, 96)
            nc.gpsimd.tensor_scalar(km[ROWS:ROWS_SHIFTED, :, :, :],
                                    cst[ROWS:ROWS_SHIFTED, ONES:ONES + HG].unsqueeze(1).unsqueeze(3).broadcast_to(
                                        [ROWS_SHIFTED - ROWS, G, HG, T]), 1.0, 1.0, ALU.mult, ALU.mult
                                    ).then_inc(operands_cleared, 1)
            pool.wait_ge(operands_cleared, 1)
            qk_lower(0, use_number(None, "q"), 0)
            qk_lower(0, use_number(None, "k"), 1)
            for g in range(G - 1):
                place_v(0, g, use_number(None, "v"))
            inverse_deviation(0, 1)
            split_shift(0, 0)
            iteration(0, False, True, use_number(None, "v"), True)
            iteration(1, True, True, use_number(0, "v"), True)
            with pool.Fori(2, B - 2) as b:
                iteration(b, True, True, use_number(b, "v") - len(USES), True)
            iteration(B - 2, True, True, use_number(B - 3, "v"), False)
            iteration(B - 1, True, False, use_number(B - 2, "v"), False)
            mask_exponentials(B - 1, G - 1, False)
            inverse_deviation(1, B - 1)
            add_x(B - 1)
            inverse_deviation(2, B - 1)

            def hidden_lower(b, p):
                q = b * NP + p
                pool.wait_ge(h_hi_done, q + 1)
                nc.gpsimd.tensor_tensor(h_lo[p % 3], hbuf[p % 3], h_hi[p % 3].bitcast(F32), ALU.subtract
                                        ).then_inc(h_split, 1)

            def finish(b):
                pool.wait_ge(y_normed, b + 1)
                pool.wait_ge(stored, b * 16 + 1)
                nc.gpsimd.tensor_tensor(out_sb, y_n, xall[:, batch_of(b, NT), :], ALU.add).then_inc(out_ready, 1)

            def expert_batch(b, first):
                for p in range(NP):
                    hidden_lower(b, p)
                    if p == 5 and not first:
                        inverse_deviation(3, b - 1)
                    if p == 7 and not first:
                        finish(b - 1)

            expert_batch(0, True)
            with pool.Fori(1, B) as b:
                expert_batch(b, False)
            inverse_deviation(3, B - 1)
            finish(B - 1)


_OUT = ((B, T, C), "float32")


def kernel(**inputs):
    import concourse.bacc as bacc
    from concourse.bass_utils import run_bass_kernel_spmd

    a = {k: np.asarray(v) for k, v in inputs.items()}
    at, ff = (lambda n: a["L0_attn_" + n]), (lambda n: a["L0_ffn_" + n])

    def pairs_in(w):
        return w.reshape(E // 2, 2, C, INTER).transpose(2, 0, 1, 3).reshape(C, E // 2, P)

    def up_weights(shared, experts):
        return np.concatenate([shared[:, None, :], pairs_in(experts)], axis=1)

    w_attn = np.stack([at("Wq").T, at("Wk").T, at("Wv").T, at("Wo").T], axis=1)
    cols = np.stack([at("bq"), at("bk"), at("bv"), ff("bs2"),
                     np.broadcast_to(at("attn_scale"), (C,))], axis=1)
    w13 = np.stack([up_weights(ff("ws1"), ff("We1")), up_weights(ff("ws3"), ff("We3"))], axis=1).reshape(C, -1)
    w2 = np.concatenate([ff("ws2")[None], ff("We2").reshape(E // 2, P, C)], axis=0).transpose(1, 0, 2).reshape(P, -1)
    b13 = np.stack([np.concatenate([ff("bs1")[None], ff("be1").reshape(E // 2, P)], axis=0).T,
                    np.concatenate([ff("bs3")[None], ff("be3").reshape(E // 2, P)], axis=0).T], axis=1)
    rows = np.broadcast_to(np.concatenate([at("bo"), ff("gate_b")])[None, :], (P, C + E))
    arrays = {
        "x": a["L0_attn_x"].reshape(B * T, C), "w_attn": w_attn, "cols": cols, "w13": w13, "w2": w2, "b13": b13,
        "gate_w": ff("gate_w").T, "rows": rows, "be2": np.concatenate([ff("be2"), ff("be2")], axis=0),
        "const": shape_constants(),
    }
    arrays = {k: np.ascontiguousarray(v) for k, v in arrays.items()}
    nc = bacc.Bacc("TRN2", target_bir_lowering=False, num_devices=1)
    args = [nc.dram_tensor(f"in_{k}", v.shape, mybir.dt.from_np(v.dtype), kind="ExternalInput").ap()
            for k, v in arrays.items()]
    args.append(nc.dram_tensor("out_0", (B * T, C), F32, kind="ExternalOutput").ap())
    block_kernel(nc, *args)
    r = run_bass_kernel_spmd(nc, [{f"in_{k}": v for k, v in arrays.items()}], core_ids=[0])
    return r.results[0]["out_0"].reshape(_OUT[0])
```

```python
from contextlib import ExitStack

import numpy as np

import concourse.bass as bass
from concourse import mybir

F32 = mybir.dt.float32
F32R = mybir.dt.float32r
BF16 = mybir.dt.bfloat16
ALU = mybir.AluOpType
ACT = mybir.ActivationFunctionType
AX = mybir.AxisListType

P = 128
B, T, C = 8, 512, 128
NT = T // P
CHUNK = 64
H, D = 16, 8
G, HG = 4, 4
E, INTER = 16, 64
NP = 1 + E // 2
EG = 4
VW = 32
EPS = 1e-5
MASKED = -3.0e38
BIG = 1.0e30

ROWS = 3 * HG * D
ROWS_SHIFTED = ROWS + 2 * HG

MAX_UNITS = [(0, (0, 1)), (0, (2, 3)), (1, (0, 1)), (1, (2, 3)), (2, (0, 1, 2, 3)), (3, (0, 1, 2, 3))]
NU = len(MAX_UNITS)
EXP_UNITS = [(3, (0,)), (3, (1,)), (3, (2,)), (3, (3,)), (2, (0,)), (2, (1,)), (2, (2,)), (2, (3,)),
             (1, (0, 1)), (1, (2, 3)), (0, (0, 1, 2, 3))]
NV = len(EXP_UNITS)
SHIFT_PLACE = 8


def exp_bank(v):
    return v % 2 if v < SHIFT_PLACE else (v + 1) % 2


USES = ["xT", "otr0", "otr1", "otr2", "q", "otr3", "k", "onT", "oproj", "v", "xfT", "logits"]
TAIL = ("otr0", "otr1", "otr2", "otr3", "onT", "oproj", "xfT", "logits")
STAGE = ("xT", "q", "k", "v")
FIRST_USES = [u for u in USES if u not in TAIL]
LAST_USES = [u for u in USES if u not in STAGE]

ROUTED_EARLY = B - 2
LAST = B - 1

GROUP_DMAS = 2 + 2 * HG


def use_number(b, name):
    if b is None:
        return STAGE.index(name)
    after_prologue = len(STAGE)
    after_first = after_prologue + len(FIRST_USES)
    if isinstance(b, int) and b == 0:
        return after_prologue + FIRST_USES.index(name)
    if isinstance(b, int) and b == B - 1:
        return after_first + len(USES) * (B - 2) + LAST_USES.index(name)
    if isinstance(b, int) and b == B:
        return after_first + len(USES) * (B - 2) + len(LAST_USES) + TAIL.index(name)
    return b * len(USES) + (after_first - len(USES) + USES.index(name))


IDENT, MASK, SEL, TRI, REV = 0, P, 2 * P, 2 * P + (NP - 1) * P, 2 * P + (NP - 1) * P + EG * EG
ONES = REV + E
NCONST = ONES + HG


def follower(b, g, stage):
    if g < G - 1:
        return b, g + 1
    return (b + 1, 0) if stage else None


def units_ahead(b, g, stage, m):
    steps, u = (1, m + NU // 2) if m < NU // 2 else (2, m - NU // 2)
    if g + steps < G:
        return b, g + steps, u
    return (b + 1, g + steps - G, u) if stage else None


def shape_constants():
    c = np.zeros((P, NCONST), np.float32)
    c[:, IDENT:IDENT + P] = np.eye(P)
    q, k = np.arange(P)[:, None], np.arange(P)[None, :]
    allowed = (k // CHUNK > q // CHUNK) | ((k // CHUNK == q // CHUNK) & (k <= q))
    c[:, MASK:MASK + P] = np.where(allowed, 0.0, MASKED)
    for p in range(NP - 1):
        for col in range(P):
            for half in range(2):
                c[half * E + 2 * p + col // INTER, SEL + p * P + col] = 1.0
    c[:, TRI:TRI + EG * EG] = (np.arange(EG)[None, :] < np.arange(EG)[:, None]).astype(np.float32).reshape(1, -1)
    c[:, REV:REV + E] = E - np.arange(E)
    for j in range(HG):
        c[ROWS + j, ONES + j] = c[ROWS + HG + j, ONES + j] = 1.0
    return c


def block_kernel(nc, x, w_attn, cols, w13, w2, b13, gate_w, rows, be2, const, out):
    ctx = ExitStack()
    with ctx:
        def sb(name, shape, dt=F32):
            return ctx.enter_context(nc.sbuf_tensor(name, shape, dt))

        def sem(name):
            return ctx.enter_context(nc.semaphore(name))

        xall = sb("xall", [P, B * NT, C])
        cst = sb("cst", [P, NCONST])
        ident_bf = sb("ident_bf", [P, P], BF16)
        mask_bf = sb("mask_bf", [P, P], BF16)
        sel = sb("sel", [2 * E, (NP - 1) * P], F32R)
        wa = sb("wa", [P, 4, C])
        wa_hi = sb("wa_hi", [P, 4, C], F32R)
        wa_lo = sb("wa_lo", [P, 4, C], F32R)
        gw = sb("gw", [P, E])
        gw_split = sb("gw_split", [P, 2, E], F32R)
        gw_hi, gw_lo = gw_split[:, 0, :], gw_split[:, 1, :]
        col = sb("col", [P, 6])
        b13c = sb("b13c", [P, 2, NP])
        row = sb("row", [P, C + E])
        be = sb("be", [2 * E, C])
        be_hi = sb("be_hi", [2 * E, C], F32R)
        be_lo = sb("be_lo", [2 * E, C], F32R)
        w13_hi = sb("w13_hi", [P, 2, NP, P], F32R)
        w13_lo = sb("w13_lo", [P, 2, NP, P], F32R)
        w2_hi = sb("w2_hi", [P, NP, C], F32R)
        w2_lo = sb("w2_lo", [P, NP, C], F32R)
        halfneg = sb("halfneg", [P, NT])
        pt = sb("pt", [P, NT, HG, T])
        km = sb("km", [P, G, HG, T], F32R)
        qd = sb("qd", [P, G, T], F32R)
        vaug = sb("vaug", [P, NT, H, VW])
        xn = sb("xn", [P, NT, C])
        xnT_hi = sb("xnT_hi", [P, T], F32R)
        xnT_lo = sb("xnT_lo", [P, T], F32R)
        spare = sb("spare", [P, 2, T])
        qk_split = sb("qk_split", [P, 2, 2, T], F32R)
        vraw = sb("vraw", [P, NT, C])
        negmax = sb("negmax", [P, 2, NT, HG])
        shift = sb("shift", [P, NT, 2 * HG])
        o_raw = sb("o_raw", [P, G, T])
        rsum = sb("rsum", [P, NT, H])
        oT_hi = sb("oT_hi", [P, T], F32R)
        oT_lo = sb("oT_lo", [P, T], F32R)
        bst = sb("bst", [P, 4, NT, 6])
        mv = sb("mv", [P, 4, NT, 2])
        ve = sb("ve", [P, 4, NT])
        rstd = sb("rstd", [P, 4, NT])
        xfT_hi = [sb(f"xfT_hi{i}", [P, T], F32R) for i in range(2)]
        xfT_lo = [sb(f"xfT_lo{i}", [P, T], F32R) for i in range(2)]
        xfT_kept = nc.dram_tensor("xfT_kept", [2, P, B * T], F32, kind="Internal").ap()
        xfs_hi = sb("xfs_hi", [P, T], F32R)
        xfs_lo = sb("xfs_lo", [P, T], F32R)
        lraw = sb("lraw", [P, NT, E])
        lmax = sb("lmax", [P, NT])
        after = sb("after", [P, 5, T])
        on, att, attn_n, xf = (after[:, i, :].rearrange("p (t c) -> p t c", t=NT) for i in range(4))
        gexp = after[:, 4, :].rearrange("p (b t e) -> p b t e", b=B, t=NT)
        w13_raw = after[:, :, :].rearrange("p a b -> p (a b)")[:, 0:2 * NP * P]
        w2_raw = o_raw[:, :, :].rearrange("p a b -> p (a b)")[:, 0:NP * C]
        ptf = pt[:, :, :, :].rearrange("p k h t -> p (k h) t")
        silu = [ptf[:, i, :] for i in range(3)]
        gated = [ptf[:, 3 + i, :] for i in range(3)]
        hbuf = [ptf[:, 6 + i, :] for i in range(3)]
        y_sb = ptf[:, 9, :]
        y_n = ptf[:, 10, :].rearrange("p (t c) -> p t c", t=NT)
        out_sb = ptf[:, 11, :].rearrange("p (t c) -> p t c", t=NT)
        kmf = km[:, :, :, :].rearrange("p g j t -> p (g j) t")
        h_hi = [kmf[:, i, :] for i in range(3)]
        h_lo = [kmf[:, 3 + i, :] for i in range(3)]
        cT = [kmf[0:2 * E, 6 + i, :] for i in range(2)]
        comb = sb("comb", [P, NT, 2 * E])
        comb_all = sb("comb_all", [P, B * NT, E])
        router_tiles = [xn[:, :, :].rearrange("p t c -> p (t c)"), vraw[:, :, :].rearrange("p t c -> p (t c)"),
                        spare[:, 0, :], spare[:, 1, :]]
        router_groups = [wa[:, i, :] for i in range(4)]
        rm = [sb(f"rm{i}", [P, B * NT]) for i in range(4)]

        ps_a = [ctx.enter_context(nc.psum_tensor(f"ps_a{i}", [P, 1024], F32)) for i in range(2)]
        ps_b = [ctx.enter_context(nc.psum_tensor(f"ps_b{i}", [P, 512], F32)) for i in range(2)]
        ps_o = ctx.enter_context(nc.psum_tensor("ps_o", [P, 512], F32))
        ps_m = ctx.enter_context(nc.psum_tensor("ps_m", [P, 512], F32))
        ps_h1 = [ps_a[0][:, 512 * i:512 * i + 512] for i in range(2)]
        ps_h3 = [ps_a[1][:, 512 * i:512 * i + 512] for i in range(2)]
        ps_c = ps_b
        first_banks = [ps_m[:, :], ps_a[0][:, 0:512], ps_a[1][:, 0:512], ps_o[:, :]]
        ps_y = ps_o

        x_first, x_rest = sem("x_first"), sem("x_rest")
        const_in, wattn_in, w_in = sem("const_in"), sem("wattn_in"), sem("w_in")
        attn_weights, small_hi = sem("attn_weights"), sem("small_hi")
        weights_hi, weights_lo = sem("weights_hi"), sem("weights_lo")
        operands_cleared, ones_placed, half_set = sem("operands_cleared"), sem("ones_placed"), sem("half_set")
        scores_ready, maxes_done = sem("scores_ready"), sem("maxes_done")
        shift_hi, shift_split = sem("shift_hi"), sem("shift_split")
        shift_in_psum, shift_placed = sem("shift_in_psum"), sem("shift_placed")
        st_ready, exps_done, masks_done = sem("st_ready"), sem("exps_done"), sem("masks_done")
        pv_done, o_evacuated = sem("pv_done"), sem("o_evacuated")
        misc_ready, misc_evacuated = sem("misc_ready"), sem("misc_evacuated")
        xT_hi, onT_hi, xfT_hi_done = sem("xT_hi"), sem("onT_hi"), sem("xfT_hi_done")
        stats = [sem(f"stats{i}") for i in range(4)]
        moments = [sem(f"moments{i}") for i in range(4)]
        eps_added = [sem(f"eps_added{i}") for i in range(4)]
        rstds = [sem(f"rstds{i}") for i in range(4)]
        xn_ready, attn_normed, x2_ready, xf_ready = sem("xn_ready"), sem("attn_normed"), sem("x2_ready"), sem("xf_ready")
        sums_inverted, logit_max, gate_exp = sem("sums_inverted"), sem("logit_max"), sem("gate_exp")
        logits_shifted = sem("logits_shifted")
        qk_hi_done, v_placed, q_scaled = sem("qk_hi_done"), sem("v_placed"), sem("q_scaled")
        kq_in = [sem(f"kq_in{g}") for g in range(G)]
        h1_ready, h3_ready, silu_done, gated_done, h_done = (
            sem("h1_ready"), sem("h3_ready"), sem("silu_done"), sem("gated_done"), sem("h_done"))
        h_hi_done, h_split, down_done = sem("h_hi_done"), sem("h_split"), sem("down_done")
        y_evacuated, yT_ready, y_normed = sem("y_evacuated"), sem("yT_ready"), sem("y_normed")
        router_step, cT_in_psum, cT_ready = sem("router_step"), sem("cT_in_psum"), sem("cT_ready")
        xf_saved, combine_ready, comb_hi, km_zeroed = sem("xf_saved"), sem("combine_ready"), sem("comb_hi"), sem("km_zeroed")
        xf_in = [sem("xf_in0"), sem("xf_in1")]
        wait_carrier = [sem("wait_carrier_dve"), sem("wait_carrier_pool")]
        out_ready, stored = sem("out_ready"), sem("stored")

        def bank_of(number):
            return first_banks[number] if isinstance(number, int) and number < len(STAGE) else ps_m[:, :]

        block = ctx.enter_context(nc.Block())

        def tile_of(b, t):
            return bass.ds(b * NT + t, 1) if not isinstance(b, int) else slice(b * NT + t, b * NT + t + 1)

        def batch_of(b, width):
            return bass.ds(b * width, width) if not isinstance(b, int) else slice(b * width, (b + 1) * width)

        def third(part):
            if part == 0:
                hi, lo = (w[:, :, :].rearrange("p b c -> p (b c)") for w in (w2_hi, w2_lo))
                return hi, lo, w2_raw
            hi, lo = (w[:, part - 1, :, :].rearrange("p b c -> p (b c)") for w in (w13_hi, w13_lo))
            return hi, lo, w13_raw[:, NP * P * (part - 1):NP * P * part]

        x_dram = x.rearrange("(n p) c -> p n c", p=P)
        out_dram = out.rearrange("(n p) c -> p n c", p=P)

        @block.sync
        def _(sp):
            sp.sem_inc(xf_saved, 1)
            sp.sem_inc(stored, 1)
            sp.dma_start(xall[:, 0:NT, :], x_dram[:, 0:NT, :]).then_inc(x_first, 16)
            sp.dma_start(col[:, 0:5], cols).then_inc(wattn_in, 16)
            sp.dma_start(wa[:, :, :], w_attn).then_inc(wattn_in, 16)
            sp.dma_start(cst[:, :], const).then_inc(const_in, 16)
            sp.dma_start(row[:, :], rows).then_inc(const_in, 16)
            sp.dma_start(gw[:, :], gate_w).then_inc(const_in, 16)
            sp.dma_start(be[:, :], be2).then_inc(const_in, 16)
            sp.dma_start(b13c[:, :, :], b13).then_inc(const_in, 16)
            sp.dma_start(xall[:, NT:, :], x_dram[:, NT:, :]).then_inc(x_rest, 16)
            sp.dma_start(w2_raw, w2).then_inc(w_in, 16)
            sp.dma_start(w13_raw, w13).then_inc(w_in, 16)

            def place_group(s, g):
                if isinstance(s, int) and s == 0:
                    sp.wait_ge(misc_evacuated, use_number(None, "q") + 1)
                else:
                    if g == 0:
                        sp.wait_ge(misc_evacuated, use_number(0 if isinstance(s, int) else s - 1, "k") + 1)
                    sp.wait_ge(st_ready, s * (G * NV) + (NV * (g + 1) - G * NV))
                rows_of = HG * D
                sp.dma_start(qd[0:2 * rows_of, g, :].bitcast(F32),
                             qk_split[rows_of * g:rows_of * (g + 1), 0, :, :].bitcast(F32)).then_inc(kq_in[g], 16)
                sp.dma_start(qd[2 * rows_of:ROWS, g, :].bitcast(F32),
                             qk_split[rows_of * g:rows_of * (g + 1), 0, 0, :].bitcast(F32)).then_inc(kq_in[g], 16)
                if isinstance(s, int) and s == 0:
                    sp.wait_ge(misc_evacuated, use_number(None, "k") + 1)
                    sp.wait_ge(operands_cleared, g + 1)
                for j in range(HG):
                    own = slice(rows_of * g + D * j, rows_of * g + D * (j + 1))
                    sp.dma_start(km[2 * D * j:2 * D * (j + 1), g, j, :].bitcast(F32),
                                 qk_split[own, 1, 0, :].bitcast(F32).unsqueeze(1).broadcast_to([D, 2, T])
                                 ).then_inc(kq_in[g], 16)
                    sp.dma_start(km[2 * rows_of + D * j:2 * rows_of + D * (j + 1), g, j, :].bitcast(F32),
                                 qk_split[own, 1, 1, :].bitcast(F32)).then_inc(kq_in[g], 16)

            for g in range(G):
                place_group(0, g)

            def save_xf(b, number):
                sp.wait_ge(misc_evacuated, number + 1)
                sp.dma_start(xfT_kept[0, :, batch_of(b, T)], xfs_hi[:, :].bitcast(F32)).then_inc(xf_saved, 16)
                sp.dma_start(xfT_kept[1, :, batch_of(b, T)], xfs_lo[:, :].bitcast(F32)).then_inc(xf_saved, 16)

            def load_xf(b, parity):
                if not (isinstance(b, int) and b < 2):
                    sp.wait_ge(h3_ready, (b - 1) * NP)
                sp.dma_start(xfT_hi[parity][:, :].bitcast(F32), xfT_kept[0, :, batch_of(b, T)]).then_inc(xf_in[parity], 16)
                sp.dma_start(xfT_lo[parity][:, :].bitcast(F32), xfT_kept[1, :, batch_of(b, T)]).then_inc(xf_in[parity], 16)

            def store_out(b):
                sp.wait_ge(out_ready, b + 1)
                sp.dma_start(out_dram[:, batch_of(b, NT), :], out_sb).then_inc(stored, 16)

            for g in range(G):
                place_group(1, g)
            with sp.Fori(1, B - 1) as b:
                for g in range(G):
                    place_group(b + 1, g)
                save_xf(b - 1, use_number(b, "xfT"))
            sp.wait_ge(xf_saved, 32 * (B - 2) + 1)
            load_xf(0, 0)
            load_xf(1, 1)
            save_xf(B - 2, use_number(LAST, "xfT"))
            load_xf(2, 0)
            save_xf(LAST, use_number(B, "xfT"))
            sp.wait_ge(xf_saved, 32 * B + 1)
            with sp.Fori(0, B // 2 - 2) as i:
                store_out(i * 2)
                load_xf(i * 2 + 3, 1)
                store_out(i * 2 + 1)
                load_xf(i * 2 + 4, 0)
            store_out(B - 4)
            load_xf(B - 1, 1)
            for b in range(B - 3, B):
                store_out(b)
            sp.wait_ge(stored, 16 * B + 1)

        @block.tensor
        def _(pe):
            ident = cst[:, IDENT:IDENT + P]

            def claim_misc(number):
                if isinstance(number, int) and number < len(STAGE):
                    return first_banks[number]
                pe.wait_ge(misc_evacuated, number)
                return ps_m[:, :]

            def three_pass(dst, lhs_hi, lhs_lo, rhs_hi, rhs_lo, start=True, stop=True):
                nc.tensor.matmul(dst, lhs_hi, rhs_hi, start=start, stop=False)
                nc.tensor.matmul(dst, lhs_hi, rhs_lo, start=False, stop=False)
                return nc.tensor.matmul(dst, lhs_lo, rhs_hi, start=False, stop=stop)

            def transpose_tiles(number, src):
                claim_misc(number)
                for t in range(NT):
                    last = nc.tensor.transpose(ps_m[:, P * t:P * t + P], src[:, t, :], ident)
                last.then_inc(misc_ready, 1)

            def project_T(number, which):
                bank = claim_misc(number)
                three_pass(bank, wa_hi[:, which, :], wa_lo[:, which, :], xnT_hi[:, :], xnT_lo[:, :]
                           ).then_inc(misc_ready, 1)

            def project_tokens(number, which, src_hi, src_lo):
                bank = claim_misc(number)
                for t in range(NT):
                    s = slice(P * t, P * t + P)
                    last = three_pass(bank[:, s], src_hi[:, s], src_lo[:, s], wa_hi[:, which, :], wa_lo[:, which, :])
                last.then_inc(misc_ready, 1)

            def scores(b, g, u):
                t, heads = MAX_UNITS[u]
                n6 = b * (G * NU) + (g * NU + u)
                if not (isinstance(b, int) and b == 0 and g == 0 and u < 2):
                    pe.wait_ge(maxes_done, n6 - 1)
                if u == 0:
                    pe.wait_ge(kq_in[g], b * (16 * GROUP_DMAS) + 16 * GROUP_DMAS)
                width = T - P * t
                pitch = 512 if width > 256 else width
                a = ps_a[u % 2]
                per_bank = T // pitch
                heads_of = [heads[i:i + per_bank] for i in range(0, len(heads), per_bank)]
                banks = [a[:, T * i:T * i + len(js) * pitch].rearrange("p (j k) -> p j k", k=pitch)
                         for i, js in enumerate(heads_of)]
                for bank, js in zip(banks, heads_of):
                    nc.tensor.matmul(bank[:, :, 0:width], qd[0:ROWS, g, P * t:P * t + P],
                                     km[0:ROWS, g, js[0]:js[-1] + 1, P * t:T], start=True, stop=False)
                for bank, js in zip(banks, heads_of):
                    last = nc.tensor.matmul(bank[:, :, 0:P], ident_bf[:, :],
                                            mask_bf[:, :].unsqueeze(1).broadcast_to([P, len(js), P]),
                                            start=False, stop=True)
                last.then_inc(scores_ready, 1)

            def shift_rows(b, g):
                n = b * G + g
                pe.wait_ge(shift_split, n + 1)
                if not (isinstance(n, int) and n == 0):
                    pe.wait_ge(exps_done, n * NV + (SHIFT_PLACE - 1 - NV))
                for t in range(NT):
                    last = nc.tensor.transpose(ps_b[0][0:2 * HG, P * t:P * t + P], shift[:, t, :], ident)
                last.then_inc(shift_in_psum, 1)

            def scores_T(b, g, v):
                k, heads = EXP_UNITS[v]
                n = b * G + g
                if v == 0:
                    pe.wait_ge(shift_placed, n + 1)
                if v == SHIFT_PLACE + 1 and not (isinstance(n, int) and n == B * G - 1):
                    pe.wait_ge(shift_placed, n + 2)
                elif not (isinstance(n, int) and n == 0 and v < 2):
                    pe.wait_ge(exps_done, n * NV + (v if v == SHIFT_PLACE else v - 1))
                width = P * (k + 1)
                bank = ps_b[exp_bank(v)]
                for i, j in enumerate(heads):
                    last = nc.tensor.matmul(bank[:, i * width:i * width + width],
                                            km[0:ROWS_SHIFTED, g, j, P * k:P * k + P],
                                            qd[0:ROWS_SHIFTED, g, 0:width], start=True, stop=True)
                last.then_inc(st_ready, 1)

            def values(b, g, k):
                n = b * G + g
                if k == NT - 1:
                    pe.wait_ge(v_placed, n + 1)
                    if not (isinstance(n, int) and n == 0):
                        pe.wait_ge(o_evacuated, n)
                pe.wait_ge(masks_done, n * 6 + (3 if k >= 2 else 6))
                width = P * (k + 1)
                for j in range(HG):
                    last = nc.tensor.matmul(ps_o[32 * j:32 * j + VW, 0:width], vaug[:, k, HG * g + j, :],
                                            pt[:, k, j, T - width:T], start=k == NT - 1, stop=k == 0)
                last.then_inc(pv_done, 1)

            def o_transposes(b, t, number):
                if t == 0:
                    pe.wait_ge(o_evacuated, b * G + G)
                claim_misc(number)
                for g in range(G):
                    last = nc.tensor.transpose(ps_m[:, P * g:P * g + P], o_raw[:, g, P * t:P * t + P], ident)
                last.then_inc(misc_ready, 1)

            def logits(b, number):
                claim_misc(number)
                for t in range(NT):
                    hi, lo = xfs_hi[:, P * t:P * t + P], xfs_lo[:, P * t:P * t + P]
                    nc.tensor.matmul(ps_m[:, 2 * E * t:2 * E * (t + 1)], hi,
                                     gw_split[:, :, :].rearrange("p a e -> p (a e)"), start=True, stop=False)
                    last = nc.tensor.matmul(ps_m[:, 2 * E * t:2 * E * t + E], lo, gw_hi, start=False, stop=True)
                last.then_inc(misc_ready, 1)

            def iteration(b, tail, stage):
                def use(name):
                    return use_number(b, name)

                for g in range(G):
                    ahead = [units_ahead(b, g, stage, m) for m in range(NU)]
                    before = (b, g - 1) if g else (b - 1, G - 1)
                    has_before = tail or g > 0

                    def scores_ahead(m):
                        if ahead[m]:
                            scores(*ahead[m])

                    scores_ahead(0)
                    if has_before:
                        values(*before, 3)
                    scores_T(b, g, 0)
                    if g == 0 and stage:
                        pe.wait_ge(xn_ready, b + 2)
                        transpose_tiles(use("xT"), xn)
                    if g == 1 and tail:
                        o_transposes(b - 1, 2, use("otr2"))
                    if g == 2 and tail:
                        project_tokens(use("oproj"), 3, oT_hi, oT_lo)
                    scores_T(b, g, 1)
                    scores_ahead(1)
                    if g == 1 and stage:
                        project_T(use("q"), 0)
                    scores_T(b, g, 2)
                    if has_before:
                        values(*before, 2)
                    scores_T(b, g, 3)
                    scores_ahead(2)
                    if g == 1 and tail:
                        o_transposes(b - 1, 3, use("otr3"))
                    scores_T(b, g, 4)
                    if has_before:
                        values(*before, 1)
                    scores_T(b, g, 5)
                    scores_ahead(3)
                    if g == 1 and stage:
                        project_T(use("k"), 1)
                    scores_T(b, g, 6)
                    scores_ahead(4)
                    scores_T(b, g, 7)
                    if has_before:
                        values(*before, 0)
                    if follower(b, g, stage):
                        shift_rows(*follower(b, g, stage))
                    if g == 3 and tail:
                        pe.wait_ge(xf_ready, b)
                        transpose_tiles(use("xfT"), xf)
                    scores_T(b, g, 8)
                    if g == 0 and tail:
                        o_transposes(b - 1, 0, use("otr0"))
                    if g == 1 and tail:
                        transpose_tiles(use("onT"), on)
                    if g == 2 and stage:
                        project_tokens(use("v"), 2, xnT_hi, xnT_lo)
                    scores_ahead(5)
                    scores_T(b, g, 9)
                    if g == 0 and tail:
                        o_transposes(b - 1, 1, use("otr1"))
                    scores_T(b, g, 10)
                    if g == 3 and tail and stage:
                        logits(b - 1, use("logits"))

            pe.wait_ge(const_in, 80)
            pe.wait_ge(xn_ready, 1)
            transpose_tiles(use_number(None, "xT"), xn)
            pe.wait_ge(attn_weights, 2)
            pe.wait_ge(misc_evacuated, 1)
            project_T(use_number(None, "q"), 0)
            project_T(use_number(None, "k"), 1)
            project_tokens(use_number(None, "v"), 2, xnT_hi, xnT_lo)
            pe.wait_ge(small_hi, 3)
            pe.wait_ge(misc_evacuated, len(STAGE))
            for u in range(NU):
                scores(0, 0, u)
            for u in range(NU // 2):
                scores(0, 1, u)
            shift_rows(0, 0)
            iteration(0, tail=False, stage=True)
            with pe.Fori(1, B - 1) as b:
                iteration(b, tail=True, stage=True)
            iteration(B - 1, tail=True, stage=False)
            def unit(b, p, par, down_prev):
                q = b * NP + p
                odd = (par + p) % 2
                if p == 0:
                    pe.wait_ge(xf_in[odd], 32 * (b // 2) + 32 if isinstance(b, int) else (b - odd) * 16 + 32)
                xs_hi, xs_lo = xfT_hi[odd][:, :], xfT_lo[odd][:, :]
                early = isinstance(q, int) and q < 2
                if not early:
                    pe.wait_ge(silu_done, q - 1)
                three_pass(ps_h1[par], w13_hi[:, 0, p, :], w13_lo[:, 0, p, :], xs_hi, xs_lo
                           ).then_inc(h1_ready, 1)
                if not early:
                    pe.wait_ge(h_done, q - 1)
                last = three_pass(ps_h3[par], w13_hi[:, 1, p, :], w13_lo[:, 1, p, :], xs_hi, xs_lo)
                if p >= 1:
                    if p == 1:
                        pe.wait_ge(cT_ready, b + 1)
                    last = nc.tensor.matmul(ps_c[par][:, :], sel[:, P * (p - 1):P * p], cT[b_parity(b, par, p)],
                                            start=True, stop=True)
                last.then_inc(h3_ready, 1)
                if down_prev:
                    down(b if p >= 2 else b - 1, (p - 2) % NP, par)

            def b_parity(b, par, p):
                return (par + p) % 2

            def down(b, p, par):
                q = b * NP + p
                if p == 0 and not (isinstance(b, int) and b == 0):
                    pe.wait_ge(y_evacuated, b)
                pe.wait_ge(h_split, q + 1)
                if p == 1:
                    c = cT[b_parity(b, par, p)]
                    nc.tensor.matmul(ps_y[:, :], be_hi[:, :], c, start=False, stop=False)
                    nc.tensor.matmul(ps_y[:, :], be_lo[:, :], c, start=False, stop=False)
                last = three_pass(ps_y[:, :], w2_hi[:, p, :], w2_lo[:, p, :], h_hi[p % 3], h_lo[p % 3],
                                  start=p == 0, stop=p == NP - 1)
                last.then_inc(down_done, 1)

            def y_transposes(b):
                pe.wait_ge(y_evacuated, b + 1)
                pe.wait_ge(cT_ready, min(b + 3, B) if isinstance(b, int) else b + 3)
                for t in range(NT):
                    last = nc.tensor.transpose(ps_m[:, P * t:P * t + P], y_sb[:, P * t:P * t + P], ident)
                last.then_inc(yT_ready, 1)

            def c_transposes(b):
                pe.wait_ge(combine_ready, b + 1)
                for t in range(NT):
                    last = nc.tensor.transpose(ps_m[0:2 * E, P * t:P * t + P], comb[:, t, :], ident)
                last.then_inc(cT_in_psum, 1)

            def rest_of_last(b, p):
                if (b, p) in ((0, 0), (0, 1), (0, 3), (0, 4)):
                    t = ((0, 0), (0, 1), (0, 3), (0, 4)).index((b, p))
                    pe.wait_ge(cT_ready, 1 if t < 2 else 2)
                    o_transposes(LAST, t, use_number(B, f"otr{t}"))
                if (b, p) == (0, 6):
                    transpose_tiles(use_number(B, "onT"), on)
                if (b, p) == (0, 8):
                    project_tokens(use_number(B, "oproj"), 3, oT_hi, oT_lo)
                if (b, p) == (1, 7):
                    pe.wait_ge(y_normed, 1)
                    pe.wait_ge(xf_ready, B)
                    transpose_tiles(use_number(B, "xfT"), xf)
                if (b, p) == (1, 8):
                    logits(LAST, use_number(B, "logits"))

            def last_misc_before_c(b):
                return {0: use_number(LAST, "logits"), 1: use_number(B, "otr1"), 2: use_number(B, "oproj"),
                        3: use_number(B, "logits")}[b]

            def expert_batch(b, parity):
                for p in range(NP):
                    unit(b, p, (parity + p) % 2, not (isinstance(b, int) and b == 0) or p >= 2)
                    if isinstance(b, int) and b == 0 and p == 0:
                        for k in (3, 2, 1, 0):
                            values(LAST, G - 1, k)
                        logits(LAST - 1, use_number(LAST, "logits"))
                        claim_misc(last_misc_before_c(0) + 1)
                        c_transposes(0)
                        pe.wait_ge(exps_done, B * G * NV)
                        pe.wait_ge(o_evacuated, B * G)
                    if isinstance(b, int) and b < 3:
                        rest_of_last(b, p)
                    if p == 2 and not (isinstance(b, int) and b == LAST):
                        if isinstance(b, int):
                            claim_misc(last_misc_before_c(b + 1) + 1)
                        else:
                            pe.wait_ge(y_normed, b - 1)
                        c_transposes(b + 1)
                    if p == 3 and not (isinstance(b, int) and b == 0):
                        y_transposes(b - 1)

            pe.wait_ge(maxes_done, B * G * NU)
            pe.wait_ge(weights_lo, 5)
            for b in range(3):
                expert_batch(b, b % 2)
            with pe.Fori(0, (B - 4) // 2) as i:
                expert_batch(i * 2 + 3, 1)
                expert_batch(i * 2 + 4, 0)
            expert_batch(LAST, 1)
            down(B - 1, NP - 2, (B - 1 + NP - 2) % 2)
            down(B - 1, NP - 1, (B - 1 + NP - 1) % 2)
            y_transposes(B - 1)

        @block.scalar
        def _(act):
            def split_hi(number, dst, bias, done):
                act.wait_ge(misc_ready, number + 1)
                nc.scalar.activation(dst, ps_m[:, :], ACT.Identity, bias=bias).then_inc(done, 1)

            def read_qk(s, number, which):
                if which == 0 and not (isinstance(s, int) and s == 0):
                    for g in range(G):
                        act.wait_ge(kq_in[g], s * (16 * GROUP_DMAS))
                act.wait_ge(misc_ready, number + 1)
                bias = col[:, 5:6] if which == 0 else col[:, 1:2]
                nc.scalar.activation(qk_split[:, which, 0, :], bank_of(number), ACT.Identity, bias=bias
                                     ).then_inc(qk_hi_done, 1)

            def read_v(s, number):
                if not (isinstance(s, int) and s == 0):
                    act.wait_ge(v_placed, s * G)
                act.wait_ge(misc_ready, number + 1)
                nc.scalar.activation(vraw[:, :, :].rearrange("p t c -> p (t c)"), bank_of(number), ACT.Identity
                                     ).then_inc(misc_evacuated, 1)

            def place_shift(b, g):
                act.wait_ge(shift_in_psum, b * G + (g + 1))
                nc.scalar.activation(qd[ROWS:ROWS_SHIFTED, g, :], ps_b[0][0:2 * HG, :], ACT.Identity
                                     ).then_inc(shift_placed, 1)

            def exponentials(b, g, v):
                k, heads = EXP_UNITS[v]
                n = b * G + g
                if v in (0, 4, 8, 10) and not (isinstance(n, int) and n == 0):
                    act.wait_ge(pv_done, n * NT - k)
                act.wait_ge(st_ready, n * NV + (v + 1))
                width = P * (k + 1)
                src = ps_b[exp_bank(v)][:, 0:len(heads) * width].rearrange("p (h q) -> p h q", q=width)
                nc.scalar.activation(pt[:, k, heads[0]:heads[0] + len(heads), T - width:T], src, ACT.Exp
                                     ).then_inc(exps_done, 1)

            def evacuate_o(b, g):
                act.wait_ge(pv_done, (b * G + g) * NT + NT)
                nc.scalar.activation(o_raw[:, g, :], ps_o[:, :], ACT.Identity).then_inc(o_evacuated, 1)

            def gate_exponentials(first, after_last):
                act.wait_ge(logits_shifted, after_last)
                ge = gexp[:, first:after_last, :, :].rearrange("p b t e -> p (b t e)")
                nc.scalar.activation(ge, ge, ACT.Exp).then_inc(gate_exp, 1)

            def split_experts(part):
                if part == 0:
                    act.wait_ge(w_in, 32)
                    for dst, src in ((gw_hi, gw[:, :]), (be_hi[:, :], be[:, :])):
                        nc.scalar.activation(dst, src, ACT.Identity).then_inc(weights_hi, 1)
                    nc.scalar.activation(sel[:, :], cst[0:2 * E, SEL:TRI], ACT.Identity).then_inc(weights_hi, 1)
                dst, _, src = third(part)
                nc.scalar.activation(dst, src, ACT.Identity).then_inc(weights_hi, 1)

            def iteration(b, tail, stage):
                def use(name):
                    return use_number(b, name)

                for g in range(G):
                    before = (b, g - 1) if g else (b - 1, G - 1)
                    for v in range(NV):
                        exponentials(b, g, v)
                        if v == SHIFT_PLACE - 1 and g == 1 and not tail:
                            act.wait_ge(weights_lo, 3)
                        if v == SHIFT_PLACE - 1 and (tail or g):
                            if tail and g == 1:
                                act.wait_ge(misc_ready, use("otr3") + 1)
                            evacuate_o(*before)
                        if v == SHIFT_PLACE - 1 and follower(b, g, stage):
                            place_shift(*follower(b, g, stage))
                        if v == 2 and g == 0 and not stage:
                            gate_exponentials(0, ROUTED_EARLY)
                        if v == 0 and g == 0 and stage:
                            split_hi(use("xT"), xnT_hi[:, :], 0.0, xT_hi)
                        if v == 1 and g == 1 and stage:
                            read_qk(b + 1, use("q"), 0)
                        if v == 5 and g == 1 and stage:
                            read_qk(b + 1, use("k"), 1)
                        if v == 8 and g == 1 and tail:
                            split_hi(use("onT"), oT_hi[:, :], col[:, 2:3], onT_hi)
                        if v == 8 and g == 2 and stage:
                            read_v(b + 1, use("v"))
                        if v == 7 and g == 3 and tail:
                            act.wait_ge(xf_saved, (b - 1) * 32 + 1)
                            split_hi(use("xfT"), xfs_hi[:, :], 0.0, xfT_hi_done)
                        if v == 5 and g < 3 and not tail:
                            split_experts(g)

            act.wait_ge(wattn_in, 32)
            nc.scalar.activation(wa[:, 0, :], wa[:, 0, :], ACT.Identity, scale=col[:, 4:5]).then_inc(q_scaled, 1)
            act.wait_ge(q_scaled, 1)
            nc.scalar.activation(wa_hi[:, :, :], wa[:, :, :], ACT.Identity).then_inc(attn_weights, 1)
            act.wait_ge(const_in, 80)
            nc.scalar.activation(ident_bf[:, :], cst[:, IDENT:IDENT + P], ACT.Identity).then_inc(small_hi, 1)
            nc.scalar.activation(mask_bf[:, :], cst[:, MASK:MASK + P], ACT.Identity).then_inc(small_hi, 1)
            nc.scalar.activation(col[:, 5:6], col[:, 0:1], ACT.Identity, scale=col[:, 4:5]).then_inc(small_hi, 1)
            split_hi(use_number(None, "xT"), xnT_hi[:, :], 0.0, xT_hi)
            act.wait_ge(small_hi, 3)
            read_qk(0, use_number(None, "q"), 0)
            read_qk(0, use_number(None, "k"), 1)
            act.wait_ge(misc_evacuated, use_number(None, "k") + 1)
            read_v(0, use_number(None, "v"))
            place_shift(0, 0)
            iteration(0, tail=False, stage=True)
            with act.Fori(1, B - 1) as b:
                iteration(b, tail=True, stage=True)
            iteration(B - 1, tail=True, stage=False)
            def silu_tile(b, p, par):
                q = b * NP + p
                act.wait_ge(h1_ready, q + 1)
                if not (isinstance(q, int) and q < 3):
                    act.wait_ge(h_done, q - 2)
                nc.scalar.activation(silu[p % 3], ps_h1[par], ACT.Silu, bias=b13c[:, 0, p:p + 1]).then_inc(silu_done, 1)

            def hidden_hi(b, p):
                q = b * NP + p
                act.wait_ge(h_done, q + 1)
                if not (isinstance(q, int) and q < 3):
                    act.wait_ge(down_done, q - 2)
                nc.scalar.activation(h_hi[p % 3], hbuf[p % 3], ACT.Identity).then_inc(h_hi_done, 1)

            def evacuate_y(b):
                act.wait_ge(down_done, b * NP + NP)
                nc.scalar.activation(y_sb, ps_y[:, :], ACT.Identity, bias=col[:, 3:4]).then_inc(y_evacuated, 1)

            def evacuate_c(b, parity):
                if not (isinstance(b, int) and b < 2):
                    act.wait_ge(down_done, (b - 1) * NP)
                act.wait_ge(cT_in_psum, b + 1)
                nc.scalar.activation(cT[parity], ps_m[0:2 * E, :], ACT.Identity).then_inc(cT_ready, 1)

            def rest_of_last(b, p):
                if (b, p) == (0, 7):
                    split_hi(use_number(B, "onT"), oT_hi[:, :], col[:, 2:3], onT_hi)
                if (b, p) == (1, 8):
                    act.wait_ge(xf_saved, LAST * 32 + 1)
                    split_hi(use_number(B, "xfT"), xfs_hi[:, :], 0.0, xfT_hi_done)
                if (b, p) == (2, 1):
                    gate_exponentials(ROUTED_EARLY, B)

            def expert_batch(b, parity):
                for p in range(NP):
                    if isinstance(b, int) and b < 3:
                        rest_of_last(b, p)
                    if p == 2 and not (isinstance(b, int) and b == 0):
                        evacuate_y(b - 1)
                    if p == 3 and not (isinstance(b, int) and b == LAST):
                        evacuate_c(b + 1, 1 - parity)
                    silu_tile(b, p, (parity + p) % 2)
                    if not (isinstance(b, int) and b == 0) or p >= 1:
                        hidden_hi(b if p else b - 1, (p - 1) % NP)

            act.wait_ge(pv_done, B * G * NT)
            act.wait_ge(st_ready, B * G * NV)
            evacuate_o(LAST, G - 1)
            evacuate_c(0, 0)
            for b in range(3):
                expert_batch(b, b % 2)
            with act.Fori(0, (B - 4) // 2) as i:
                expert_batch(i * 2 + 3, 1)
                expert_batch(i * 2 + 4, 0)
            expert_batch(LAST, 1)
            hidden_hi(B - 1, NP - 1)
            evacuate_y(B - 1)

        @block.vector
        def _(dve):
            def norm_stats(i, count, tiles):
                for t in range(NT):
                    nc.vector.bn_stats(bst[:, i, t, :], tiles(t)).then_inc(stats[i], 1)
                dve.wait_ge(stats[i], count * NT + NT)
                dve.sem_inc(wait_carrier[0], 1)
                for t in range(NT):
                    last = nc.vector.bn_aggr(mv[:, i, t, :], bst[:, i, t, :])
                last.then_inc(moments[i], 1)

            def normalise(i, count, tiles, dst, done):
                dve.wait_ge(rstds[i], count + 1)
                for t in range(NT):
                    last = nc.vector.tensor_scalar(dst[:, t, :], tiles(t), mv[:, i, t, 0:1], rstd[:, i, t:t + 1],
                                                   ALU.subtract, ALU.mult)
                last.then_inc(done, 1)

            def x_tile(b):
                return lambda t: xall[:, tile_of(b, t), :].rearrange("p a c -> p (a c)")

            def tile_in(buf):
                return lambda t: buf[:, t, :]

            def split_lo(dst, hi, hi_done, count, bias=0.0):
                dve.wait_ge(hi_done, count + 1)
                nc.vector.scalar_tensor_tensor(dst, ps_m[:, :], bias, hi.bitcast(F32), ALU.add, ALU.subtract
                                               ).then_inc(misc_evacuated, 1)

            def split_qk_lo(s, number, which):
                dve.wait_ge(qk_hi_done, s * 2 + (which + 1))
                bias = col[:, 5:6] if which == 0 else col[:, 1:2]
                nc.vector.scalar_tensor_tensor(qk_split[:, which, 1, :], bank_of(number), bias,
                                               qk_split[:, which, 0, :].bitcast(F32), ALU.add, ALU.subtract
                                               ).then_inc(misc_evacuated, 1)

            def maxima(b, g, u):
                t, heads = MAX_UNITS[u]
                n = b * G + g
                if u == 0 and not (isinstance(n, int) and n < 2):
                    dve.wait_ge(shift_split, n - 1)
                dve.wait_ge(scores_ready, n * NU + (u + 1))
                width = T - P * t
                pitch = 512 if width > 256 else width
                src = ps_a[u % 2][:, 0:len(heads) * pitch].rearrange("p (h k) -> p h k", k=pitch)[:, :, 0:width]
                nc.vector.tensor_reduce(negmax[:, g % 2, t, heads[0]:heads[0] + len(heads)], src, AX.X, ALU.max,
                                        negate=True).then_inc(maxes_done, 1)

            def normalise_o(b, t, number):
                dve.wait_ge(misc_ready, number + 1)
                heads = ps_m[:, :].rearrange("p (h w) -> p h w", w=VW)
                nc.vector.reciprocal(rsum[:, t, :], heads[:, :, D]).then_inc(sums_inverted, 1)
                dve.wait_ge(sums_inverted, b * NT + (t + 1))
                nc.vector.tensor_tensor(on[:, t, :].rearrange("p (h d) -> p h d", d=D), heads[:, :, 0:D],
                                        rsum[:, t, :].unsqueeze(2).broadcast_to([P, H, D]), ALU.mult
                                        ).then_inc(misc_evacuated, 1)

            def add_bo(number):
                dve.wait_ge(misc_ready, number + 1)
                nc.vector.tensor_tensor(att[:, :, :], ps_m[:, :].rearrange("p (t c) -> p t c", t=NT),
                                        row[:, 0:C].unsqueeze(1).broadcast_to([P, NT, C]), ALU.add
                                        ).then_inc(misc_evacuated, 1)

            def shift_logits(b, number):
                dve.wait_ge(misc_ready, number + 1)
                halves = ps_m[:, 0:NT * 2 * E].rearrange("p (t a e) -> p t a e", a=2, e=E)
                nc.vector.tensor_reduce(lraw[:, :, :], halves.rearrange("p t a e -> p t e a"), AX.X, ALU.add
                                        ).then_inc(misc_evacuated, 1)
                dve.wait_ge(misc_evacuated, number + 1)
                nc.vector.tensor_reduce(lmax[:, :], lraw[:, :, :], AX.X, ALU.max).then_inc(logit_max, 1)
                dve.wait_ge(logit_max, b + 1)
                nc.vector.tensor_tensor(gexp[:, batch_of(b, 1), :, :].rearrange("p a t e -> p (a t) e"),
                                        lraw[:, :, :], lmax[:, :].unsqueeze(2).broadcast_to([P, NT, E]),
                                        ALU.subtract).then_inc(logits_shifted, 1)

            def split_experts(part):
                dve.wait_ge(weights_hi, 4 + part)
                if part == 0:
                    for dst, src, hi in ((gw_lo, gw[:, :], gw_hi), (be_lo[:, :], be[:, :], be_hi[:, :])):
                        nc.vector.tensor_tensor(dst, src, hi.bitcast(F32), ALU.subtract
                                                ).then_inc(weights_lo, 1)
                hi, lo, src = third(part)
                nc.vector.tensor_tensor(lo, src, hi.bitcast(F32), ALU.subtract).then_inc(weights_lo, 1)

            steps = [0]

            def step(instruction):
                steps[0] += 1
                instruction.then_inc(router_step, 1)
                dve.wait_ge(router_step, steps[0])

            def tt(dst, a, b, op):
                step(nc.vector.tensor_tensor(dst, a, b, op))

            def route(part, first, after_last):
                n = (after_last - first) * NT
                tiles = slice(first * NT, after_last * NT)
                orig = comb_all[:, tiles, :]
                s, pairs, a, b_ = (r[:, 0:n * E].rearrange("p (t e) -> p t e", e=E) for r in router_tiles)
                hi2 = pairs[:, :, 0:2 * EG].rearrange("p t (g k) -> p t g k", k=2)
                lo2 = pairs[:, :, 2 * EG:4 * EG].rearrange("p t (g k) -> p t g k", k=2)
                top, mn, ml, gs = (r[:, 0:n * EG].rearrange("p (t g) -> p t g", g=EG) for r in router_groups)
                total, inv, largest, weight = (r[:, 0:n] for r in rm)
                s4 = s.rearrange("p t (g k) -> p t g k", k=E // EG)
                rev = cst[:, REV:REV + E].unsqueeze(1).broadcast_to([P, n, E])

                def per_tile(v):
                    return v.unsqueeze(2).broadcast_to([P, n, E])

                def first_largest(one_hot):
                    step(nc.vector.tensor_reduce(largest, s, AX.X, ALU.max))
                    tt(pairs, s, per_tile(largest), ALU.is_equal)
                    tt(pairs, pairs, rev, ALU.mult)
                    step(nc.vector.tensor_reduce(weight, pairs, AX.X, ALU.max))
                    tt(one_hot, pairs, per_tile(weight), ALU.is_equal)

                if part == "softmax":
                    dve.wait_ge(gate_exp, 1 if first == 0 else 2)
                    ge = gexp[:, first:after_last, :, :].rearrange("p b t e -> p (b t) e")
                    step(nc.vector.tensor_reduce(total, ge, AX.X, ALU.add))
                    step(nc.vector.reciprocal(inv, total))
                    tt(orig, ge, per_tile(inv), ALU.mult)
                    tt(s, orig, row[:, C:C + E].unsqueeze(1).broadcast_to([P, n, E]), ALU.add)
                if part == "pairs":
                    quad = s.rearrange("p t (g k a) -> p t g k a", k=2, a=2)
                    for k in range(2):
                        tt(hi2[:, :, :, k], quad[:, :, :, k, 0], quad[:, :, :, k, 1], ALU.max)
                        tt(lo2[:, :, :, k], quad[:, :, :, k, 0], quad[:, :, :, k, 1], ALU.min)
                if part == "group sums":
                    tt(top, hi2[:, :, :, 0], hi2[:, :, :, 1], ALU.max)
                    tt(mn, hi2[:, :, :, 0], hi2[:, :, :, 1], ALU.min)
                    tt(ml, lo2[:, :, :, 0], lo2[:, :, :, 1], ALU.max)
                    tt(mn, mn, ml, ALU.max)
                    tt(gs, top, mn, ALU.add)
                if part == "ranks":
                    other = gs.unsqueeze(2).broadcast_to([P, n, EG, EG])
                    own = gs.unsqueeze(3).broadcast_to([P, n, EG, EG])
                    gt = a.rearrange("p t (g h) -> p t g h", h=EG)
                    eq = b_.rearrange("p t (g h) -> p t g h", h=EG)
                    tt(gt, other, own, ALU.is_gt)
                    tt(eq, other, own, ALU.is_equal)
                    tt(b_, b_, cst[:, TRI:TRI + EG * EG].unsqueeze(1).broadcast_to([P, n, EG * EG]), ALU.mult)
                    tt(a, a, b_, ALU.add)
                    step(nc.vector.tensor_reduce(top, gt, AX.X, ALU.add))
                if part == "group mask":
                    step(nc.vector.tensor_scalar(mn, top, 2.0, None, ALU.is_lt))
                    step(nc.vector.tensor_scalar(ml, mn, BIG, BIG, ALU.mult, ALU.subtract))
                    tt(s4, s4, mn.unsqueeze(3).broadcast_to([P, n, EG, E // EG]), ALU.mult)
                    tt(s4, s4, ml.unsqueeze(3).broadcast_to([P, n, EG, E // EG]), ALU.add)
                if part == "first":
                    first_largest(a)
                if part == "second":
                    step(nc.vector.scalar_tensor_tensor(s, a, -BIG, s, ALU.mult, ALU.add))
                    first_largest(b_)
                if part == "weights":
                    tt(a, a, b_, ALU.add)
                    tt(orig, orig, a, ALU.mult)

            def combine(b):
                if not (isinstance(b, int) and b == 0):
                    dve.wait_ge(cT_in_psum, b)
                c = comb_all[:, batch_of(b, NT), :]
                nc.vector.tensor_copy(comb[:, :, 0:E].bitcast(F32R), c).then_inc(comb_hi, 1)
                dve.wait_ge(comb_hi, b + 1)
                nc.vector.tensor_tensor(comb[:, :, E:2 * E].bitcast(F32R), c, comb[:, :, 0:E], ALU.subtract
                                        ).then_inc(combine_ready, 1)

            def early_route(g, m):
                if (g, m) == (1, 0):
                    dve.wait_ge(v_placed, B * G)
                    dve.wait_ge(xn_ready, B)
                    dve.wait_ge(attn_weights, 2)
                    route("softmax", 0, ROUTED_EARLY)
                for place, part in (((1, 3), "pairs"), ((2, 2), "group sums"), ((2, 4), "ranks"),
                                    ((2, 5), "group mask"), ((3, 1), "first"), ((3, 3), "second"), ((3, 4), "weights")):
                    if (g, m) == place:
                        route(part, 0, ROUTED_EARLY)
                if (g, m) == (3, 4):
                    combine(0)

            def iteration(b, tail, stage, stage_norm):
                def use(name):
                    return use_number(b, name)

                for g in range(G):
                    for m in range(NU):
                        if units_ahead(b, g, stage, m):
                            maxima(*units_ahead(b, g, stage, m))
                        if m == 0:
                            if g == 0 and stage:
                                split_lo(xnT_lo[:, :], xnT_hi[:, :], xT_hi, b + 1)
                            if g == 1 and tail:
                                normalise_o(b - 1, 2, use("otr2"))
                            if g == 2 and tail:
                                add_bo(use("oproj"))
                            if g == 3 and tail:
                                dve.wait_ge(x2_ready, b)
                                norm_stats(2, b - 1, x_tile(b - 1))
                        if m == 1:
                            if g == 1 and stage:
                                split_qk_lo(b + 1, use("q"), 0)
                            if g == 0 and stage_norm:
                                norm_stats(0, b + 2, x_tile(b + 2))
                            if g == 2 and tail:
                                dve.wait_ge(misc_evacuated, use("oproj") + 1)
                                norm_stats(1, b - 1, tile_in(att))
                        if m == 2:
                            if g == 1 and tail:
                                normalise_o(b - 1, 3, use("otr3"))
                            if g == 2 and stage_norm:
                                dve.wait_ge(misc_ready, use("xT") + 1)
                                normalise(0, b + 2, x_tile(b + 2), xn, xn_ready)
                            if g == 3 and tail:
                                normalise(2, b - 1, x_tile(b - 1), xf, xf_ready)
                        if m == 3:
                            if g == 1 and stage:
                                split_qk_lo(b + 1, use("k"), 1)
                            if g == 2 and tail:
                                normalise(1, b - 1, tile_in(att), attn_n, attn_normed)
                        if m == 4 and g == 0 and tail:
                            normalise_o(b - 1, 0, use("otr0"))
                        if m == 4 and g == 1 and tail:
                            split_lo(oT_lo[:, :], oT_hi[:, :], onT_hi, b - 1, col[:, 2:3])
                        if m == 4 and g == 3 and tail:
                            split_lo(xfs_lo[:, :], xfs_hi[:, :], xfT_hi_done, b - 1)
                        if m == 5:
                            if g == 0 and tail:
                                normalise_o(b - 1, 1, use("otr1"))
                            if g == 3 and tail:
                                shift_logits(b - 1, use("logits"))
                        if m == 4 and g < 3 and not tail:
                            split_experts(g)
                        if not stage:
                            early_route(g, m)

            nc.vector.memset(halfneg[:, :], -0.5).then_inc(half_set, 1)
            dve.wait_ge(x_first, 16)
            norm_stats(0, 0, x_tile(0))
            dve.wait_ge(attn_weights, 1)
            nc.vector.tensor_tensor(wa_lo[:, :, :], wa[:, :, :], wa_hi[:, :, :].bitcast(F32), ALU.subtract
                                    ).then_inc(attn_weights, 1)
            normalise(0, 0, x_tile(0), xn, xn_ready)
            split_lo(xnT_lo[:, :], xnT_hi[:, :], xT_hi, 0)
            for which, name in enumerate(("q", "k")):
                split_qk_lo(0, use_number(None, name), which)
            dve.wait_ge(x_rest, 16)
            norm_stats(0, 1, x_tile(1))
            normalise(0, 1, x_tile(1), xn, xn_ready)
            for u in range(NU):
                maxima(0, 0, u)
            for u in range(NU // 2):
                maxima(0, 1, u)
            iteration(0, tail=False, stage=True, stage_norm=True)
            with dve.Fori(1, B - 2) as b:
                iteration(b, tail=True, stage=True, stage_norm=True)
            iteration(B - 2, tail=True, stage=True, stage_norm=False)
            iteration(B - 1, tail=True, stage=False, stage_norm=False)
            def hidden(b, p, par):
                q = b * NP + p
                dve.wait_ge(silu_done, q + 1)
                dve.wait_ge(h3_ready, q + 1)
                if not (isinstance(q, int) and q < 3):
                    dve.wait_ge(h_split, q - 2)
                if p == 0:
                    nc.vector.scalar_tensor_tensor(hbuf[0], ps_h3[par], b13c[:, 1, 0:1], silu[0], ALU.add, ALU.mult
                                                   ).then_inc(h_done, 1)
                    return
                nc.vector.scalar_tensor_tensor(gated[p % 3], ps_h3[par], b13c[:, 1, p:p + 1], silu[p % 3],
                                               ALU.add, ALU.mult).then_inc(gated_done, 1)
                dve.wait_ge(gated_done, b * (NP - 1) + p)
                nc.vector.tensor_tensor(hbuf[p % 3], ps_c[par][:, :], gated[p % 3], ALU.mult).then_inc(h_done, 1)

            def y_tiles(t):
                return ps_m[:, P * t:P * t + P]

            def rest_of_last(b, p):
                if (b, p) in ((0, 0), (0, 1), (0, 3), (0, 4)):
                    t = ((0, 0), (0, 1), (0, 3), (0, 4)).index((b, p))
                    normalise_o(LAST, t, use_number(B, f"otr{t}"))
                if (b, p) == (0, 6):
                    split_lo(oT_lo[:, :], oT_hi[:, :], onT_hi, LAST, col[:, 2:3])
                if (b, p) == (0, 8):
                    add_bo(use_number(B, "oproj"))
                if (b, p) == (1, 0):
                    dve.wait_ge(misc_evacuated, use_number(B, "oproj") + 1)
                    norm_stats(1, LAST, tile_in(att))
                if (b, p) == (1, 1):
                    normalise(1, LAST, tile_in(att), attn_n, attn_normed)
                if (b, p) == (1, 3):
                    dve.wait_ge(x2_ready, B)
                    norm_stats(2, LAST, x_tile(LAST))
                if (b, p) == (1, 5):
                    normalise(2, LAST, x_tile(LAST), xf, xf_ready)
                if (b, p) == (1, 7):
                    split_lo(xfs_lo[:, :], xfs_hi[:, :], xfT_hi_done, LAST)
                if (b, p) == (1, 8):
                    shift_logits(LAST, use_number(B, "logits"))
                for place, part in enumerate(("softmax", "pairs", "group sums", "ranks", "group mask", "first",
                                              "second", "weights")):
                    if (b, p) == (2, place + 1):
                        route(part, ROUTED_EARLY, B)

            def finish(b):
                dve.wait_ge(y_normed, b + 1)
                dve.wait_ge(stored, b * 16 + 1)
                nc.vector.tensor_tensor(out_sb, y_n, xall[:, batch_of(b, NT), :], ALU.add).then_inc(out_ready, 1)

            def expert_batch(b, parity):
                for p in range(NP):
                    hidden(b, p, (parity + p) % 2)
                    if p == 1 and not (isinstance(b, int) and b == LAST):
                        combine(b + 1)
                    if isinstance(b, int) and b < 3:
                        rest_of_last(b, p)
                    if p == 4 and not (isinstance(b, int) and b == 0):
                        dve.wait_ge(yT_ready, b)
                        norm_stats(3, b - 1, y_tiles)
                    if p == 6 and not (isinstance(b, int) and b == 0):
                        normalise(3, b - 1, y_tiles, y_n, y_normed)
                    if p == 7 and not (isinstance(b, int) and b == 0):
                        finish(b - 1)

            for b in range(3):
                expert_batch(b, b % 2)
            with dve.Fori(0, (B - 4) // 2) as i:
                expert_batch(i * 2 + 3, 1)
                expert_batch(i * 2 + 4, 0)
            expert_batch(LAST, 1)
            dve.wait_ge(yT_ready, B)
            norm_stats(3, B - 1, y_tiles)
            normalise(3, B - 1, y_tiles, y_n, y_normed)
            finish(B - 1)

        @block.gpsimd
        def _(pool):
            def carry_wait():
                pool.sem_inc(wait_carrier[1], 1)

            def inverse_deviation(i, count):
                pool.wait_ge(moments[i], count + 1)
                carry_wait()
                nc.gpsimd.tensor_scalar(ve[:, i, :], mv[:, i, :, 1], EPS, 1.0, ALU.add, ALU.mult
                                        ).then_inc(eps_added[i], 1)
                pool.wait_ge(eps_added[i], count + 1)
                nc.gpsimd.tensor_tensor(rstd[:, i, :], ve[:, i, :], halfneg[:, :], ALU.pow).then_inc(rstds[i], 1)
                pool.wait_ge(rstds[i], count + 1)

            def place_v(s, g, number):
                pool.wait_ge(misc_evacuated, number + 1)
                if not (isinstance(s, int) and s == 0):
                    pool.wait_ge(pv_done, (s * G + g - G) * NT + NT)
                carry_wait()
                nc.gpsimd.tensor_scalar(vaug[:, :, HG * g:HG * (g + 1), 0:D],
                                        vraw[:, :, D * HG * g:D * HG * (g + 1)].rearrange("p t (h d) -> p t h d", d=D),
                                        1.0, 1.0, ALU.mult, ALU.mult).then_inc(v_placed, 1)
                pool.wait_ge(v_placed, s * G + (g + 1))

            def mask_exponentials(b, g, upper):
                n = b * G + g
                pool.wait_ge(exps_done, n * NV + (8 if upper else NV))
                carry_wait()
                k = slice(2, 4) if upper else slice(0, 2)
                d = T - P
                for part in range(2):
                    v = pt[CHUNK * part:CHUNK * (part + 1), k, :, d + CHUNK * part:d + CHUNK * (part + 1)]
                    nc.gpsimd.affine_select(out=v, in_=v, compare_op=ALU.is_ge, fill=0.0, base=0,
                                            pattern=[[0, 2], [0, HG], [1, CHUNK]], channel_multiplier=-1
                                            ).then_inc(masks_done, 1)
                    pool.wait_ge(masks_done, n * 6 + ((0 if upper else 3) + part + 1))
                    carry_wait()
                nc.gpsimd.memset(pt[0:CHUNK, k, :, d + CHUNK:T], 0.0).then_inc(masks_done, 1)
                pool.wait_ge(masks_done, n * 6 + (3 if upper else 6))

            def split_shift(b, g):
                n = b * G + g
                pool.wait_ge(maxes_done, n * NU + NU)
                if not (isinstance(n, int) and n == 0):
                    pool.wait_ge(shift_in_psum, n)
                carry_wait()
                src = negmax[:, g % 2, :, :]
                nc.gpsimd.tensor_scalar(shift[:, :, 0:HG].bitcast(F32R), src, 1.0, 1.0, ALU.mult, ALU.mult
                                        ).then_inc(shift_hi, 1)
                pool.wait_ge(shift_hi, n + 1)
                nc.gpsimd.tensor_tensor(shift[:, :, HG:2 * HG].bitcast(F32R), src, shift[:, :, 0:HG], ALU.subtract
                                        ).then_inc(shift_split, 1)
                pool.wait_ge(shift_split, n + 1)

            def add_x(b):
                pool.wait_ge(attn_normed, b + 1)
                v = xall[:, batch_of(b, NT), :]
                nc.gpsimd.tensor_tensor(v, v, attn_n[:, :, :], ALU.add).then_inc(x2_ready, 1)
                pool.wait_ge(x2_ready, b + 1)

            def iteration(b, tail, stage, v_number, stage_norm):
                def use(name):
                    return use_number(b, name)

                for g in range(G):
                    if tail or g:
                        mask_exponentials(*((b, g - 1) if g else (b - 1, G - 1)), False)
                    if g == 3 and tail:
                        inverse_deviation(2, b - 1)
                    if follower(b, g, stage):
                        split_shift(*follower(b, g, stage))
                    if g == 0:
                        place_v(b, G - 1, v_number)
                    if g == 2 and tail:
                        inverse_deviation(1, b - 1)
                    mask_exponentials(b, g, True)
                    if g == 1 and stage_norm:
                        inverse_deviation(0, b + 2)
                    if g == 2 and tail:
                        add_x(b - 1)
                    if g == 3 and stage:
                        for gg in range(G - 1):
                            place_v(b + 1, gg, use("v"))

            pool.wait_ge(half_set, 1)
            inverse_deviation(0, 0)
            pool.wait_ge(const_in, 80)

            def clear_operand(g):
                nc.gpsimd.memset(km[:, g, :, :].rearrange("p j t -> p (j t)").bitcast(F32), 0.0).then_inc(km_zeroed, 1)
                pool.wait_ge(km_zeroed, g + 1)
                nc.gpsimd.tensor_scalar(km[ROWS:ROWS_SHIFTED, g, :, :],
                                        cst[ROWS:ROWS_SHIFTED, ONES:ONES + HG].unsqueeze(2).broadcast_to(
                                            [ROWS_SHIFTED - ROWS, HG, T]), 1.0, 1.0, ALU.mult, ALU.mult
                                        ).then_inc(operands_cleared, 1)
                pool.wait_ge(operands_cleared, g + 1)

            clear_operand(0)
            clear_operand(1)
            nc.gpsimd.memset(vaug[:, :, :, D + 1:VW], 0.0).then_inc(ones_placed, 1)
            nc.gpsimd.memset(vaug[:, :, :, D:D + 1], 1.0).then_inc(ones_placed, 1)
            pool.wait_ge(ones_placed, 2)
            inverse_deviation(0, 1)
            for g in range(2, G):
                clear_operand(g)
            for g in range(G - 1):
                place_v(0, g, use_number(None, "v"))
            split_shift(0, 0)
            iteration(0, False, True, use_number(None, "v"), True)
            iteration(1, True, True, use_number(0, "v"), True)
            with pool.Fori(2, B - 2) as b:
                iteration(b, True, True, use_number(b, "v") - len(USES), True)
            iteration(B - 2, True, True, use_number(B - 3, "v"), False)
            iteration(B - 1, True, False, use_number(B - 2, "v"), False)
            mask_exponentials(B - 1, G - 1, False)

            def hidden_lower(b, p):
                q = b * NP + p
                pool.wait_ge(h_hi_done, q + 1)
                nc.gpsimd.tensor_tensor(h_lo[p % 3], hbuf[p % 3], h_hi[p % 3].bitcast(F32), ALU.subtract
                                        ).then_inc(h_split, 1)

            def expert_batch(b):
                for p in range(NP):
                    hidden_lower(b, p)
                    if p == 4 and not (isinstance(b, int) and b == 0):
                        inverse_deviation(3, b - 1)
                    if isinstance(b, int) and (b, p) == (1, 0):
                        inverse_deviation(1, LAST)
                    if isinstance(b, int) and (b, p) == (1, 1):
                        add_x(LAST)
                    if isinstance(b, int) and (b, p) == (1, 3):
                        inverse_deviation(2, LAST)

            expert_batch(0)
            expert_batch(1)
            with pool.Fori(2, B) as b:
                expert_batch(b)
            inverse_deviation(3, B - 1)


_OUT = ((B, T, C), "float32")


def kernel(**inputs):
    import concourse.bacc as bacc
    from concourse.bass_utils import run_bass_kernel_spmd

    a = {k: np.asarray(v) for k, v in inputs.items()}
    at, ff = (lambda n: a["L0_attn_" + n]), (lambda n: a["L0_ffn_" + n])

    def pairs_in(w):
        return w.reshape(E // 2, 2, C, INTER).transpose(2, 0, 1, 3).reshape(C, E // 2, P)

    def up_weights(shared, experts):
        return np.concatenate([shared[:, None, :], pairs_in(experts)], axis=1)

    w_attn = np.stack([at("Wq").T, at("Wk").T, at("Wv").T, at("Wo").T], axis=1)
    cols = np.stack([at("bq"), at("bk"), at("bv"), ff("bs2"),
                     np.broadcast_to(at("attn_scale"), (C,))], axis=1)
    w13 = np.stack([up_weights(ff("ws1"), ff("We1")), up_weights(ff("ws3"), ff("We3"))], axis=1).reshape(C, -1)
    w2 = np.concatenate([ff("ws2")[None], ff("We2").reshape(E // 2, P, C)], axis=0).transpose(1, 0, 2).reshape(P, -1)
    b13 = np.stack([np.concatenate([ff("bs1")[None], ff("be1").reshape(E // 2, P)], axis=0).T,
                    np.concatenate([ff("bs3")[None], ff("be3").reshape(E // 2, P)], axis=0).T], axis=1)
    rows = np.broadcast_to(np.concatenate([at("bo"), ff("gate_b")])[None, :], (P, C + E))
    arrays = {
        "x": a["L0_attn_x"].reshape(B * T, C), "w_attn": w_attn, "cols": cols, "w13": w13, "w2": w2, "b13": b13,
        "gate_w": ff("gate_w").T, "rows": rows, "be2": np.concatenate([ff("be2"), ff("be2")], axis=0),
        "const": shape_constants(),
    }
    arrays = {k: np.ascontiguousarray(v) for k, v in arrays.items()}
    nc = bacc.Bacc("TRN2", target_bir_lowering=False, num_devices=1)
    args = [nc.dram_tensor(f"in_{k}", v.shape, mybir.dt.from_np(v.dtype), kind="ExternalInput").ap()
            for k, v in arrays.items()]
    args.append(nc.dram_tensor("out_0", (B * T, C), F32, kind="ExternalOutput").ap())
    block_kernel(nc, *args)
    r = run_bass_kernel_spmd(nc, [{f"in_{k}": v for k, v in arrays.items()}], core_ids=[0])
    return r.results[0]["out_0"].reshape(_OUT[0])
```
